# Optimizing a Trainium2 kernel written in Bass

```python
import numpy as np
import jax
import jax.numpy as jnp

def _softmax(x, axis=-1):
    return jax.nn.softmax(x, axis=axis)

def _gelu(x):
    return jax.nn.gelu(x, approximate=True)

def _silu(x):
    return jax.nn.silu(x)

def _sigmoid(x):
    return jax.nn.sigmoid(x)

def _layernorm(x, axis=-1, eps=1e-05):
    m = jnp.mean(x, axis=axis, keepdims=True)
    v = jnp.var(x, axis=axis, keepdims=True)
    return (x - m) / jnp.sqrt(v + eps)

def _scatter_add(tgt, idx, src, axis=0):
    return tgt.at[idx].add(src)

def _segment_sum(src, seg, n):
    return jax.ops.segment_sum(src, seg, n)
kernel_name = 'mk_adj_ffn_d2_adj_r2_6a3552'

def setup_inputs(seed: int=0):
    np.random.seed(seed)
    _w = jnp.asarray

    def _rec_inputs():
        import jax
        import jax.numpy as jnp
        _gk = jax.random.key(seed)
        x = -0.0005207 + 1.001 * jax.random.normal(jax.random.fold_in(_gk, 1), (16, 512, 128), jnp.float32)
        _a = jax.random.bernoulli(jax.random.fold_in(_gk, 2), 0.015625, (16, 512, 512))
        _af = _a.astype(jnp.float32)
        adj = _af
        return (x, adj)
    x, adj = _rec_inputs()

    def _L0_gnn_setup():
        import jax, jax.numpy as jnp
        import numpy as np
        DIM = 128
        HEADS = 8
        BS = 8
        N = 512
        NEG = -1000000000.0
        key = jax.random.key(seed)
        ks = jax.random.split(key, 8)
        feats = jax.random.normal(ks[0], (BS, N, DIM), dtype=jnp.float32)
        adj_mat = (jax.random.uniform(ks[1], (BS, N, N)) < 0.1).astype(jnp.float32)
        s = 1.0 / np.sqrt(DIM)
        fc_w = jax.random.normal(ks[2], (DIM, DIM * HEADS), dtype=jnp.float32) * s
        fc_b = jnp.zeros((DIM * HEADS,), dtype=jnp.float32)
        q_w = jax.random.normal(ks[3], (DIM, 1), dtype=jnp.float32) * s
        q_b = jnp.zeros((1,), dtype=jnp.float32)
        k_w = jax.random.normal(ks[4], (DIM, 1), dtype=jnp.float32) * s
        k_b = jnp.zeros((1,), dtype=jnp.float32)
        fp_w = jax.random.normal(ks[5], (DIM * HEADS, DIM), dtype=jnp.float32) * (1.0 / np.sqrt(DIM * HEADS))
        fp_b = jnp.zeros((DIM,), dtype=jnp.float32)
        return {'feats': feats, 'adj_mat': adj_mat, 'fc_w': fc_w, 'fc_b': fc_b, 'q_w': q_w, 'q_b': q_b, 'k_w': k_w, 'k_b': k_b, 'fp_w': fp_w, 'fp_b': fp_b}
    _L0_gnn_all = _L0_gnn_setup()
    _L0_gnn_in = {k: v for k, v in _L0_gnn_all.items() if k in ('fc_w', 'fc_b', 'q_w', 'q_b', 'k_w', 'k_b', 'fp_w', 'fp_b')}
    del _L0_gnn_all

    def _L0_ffn_setup():
        import math
        import jax, jax.numpy as jnp
        import numpy as np
        CAPACITY_FACTOR = 1.25
        key = jax.random.key(seed)
        ks = jax.random.split(key, 5)
        B, L, D, F, E = (8, 4096, 128, 512, 8)
        h = jax.random.normal(ks[0], (B, L, D), dtype=jnp.float32)
        gate_w = jax.random.normal(ks[1], (D, E), dtype=jnp.float32) * 0.02
        gate_b = jnp.zeros((E,), dtype=jnp.float32)
        w1 = jax.random.normal(ks[2], (E, D, F), dtype=jnp.float32) * (1.0 / math.sqrt(D))
        b1 = jnp.zeros((E, F), dtype=jnp.float32)
        w2 = jax.random.normal(ks[3], (E, F, D), dtype=jnp.float32) * (1.0 / math.sqrt(F))
        b2 = jnp.zeros((E, D), dtype=jnp.float32)
        return {'h': h, 'gate_w': gate_w, 'gate_b': gate_b, 'w1': w1, 'b1': b1, 'w2': w2, 'b2': b2}
    _L0_ffn_all = _L0_ffn_setup()
    _L0_ffn_in = {k: v for k, v in _L0_ffn_all.items() if k in ('gate_w', 'gate_b', 'w1', 'b1', 'w2', 'b2')}
    del _L0_ffn_all

    def _L1_gnn_setup():
        import jax, jax.numpy as jnp
        import numpy as np
        IN_DIM = 128
        OUT_DIM = 128
        key = jax.random.key(seed)
        k1, k2, k3, k4 = jax.random.split(key, 4)
        B, N = (8, 1024)
        X = jax.random.normal(k1, (B, N, IN_DIM), dtype=jnp.float32)
        adj = jax.random.uniform(k2, (B, N, N), dtype=jnp.float32)
        bound = 1.0 / np.sqrt(IN_DIM)
        W = jax.random.uniform(k3, (OUT_DIM, IN_DIM), minval=-bound, maxval=bound, dtype=jnp.float32)
        b = jax.random.uniform(k4, (OUT_DIM,), minval=-bound, maxval=bound, dtype=jnp.float32)
        return {'X': X, 'adj': adj, 'W': W, 'b': b}
    _L1_gnn_all = _L1_gnn_setup()
    _L1_gnn_in = {k: v for k, v in _L1_gnn_all.items() if k in ('W', 'b')}
    del _L1_gnn_all

    def _L1_ffn_setup():
        import jax, jax.numpy as jnp
        import numpy as np
        B, S, H, NH, NE = (4, 512, 128, 4, 4)
        D = H // NH
        EPS = 1e-08

        def layernorm(x, g, b):
            m = jnp.mean(x, axis=-1, keepdims=True)
            v = jnp.mean((x - m) ** 2, axis=-1, keepdims=True)
            return (x - m) / jnp.sqrt(v + EPS) * g + b
        key = jax.random.key(seed)
        ks = jax.random.split(key, 18)
        sc = 0.05
        return {'x': jax.random.normal(ks[0], (B, S, H), jnp.float32), 'hl_w': jax.random.normal(ks[1], (NH, D, H), jnp.float32) * sc, 'hl_b': jax.random.normal(ks[2], (NH, D), jnp.float32) * sc, 'wq': jax.random.normal(ks[3], (NH, NE, D, D), jnp.float32) * sc, 'wk': jax.random.normal(ks[4], (NH, D, D), jnp.float32) * sc, 'wv': jax.random.normal(ks[5], (NH, D, D), jnp.float32) * sc, 'gate_w': jax.random.normal(ks[6], (NH, NE, NE * D), jnp.float32) * sc, 'gate_b': jax.random.normal(ks[7], (NH, NE), jnp.float32) * sc, 'ln_g': jnp.ones((D,), jnp.float32), 'ln_b': jnp.zeros((D,), jnp.float32), 'fc1_w': jax.random.normal(ks[8], (D, D), jnp.float32) * sc, 'fc1_b': jax.random.normal(ks[9], (D,), jnp.float32) * sc, 'fc2_w': jax.random.normal(ks[10], (D, D), jnp.float32) * sc, 'fc2_b': jax.random.normal(ks[11], (D,), jnp.float32) * sc, 'fnorm_g': jnp.ones((D,), jnp.float32), 'fnorm_b': jnp.zeros((D,), jnp.float32), 'fgate_w': jax.random.normal(ks[12], (NH, H), jnp.float32) * sc}
    _L1_ffn_all = _L1_ffn_setup()
    _L1_ffn_in = {k: v for k, v in _L1_ffn_all.items() if k in ('hl_w', 'hl_b', 'wq', 'wk', 'wv', 'gate_w', 'gate_b', 'ln_g', 'ln_b', 'fc1_w', 'fc1_b', 'fc2_w', 'fc2_b', 'fnorm_g', 'fnorm_b', 'fgate_w')}
    del _L1_ffn_all
    return {'x': x, 'adj': adj, 'L0_gnn_fc_w': _L0_gnn_in['fc_w'], 'L0_gnn_fc_b': _L0_gnn_in['fc_b'], 'L0_gnn_q_w': _L0_gnn_in['q_w'], 'L0_gnn_q_b': _L0_gnn_in['q_b'], 'L0_gnn_k_w': _L0_gnn_in['k_w'], 'L0_gnn_k_b': _L0_gnn_in['k_b'], 'L0_gnn_fp_w': _L0_gnn_in['fp_w'], 'L0_gnn_fp_b': _L0_gnn_in['fp_b'], 'L0_ffn_gate_w': _L0_ffn_in['gate_w'], 'L0_ffn_gate_b': _L0_ffn_in['gate_b'], 'L0_ffn_w1': _L0_ffn_in['w1'], 'L0_ffn_b1': _L0_ffn_in['b1'], 'L0_ffn_w2': _L0_ffn_in['w2'], 'L0_ffn_b2': _L0_ffn_in['b2'], 'L1_gnn_W': _L1_gnn_in['W'], 'L1_gnn_b': _L1_gnn_in['b'], 'L1_ffn_hl_w': _L1_ffn_in['hl_w'], 'L1_ffn_hl_b': _L1_ffn_in['hl_b'], 'L1_ffn_wq': _L1_ffn_in['wq'], 'L1_ffn_wk': _L1_ffn_in['wk'], 'L1_ffn_wv': _L1_ffn_in['wv'], 'L1_ffn_gate_w': _L1_ffn_in['gate_w'], 'L1_ffn_gate_b': _L1_ffn_in['gate_b'], 'L1_ffn_ln_g': _L1_ffn_in['ln_g'], 'L1_ffn_ln_b': _L1_ffn_in['ln_b'], 'L1_ffn_fc1_w': _L1_ffn_in['fc1_w'], 'L1_ffn_fc1_b': _L1_ffn_in['fc1_b'], 'L1_ffn_fc2_w': _L1_ffn_in['fc2_w'], 'L1_ffn_fc2_b': _L1_ffn_in['fc2_b'], 'L1_ffn_fnorm_g': _L1_ffn_in['fnorm_g'], 'L1_ffn_fnorm_b': _L1_ffn_in['fnorm_b'], 'L1_ffn_fgate_w': _L1_ffn_in['fgate_w']}

def reference(x, adj, L0_gnn_fc_w, L0_gnn_fc_b, L0_gnn_q_w, L0_gnn_q_b, L0_gnn_k_w, L0_gnn_k_b, L0_gnn_fp_w, L0_gnn_fp_b, L0_ffn_gate_w, L0_ffn_gate_b, L0_ffn_w1, L0_ffn_b1, L0_ffn_w2, L0_ffn_b2, L1_gnn_W, L1_gnn_b, L1_ffn_hl_w, L1_ffn_hl_b, L1_ffn_wq, L1_ffn_wk, L1_ffn_wv, L1_ffn_gate_w, L1_ffn_gate_b, L1_ffn_ln_g, L1_ffn_ln_b, L1_ffn_fc1_w, L1_ffn_fc1_b, L1_ffn_fc2_w, L1_ffn_fc2_b, L1_ffn_fnorm_g, L1_ffn_fnorm_b, L1_ffn_fgate_w):
    import jax
    import jax.numpy as jnp

    def _L0_gnn_ref(feats, adj_mat, fc_w, fc_b, q_w, q_b, k_w, k_b, fp_w, fp_b):
        import jax, jax.numpy as jnp
        import numpy as np
        DIM = 128
        HEADS = 8
        BS = 8
        N = 512
        NEG = -1000000000.0
        bs, n, dim = feats.shape
        feat_proj = (feats @ fc_w + fc_b).reshape(bs, n, HEADS, dim).transpose(0, 2, 1, 3)
        q = feat_proj @ q_w + q_b
        k = feat_proj @ k_w + k_b
        logits = q + jnp.swapaxes(k, -1, -2)
        masked = logits + (1.0 - adj_mat[:, None]) * NEG
        masked = jax.nn.leaky_relu(masked, negative_slope=0.01)
        attn = jax.nn.softmax(masked, axis=-1)
        out = attn @ feat_proj
        out = out.transpose(0, 2, 1, 3).reshape(bs, n, HEADS * dim)
        out = out @ fp_w + fp_b + feats
        return jax.nn.sigmoid(out)

    def _L0_ffn_ref(h, gate_w, gate_b, w1, b1, w2, b2):
        import math
        import jax, jax.numpy as jnp
        import numpy as np
        CAPACITY_FACTOR = 1.25
        B, L, D = h.shape
        E = gate_w.shape[1]
        T = B * L
        C = max(1, math.ceil(CAPACITY_FACTOR * T / E))
        x = h.reshape(T, D)
        logits = x @ gate_w + gate_b
        probs = jax.nn.softmax(logits, axis=-1)
        idx = jnp.argmax(probs, axis=-1)
        prb = jnp.take_along_axis(probs, idx[:, None], axis=1)[:, 0]
        one_hot = jax.nn.one_hot(idx, E, dtype=jnp.float32)
        pos = (jnp.cumsum(one_hot, axis=0) * one_hot).sum(-1).astype(jnp.int32) - 1
        kept = pos < C
        pos_safe = jnp.where(kept, pos, C)
        buf = jnp.zeros((E, C, D), dtype=h.dtype).at[idx, pos_safe].set(x, mode='drop')
        hmid = jax.nn.relu(jnp.einsum('ecd,edf->ecf', buf, w1) + b1[:, None, :])
        ybuf = jnp.einsum('ecf,efd->ecd', hmid, w2) + b2[:, None, :]
        pos_g = jnp.minimum(pos, C - 1)
        y_tok = ybuf[idx, pos_g] * (prb * kept)[:, None]
        y = y_tok.reshape(B, L, D)
        y = jnp.nan_to_num(y, nan=0.0, posinf=10000.0, neginf=-10000.0)
        return y

    def _L1_gnn_ref(X, adj, W, b):
        import jax, jax.numpy as jnp
        import numpy as np
        IN_DIM = 128
        OUT_DIM = 128
        N = adj.shape[-1]
        adj_hat = adj + jnp.eye(N, dtype=adj.dtype)
        d = jnp.sum(adj_hat, axis=-1) ** (-0.5)
        adj_norm = d[..., :, None] * adj_hat * d[..., None, :]
        H = jnp.matmul(adj_norm, X)
        out = jnp.einsum('bnf,of->bno', H, W) + b
        return jax.nn.relu(out)

    def _L1_ffn_ref(x, hl_w, hl_b, wq, wk, wv, gate_w, gate_b, ln_g, ln_b, fc1_w, fc1_b, fc2_w, fc2_b, fnorm_g, fnorm_b, fgate_w):
        import jax, jax.numpy as jnp
        import numpy as np
        B, S, H, NH, NE = (4, 512, 128, 4, 4)
        D = H // NH
        EPS = 1e-08

        def layernorm(x, g, b):
            m = jnp.mean(x, axis=-1, keepdims=True)
            v = jnp.mean((x - m) ** 2, axis=-1, keepdims=True)
            return (x - m) / jnp.sqrt(v + EPS) * g + b
        b, s, h = x.shape
        nh, d, _ = wk.shape
        ne = wq.shape[1]
        sx = jnp.einsum('bsh,ndh->bnsd', x, hl_w) + hl_b[None, :, None, :]
        pad = sx == 0
        q = jnp.einsum('bnsd,neod->bneso', sx, wq)
        k = jnp.einsum('bnsd,nod->bnso', sx, wk)
        v = jnp.einsum('bnsd,nod->bnso', sx, wv)
        causal = jnp.where(jnp.tril(jnp.ones((s, s), bool)), 0.0, -jnp.inf).astype(x.dtype)
        scores = jnp.einsum('bnesd,bntd->bnest', q, k) * d ** 0.5 + causal
        att = jax.nn.softmax(scores, axis=-1)
        qkv = jnp.einsum('bnest,bntd->bnesd', att, v)
        qkv = jnp.where(pad[:, :, None], 0.0, qkv)
        out = jnp.transpose(qkv, (0, 1, 3, 2, 4)).reshape(b, nh, s, ne * d)
        gs = jax.nn.softmax(jnp.einsum('bnsf,nef->bnse', out, gate_w) + gate_b[None, :, None, :], axis=-1)
        mixed = jnp.einsum('bnsed,bnse->bnsd', out.reshape(b, nh, s, ne, d), gs)
        resid = sx[jnp.arange(nh), jnp.arange(nh)]
        hn = layernorm(mixed + resid, ln_g, ln_b)
        f_n = jnp.transpose(hn, (0, 2, 1, 3)).reshape(b, s, h)
        fx = f_n.reshape(b, s, nh, d)
        pm = fx == 0
        hx = jnp.where(pm, 0.0, fx @ fc1_w.T + fc1_b)
        hx = jax.nn.relu(hx)
        hx = jnp.where(pm, 0.0, hx @ fc2_w.T + fc2_b)
        hx = layernorm(hx + fx, fnorm_g, fnorm_b)
        fout = hx.reshape(b, s, h)
        fg = jax.nn.softmax(fout @ fgate_w.T, axis=-1)
        return (fout.reshape(b, s, nh, d) * fg[..., None]).reshape(b, s, h)
    x = x + _L0_gnn_ref(_layernorm(x, axis=-1), adj, L0_gnn_fc_w, L0_gnn_fc_b, L0_gnn_q_w, L0_gnn_q_b, L0_gnn_k_w, L0_gnn_k_b, L0_gnn_fp_w, L0_gnn_fp_b)
    x = x + _L0_ffn_ref(_layernorm(x, axis=-1), L0_ffn_gate_w, L0_ffn_gate_b, L0_ffn_w1, L0_ffn_b1, L0_ffn_w2, L0_ffn_b2)
    x = x + _L1_gnn_ref(_layernorm(x, axis=-1), adj, L1_gnn_W, L1_gnn_b)
    x = x + _L1_ffn_ref(_layernorm(x, axis=-1), L1_ffn_hl_w, L1_ffn_hl_b, L1_ffn_wq, L1_ffn_wk, L1_ffn_wv, L1_ffn_gate_w, L1_ffn_gate_b, L1_ffn_ln_g, L1_ffn_ln_b, L1_ffn_fc1_w, L1_ffn_fc1_b, L1_ffn_fc2_w, L1_ffn_fc2_b, L1_ffn_fnorm_g, L1_ffn_fnorm_b, L1_ffn_fgate_w)
    return x

_drawn_inputs = setup_inputs


def setup_inputs(seed=0):
    import zlib

    import numpy as np

    out = dict(_drawn_inputs(seed))
    spreads = {'L0_gnn_fc_b': (0.0, 0.371),
     'L0_gnn_fp_b': (0.0, 0.379),
     'L0_ffn_gate_b': (0.0, 0.1),
     'L0_ffn_b1': (0.0, 0.8),
     'L0_ffn_b2': (0.0, 0.68),
     'L1_ffn_ln_g': (1.0, 0.2),
     'L1_ffn_ln_b': (0.0, 0.356),
     'L1_ffn_fnorm_g': (1.0, 0.2),
     'L1_ffn_fnorm_b': (0.0, 0.341)}
    factors = {'L0_gnn_q_w': 2.848,
     'L1_ffn_wq': 8.0,
     'L1_ffn_wk': 8.0,
     'L1_ffn_wv': 4.946,
     'L1_ffn_gate_w': 8.0,
     'L1_ffn_gate_b': 22.007,
     'L1_ffn_fc1_w': 5.73,
     'L1_ffn_fc1_b': 8.0,
     'L1_ffn_fc2_w': 5.286,
     'L1_ffn_fc2_b': 5.117}
    for name, (base, spread) in spreads.items():
        noise = np.random.default_rng([zlib.crc32(name.encode()), seed]).standard_normal(out[name].shape)
        drawn = base * np.exp(spread * noise) if base else spread * noise
        out[name] = jnp.asarray(drawn.astype(out[name].dtype))
    for name, factor in factors.items():
        out[name] = (out[name] * factor).astype(out[name].dtype)
    return out
```

```python
from contextlib import ExitStack

import concourse.bass as bass
from concourse import mybir

F32 = mybir.dt.float32
BF16 = mybir.dt.bfloat16
U32 = mybir.dt.uint32
ACT = mybir.ActivationFunctionType
ALU = mybir.AluOpType
AX = mybir.AxisListType.X

P = 128
B, N, D = 16, 512, 128
T = N // P
H = 8
E, F = 8, 512
CAP = B * N * 5 // 4 // E
SLOPE = 0.01


class Chain:

    def __init__(self, eng, sem):
        self.eng, self.sem, self.base, self.k = eng, sem, 0, 0

    def turn(self, start, turn, steps):
        self.base, self.k = turn * steps + start, 0

    def link(self, ins):
        self.k += 1
        ins.then_inc(self.sem, 1)
        self.eng.wait_ge(self.sem, self.base + self.k)


def later(turn):
    return not isinstance(turn, int) or turn > 0


class Banks:

    def __init__(self, whole):
        self.whole = whole
        self.banks = [whole[:, i, :] for i in range(8)]
        self.logit, self.place, self.count = self.banks[2:5]


def build(nc, t, out):
    ctx = ExitStack()
    with ctx:
        def sb(name, shape, dt=F32):
            return ctx.enter_context(nc.sbuf_tensor(name, shape, dt))

        def sem(name):
            return ctx.enter_context(nc.semaphore(name))

        x_all = sb("x_all", [P, B * T, D])
        deg = sb("deg", [P, B * T])
        ident = sb("ident", [P, P])
        ident_bf = sb("ident_bf", [P, P], BF16)
        ones = sb("ones", [P, P])
        ones_bf = sb("ones_bf", [P, 1], BF16)
        neg_half = sb("neg_half", [P, 16])
        slot_of = sb("slot_of", [P, B * T], U32)
        share = sb("share", [P, B * T])
        expert_in = nc.dram_tensor("expert_in", [E * CAP + B * N, D], F32, kind="Internal").ap()
        expert_out = nc.dram_tensor("expert_out", [E * CAP, D], F32, kind="Internal").ap()

        psum = Banks(ctx.enter_context(nc.psum_tensor("banks", [P, 8, 512], F32)))

        const_ready = sem("const_ready")

        with ExitStack() as graphs:
            adjT = graphs.enter_context(nc.sbuf_tensor("adjT", [P, B, T, N], BF16))
            with ExitStack() as stage:
                gat_layer(nc, t, stage, x_all, adjT, deg, ident, ident_bf, ones, ones_bf, neg_half, psum.banks,
                          const_ready)
            with ExitStack() as stage:
                route_tokens(nc, t, stage, x_all, expert_in, slot_of, share, ident, ident_bf, ones, neg_half, psum)
            with ExitStack() as stage:
                run_experts(nc, t, stage, expert_in, expert_out, ident, psum)
            with ExitStack() as stage:
                gcn_layer(nc, t, stage, x_all, adjT, deg, expert_out, slot_of, share, ident, ident_bf, neg_half, psum)
        with ExitStack() as stage:
            attention_layer(nc, t, stage, x_all, out, ident, ident_bf, ones, neg_half, psum)


def gat_layer(nc, t, stage, x_all, adjT, deg, ident, ident_bf, ones, ones_bf, neg_half, psum, const_ready):
    def sb(name, shape, dt=F32):
        return stage.enter_context(nc.sbuf_tensor(name, shape, dt))

    def sem(name):
        return stage.enter_context(nc.semaphore(name))

    fc_b = sb("fc_b", [P, H])
    qk_w = sb("qk_w", [P, 2])
    qk_b = sb("qk_b", [P, 2])
    fp_b = sb("fp_b", [P, D])
    value_w = sb("value_w", [P, H, D])
    mean_w = sb("mean_w", [P, D])
    head_qk = sb("head_qk", [P, H, 2])
    q_rep = sb("q_rep", [P, H, P])
    qk_sum = sb("qk_sum", [P, 2])
    logit_b = sb("logit_b", [P, H])
    out_b = sb("out_b", [P, D])

    adj_in = sb("adj_in", [P, T, N])
    adj_bf = sb("adj_bf", [P, T, N], BF16)
    xn = sb("xn", [P, T, D])
    xnT = sb("xnT", [P, N])
    stats = sb("stats", [P, T, 6])
    mv = sb("mv", [P, T, 2])
    rstd = sb("rstd", [P, T])
    wait_spot = sb("wait_spot", [P, 1])
    kmax = sb("kmax", [H, 1])
    kmax_diag = sb("kmax_diag", [H, H])
    kmax_all = sb("kmax_all", [P, H])
    relu_b = sb("relu_b", [P, H])
    kd = sb("kd", [P, T, H])
    k_steep = sb("k_steep", [P, 2, T, H])
    k_flat = sb("k_flat", [P, T, H])
    xsum = sb("xsum", [P, 1])
    xsum_rep = sb("xsum_rep", [P, P])
    lone = sb("lone", [P, 2, T])
    acc = sb("acc", [P, 2, T, D])
    value = sb("value", [P, 2, T, H, D + 1])
    q_relu = sb("q_relu", [P, 2, N])
    q_row = sb("q_row", [P, H, N])
    weight = sb("weight", [P, 2, T, N])
    fc_w = weight[:, 0, 0:2, :].rearrange("p a (h d) -> p (a h) d", d=D)
    fp_w = weight[:, 0, 2:4, :].rearrange("p a (h d) -> p (a h) d", d=D)
    fc_wT = weight[:, 1, 0:2, :].rearrange("p a (h d) -> p (a h) d", d=D)
    den = sb("den", [P, T])
    rden = sb("rden", [P, T])
    sig = sb("sig", [P, T, D])

    fc_b_rep = q_row[:, :, 0:P]

    w_in = sem("w_in")
    in_ready = sem("in_ready")
    adj_cast = sem("adj_cast")
    pe_w = sem("pe_w")
    w_done = sem("w_done")
    vec_chain = sem("gat_vec_chain")
    pool_chain = sem("gat_pool_chain")
    act_chain = sem("gat_act_chain")
    var_ready = sem("var_ready")
    rstd_ready = sem("rstd_ready")
    xn_ready = sem("xn_ready")
    adjT_pe = sem("adjT_pe")
    adjT_ready = sem("adjT_ready")
    xnT_pe = sem("xnT_pe")
    xnT_ready = sem("xnT_ready")
    k_pe = sem("k_pe")
    kdiag_ready = sem("kdiag_ready")
    kmax_pe = sem("kmax_pe")
    kd_ready = sem("kd_ready")
    kexp_ready = sem("kexp_ready")
    small_used = sem("small_used")
    value_pe = sem("value_pe")
    value_ready = sem("value_ready")
    q_pe = sem("q_pe")
    q_relu_ready = sem("q_relu_ready")
    q_row_ready = sem("q_row_ready")
    weight_ready = sem("weight_ready")
    head_pe = sem("head_pe")
    head_used = sem("head_used")
    acc_ready = sem("acc_ready")
    sig_ready = sem("sig_ready")
    x1_ready = sem("x1_ready")

    bank_t = psum[0:2]
    bank_s = psum[2]
    bank_k = psum[3]
    bank_q = psum[4:6]
    bank_o = psum[6:8]
    k_tok = bank_s[:, 0:T * H].rearrange("p (t h) -> p t h", t=T)
    deg_ps = bank_s[:, 64:64 + T]
    kmax_ps = bank_s[:, 128:128 + H]
    mean_ps = bank_s[:, 256:256 + D]
    o_ps = [bank_o[i][:, 0:2 * (D + 1)].rearrange("p (t c) -> p t c", t=2) for i in range(2)]

    adj = t["adj"].rearrange("b (t p) j -> b p t j", p=P)
    x_in = t["x"].rearrange("b (t p) d -> b p t d", p=P)

    with nc.Block() as block:
        @block.sync
        def _(sp):
            def load(b):
                sp.dma_start(x_all[:, bass.ds(b * T, T), :], x_in[b]).then_inc(in_ready, 16)
                sp.dma_start(adj_in[:], adj[b]).then_inc(in_ready, 16)

            load(0)
            for dst, src in ((fc_w, t["L0_gnn_fc_w"].rearrange("d (h c) -> d h c", h=H)),
                             (fp_w, t["L0_gnn_fp_w"].rearrange("(h c) o -> c h o", h=H)),
                             (fc_b[:], t["L0_gnn_fc_b"].rearrange("(h c) -> c h", h=H)),
                             (qk_w[:, 0:1], t["L0_gnn_q_w"]),
                             (qk_w[:, 1:2], t["L0_gnn_k_w"]),
                             (qk_b[:, 0:1], t["L0_gnn_q_b"].rearrange("(a n) -> a n", a=1).broadcast_to([P, 1])),
                             (qk_b[:, 1:2], t["L0_gnn_k_b"].rearrange("(a n) -> a n", a=1).broadcast_to([P, 1])),
                             (fp_b[:], t["L0_gnn_fp_b"].rearrange("(a n) -> a n", a=1).broadcast_to([P, D]))):
                with nc.allow_non_contiguous_dma("small weights"):
                    sp.dma_start(dst, src).then_inc(w_in, 16)
            with sp.Fori(1, B) as b:
                sp.wait_ge(in_ready, b * 32)
                sp.wait_ge(adj_cast, b)
                load(b)

        @block.gpsimd
        def _(pool):
            chain = Chain(pool, pool_chain)
            nc.gpsimd.memset(neg_half[:], -0.5)
            nc.gpsimd.memset(ones[:], 1.0).then_inc(const_ready, 1)
            nc.gpsimd.memset(ones_bf[:], 1.0).then_inc(const_ready, 1)
            chain.link(nc.gpsimd.memset(ident[:], 0.0))
            chain.link(nc.gpsimd.affine_select(out=ident[:], in_=ident[:], compare_op=ALU.not_equal, fill=1.0,
                                               base=0, pattern=[[-1, P]], channel_multiplier=1))
            nc.gpsimd.tensor_copy(ident_bf[:], ident[:]).then_inc(const_ready, 1)

            def prepare(b):
                pool.wait_ge(var_ready, b + 1)
                nc.gpsimd.tensor_tensor(rstd[:], mv[:, :, 1], neg_half[:, 0:T], ALU.pow).then_inc(rstd_ready, 1)

            prepare(0)
            with pool.Fori(0, B - 1) as b:
                prepare(b + 1)

        @block.scalar
        def _(act):
            def stage0(b):
                act.wait_ge(in_ready, (b + 1) * 32)
                if later(b):
                    act.wait_ge(adjT_pe, b * 2)
                nc.scalar.activation(adj_bf[:], adj_in[:], ACT.Copy).then_inc(adj_cast, 1)

            def stage1(b):
                for i in range(2):
                    act.wait_ge(adjT_pe, b * 2 + i + 1)
                    src = bank_t[i][:, :].bitcast(BF16).rearrange("p (t n) -> p t n", t=2)
                    nc.scalar.activation(adjT[:, b, 2 * i:2 * i + 2, :], src, ACT.Copy).then_inc(adjT_ready, 1)
                act.wait_ge(xnT_pe, b + 1)
                nc.scalar.activation(xnT[:], bank_t[0][:, :], ACT.Copy).then_inc(xnT_ready, 1)

            def stage3(b):
                act.wait_ge(kd_ready, b + 1)
                nc.scalar.activation(k_flat[:], kd[:], ACT.Exp, scale=SLOPE)
                nc.scalar.activation(k_steep[:, b % 2], kd[:], ACT.Exp, scale=1.0 - SLOPE).then_inc(kexp_ready, 1)

            def q_rows(b, h):
                act.wait_ge(q_pe, b * H + h + 1)
                act.wait_ge(kd_ready, b + 1)
                nc.scalar.activation(q_relu[:, h % 2, :], bank_q[h % 2][:, :], ACT.Relu,
                                     bias=relu_b[:, h:h + 1]).then_inc(q_relu_ready, 1)
                act.wait_ge(q_relu_ready, b * H + h + 1)
                if later(b):
                    act.wait_ge(weight_ready, (b - 1) * H + h + 1)
                nc.scalar.activation(q_row[:, h, :], q_relu[:, h % 2, :], ACT.Exp,
                                     scale=-(1.0 - SLOPE)).then_inc(q_row_ready, 1)

            def finish(b):
                act.wait_ge(acc_ready, b + 1)
                nc.scalar.activation(sig[:], acc[:, b % 2], ACT.Exp, scale=-1.0).then_inc(sig_ready, 1)

            stage0(0)
            stage1(0)
            stage3(0)
            for h in range(H):
                q_rows(0, h)
            with act.Fori(0, B - 1) as b:
                stage0(b + 1)
                stage1(b + 1)
                stage3(b + 1)
                for h in range(H):
                    q_rows(b + 1, h)
                finish(b)
            finish(B - 1)

        @block.tensor
        def _(pe):
            pe.wait_ge(w_in, 8 * 16)
            pe.wait_ge(const_ready, 3)
            for h in range(H):
                m = nc.tensor.transpose(psum[h // 4][:, (h % 4) * D:(h % 4 + 1) * D], fc_w[:, h, :], ident[:])
            m.then_inc(pe_w, 1)
            pe.wait_ge(w_done, 1)
            for h in range(H):
                m = nc.tensor.matmul(psum[2 + h // 4][:, (h % 4) * D:(h % 4 + 1) * D], fc_wT[:, h, :], fp_w[:, h, :],
                                     start=True, stop=True)
            for h in range(H):
                m = nc.tensor.matmul(psum[4][:, 2 * h:2 * h + 2], fc_wT[:, h, :], qk_w[:], start=True, stop=True)
            for h in range(H):
                m = nc.tensor.matmul(psum[4][:, 32 + h:33 + h], fc_b_rep[:, h, :], qk_sum[:, 0:1], start=True, stop=True)
            for h in range(H):
                m = nc.tensor.matmul(psum[5][:, 0:D], fc_b_rep[:, h, :], fp_w[:, h, :], start=(h == 0), stop=(h == H - 1))
            m.then_inc(pe_w, 1)
            pe.wait_ge(w_done, 2)

            def stage1(b):
                pe.wait_ge(adj_cast, b + 1)
                if later(b):
                    pe.wait_ge(value_ready, b * T * 2)
                for jt in range(T):
                    dst = bank_t[jt // 2][:, :].bitcast(BF16).rearrange("p (t n) -> p t n", t=2)
                    for it in range(T):
                        m = nc.tensor.transpose(dst[:, jt % 2, it * P:(it + 1) * P],
                                                adj_bf[:, it, jt * P:(jt + 1) * P], ident_bf[:])
                    if jt % 2:
                        m.then_inc(adjT_pe, 1)
                pe.wait_ge(xn_ready, b + 1)
                pe.wait_ge(adjT_ready, b * 2 + 1)
                for it in range(T):
                    m = nc.tensor.transpose(bank_t[0][:, it * P:(it + 1) * P], xn[:, it, :], ident[:])
                m.then_inc(xnT_pe, 1)

            def stage2(b):
                pe.wait_ge(xnT_ready, b + 1)
                pe.wait_ge(adjT_ready, b * 2 + 2)
                if later(b):
                    pe.wait_ge(small_used, b)
                m = nc.tensor.matmul(bank_k[0:H, :], head_qk[:, :, 1], xnT[:], start=True, stop=True)
                for jt in range(T):
                    nc.tensor.matmul(k_tok[:, jt, :], xnT[:, jt * P:(jt + 1) * P], head_qk[:, :, 1],
                                     start=True, stop=True)
                for it in range(T):
                    for jt in range(T):
                        m = nc.tensor.matmul(deg_ps[:, it:it + 1], adjT[:, b, jt, it * P:(it + 1) * P],
                                             ones_bf[:], start=(jt == 0), stop=(jt == T - 1))
                m.then_inc(k_pe, 1)

            def stage3(b):
                pe.wait_ge(kdiag_ready, b + 1)
                nc.tensor.matmul(kmax_ps, ones[0:H, :], kmax_diag[:], start=True, stop=True)
                nc.tensor.matmul(mean_ps, xsum_rep[:], mean_w[:], start=True, stop=True).then_inc(kmax_pe, 1)

            def values(b, jt):
                if jt == 0:
                    pe.wait_ge(xnT_ready, b + 1)
                    pe.wait_ge(adjT_ready, b * 2 + 2)
                for i in range(2):
                    if jt > 0:
                        pe.wait_ge(value_ready, (b * T + jt - 1) * 2 + i + 1)
                    nc.tensor.matmul(bank_t[i][:, :], xnT[:, jt * P:(jt + 1) * P], value_w[:, 4 * i:4 * i + 4, :],
                                     start=True, stop=True).then_inc(value_pe, 1)

            def q_rows(b, h):
                if h >= 2:
                    pe.wait_ge(q_relu_ready, b * H + h - 1)
                nc.tensor.matmul(bank_q[h % 2][:, :], q_rep[:, h, :], xnT[:], start=True, stop=True).then_inc(q_pe, 1)

            def attend(b, h):
                pe.wait_ge(weight_ready, b * H + h + 1)
                if h == 0:
                    pe.wait_ge(value_ready, (b + 1) * T * 2)
                for i in range(2):
                    pe.wait_ge(head_used, (b * H + h) * 2 + i + 1)
                    for it in (2 * i, 2 * i + 1):
                        for jt in range(T):
                            m = nc.tensor.matmul(o_ps[i][:, it % 2, :], weight[:, h % 2, jt, it * P:(it + 1) * P],
                                                 value[:, b % 2, jt, h, :], start=(jt == 0), stop=(jt == T - 1))
                    m.then_inc(head_pe, 1)

            stage1(0)
            stage2(0)
            stage3(0)
            for jt in range(T):
                values(0, jt)
            for h in range(H):
                q_rows(0, h)
            with pe.Fori(0, B - 1) as b:
                for h in range(H):
                    attend(b, h)
                    if h == 0:
                        stage1(b + 1)
                    if h == 1:
                        stage2(b + 1)
                    if h == 2:
                        stage3(b + 1)
                    if h >= 4:
                        values(b + 1, h - 4)
                        q_rows(b + 1, 2 * h - 8)
                        q_rows(b + 1, 2 * h - 7)
            for h in range(H):
                attend(B - 1, h)

        @block.vector
        def _(dve):
            chain = Chain(dve, vec_chain)
            nc.vector.memset(den[:], 0.0).then_inc(head_used, 2)
            dve.wait_ge(w_in, 8 * 16)
            dve.wait_ge(const_ready, 3)
            nc.vector.tensor_tensor(qk_sum[:, 0:1], qk_w[:, 0:1], qk_w[:, 1:2], ALU.add)
            nc.vector.tensor_tensor(qk_sum[:, 1:2], qk_b[:, 0:1], qk_b[:, 1:2], ALU.add)
            nc.vector.tensor_copy(fc_b_rep, fc_b[:].unsqueeze(2).broadcast_to([P, H, P]))
            dve.wait_ge(pe_w, 1)
            nc.vector.tensor_copy(fc_wT[:, 0:4, :], bank_t[0][:, :].rearrange("p (h d) -> p h d", h=4))
            nc.vector.tensor_copy(fc_wT[:, 4:8, :], bank_t[1][:, :].rearrange("p (h d) -> p h d", h=4)).then_inc(w_done, 1)
            dve.wait_ge(pe_w, 2)
            nc.vector.tensor_copy(value_w[:, 0:4, :], psum[2][:, :].rearrange("p (h d) -> p h d", h=4))
            nc.vector.tensor_copy(value_w[:, 4:8, :], psum[3][:, :].rearrange("p (h d) -> p h d", h=4))
            nc.vector.tensor_copy(head_qk[:], psum[4][:, 0:2 * H].rearrange("p (h c) -> p h c", c=2))
            nc.vector.tensor_copy(q_rep[:], psum[4][:, 0:2 * H:2].unsqueeze(2).broadcast_to([P, H, P]))
            nc.vector.tensor_scalar(logit_b[:], psum[4][:, 32:32 + H], qk_sum[:, 1:2], None, ALU.add)
            chain.link(nc.vector.tensor_tensor(out_b[:], psum[5][:, 0:D], fp_b[:], ALU.add))
            chain.link(nc.vector.tensor_reduce(mean_w[:], value_w[:].rearrange("p h o -> p o h"), AX, ALU.add))
            nc.vector.tensor_scalar(mean_w[:], mean_w[:], 1.0 / N, None, ALU.mult).then_inc(w_done, 1)

            def stage0(b):
                dve.wait_ge(in_ready, (b + 1) * 32)
                for it in range(T):
                    m = nc.vector.bn_stats(stats[:, it, :], x_all[:, b * T + it, :])
                chain.link(m)
                nc.vector.memset(wait_spot[:], 0.0)
                for it in range(T):
                    m = nc.vector.bn_aggr(mv[:, it, :], stats[:, it, :])
                chain.link(m)
                nc.vector.tensor_scalar(mv[:, :, 1], mv[:, :, 1], 1e-5, None, ALU.add).then_inc(var_ready, 1)
                dve.wait_ge(rstd_ready, b + 1)
                if later(b):
                    dve.wait_ge(xnT_pe, b)
                for it in range(T):
                    m = nc.vector.tensor_scalar(xn[:, it, :], x_all[:, b * T + it, :], mv[:, it, 0:1],
                                                rstd[:, it:it + 1], ALU.subtract, ALU.mult)
                m.then_inc(xn_ready, 1)

            def stage2(b):
                dve.wait_ge(k_pe, b + 1)
                nc.vector.tensor_copy(deg[:, bass.ds(b * T, T)], deg_ps)
                nc.vector.tensor_scalar(lone[:, b % 2, :], deg_ps, 0.0, None, ALU.is_equal)
                nc.vector.tensor_reduce(kmax[:], bank_k[0:H, :], AX, ALU.max)
                chain.link(nc.vector.tensor_reduce(xsum[:], xnT[:], AX, ALU.add))
                if later(b):
                    dve.wait_ge(kmax_pe, b)
                nc.vector.tensor_scalar(kmax_diag[:], ident[0:H, 0:H], kmax[:, 0:1], None, ALU.mult)
                nc.vector.tensor_scalar(xsum_rep[:], ones[:], xsum[:, 0:1], None, ALU.mult).then_inc(kdiag_ready, 1)

            def stage3(b):
                dve.wait_ge(kmax_pe, b + 1)
                chain.link(nc.vector.tensor_copy(kmax_all[:], kmax_ps))
                if later(b):
                    dve.wait_ge(kexp_ready, b)
                if later(b):
                    dve.wait_ge(q_relu_ready, b * H)
                nc.vector.tensor_tensor(kd[:], k_tok, kmax_all[:].unsqueeze(1).broadcast_to([P, T, H]), ALU.subtract)
                nc.vector.tensor_tensor(relu_b[:], kmax_all[:], logit_b[:], ALU.add).then_inc(kd_ready, 1)
                chain.link(nc.vector.tensor_tensor(acc[:, b % 2], xn[:], out_b[:].unsqueeze(1).broadcast_to([P, T, D]), ALU.add))
                for it in range(T):
                    m = nc.vector.scalar_tensor_tensor(out=acc[:, b % 2, it, :], in0=mean_ps,
                                                       scalar=lone[:, b % 2, it:it + 1], in1=acc[:, b % 2, it, :],
                                                       op0=ALU.mult, op1=ALU.add)
                m.then_inc(small_used, 1)
                dve.wait_ge(kexp_ready, b + 1)
                nc.vector.tensor_copy(value[:, b % 2, :, :, D], k_flat[:])

            def values(b, jt):
                for i in range(2):
                    dve.wait_ge(value_pe, (b * T + jt) * 2 + i + 1)
                    nc.vector.tensor_tensor(value[:, b % 2, jt, 4 * i:4 * i + 4, 0:D],
                                            bank_t[i][:, :].rearrange("p (h d) -> p h d", h=4),
                                            k_flat[:, jt, 4 * i:4 * i + 4].unsqueeze(2).broadcast_to([P, 4, D]),
                                            ALU.mult).then_inc(value_ready, 1)

            def weights(b, h):
                dve.wait_ge(q_row_ready, b * H + h + 1)
                for jt in range(T):
                    m = nc.vector.scalar_tensor_tensor(out=weight[:, h % 2, jt, :], in0=q_row[:, h, :],
                                                       scalar=k_steep[:, b % 2, jt, h:h + 1], in1=adjT[:, b, jt, :],
                                                       op0=ALU.max, op1=ALU.mult)
                m.then_inc(weight_ready, 1)

            def collect(b, h):
                for i in range(2):
                    dve.wait_ge(head_pe, (b * H + h) * 2 + i + 1)
                    its = slice(2 * i, 2 * i + 2)
                    chain.link(nc.vector.tensor_tensor(den[:, its], o_ps[i][:, :, D], lone[:, b % 2, its], ALU.add))
                    chain.link(nc.vector.reciprocal(rden[:, its], den[:, its]))
                    for it in (2 * i, 2 * i + 1):
                        m = nc.vector.scalar_tensor_tensor(out=acc[:, b % 2, it, :], in0=o_ps[i][:, it % 2, 0:D],
                                                           scalar=rden[:, it:it + 1], in1=acc[:, b % 2, it, :],
                                                           op0=ALU.mult, op1=ALU.add)
                    m.then_inc(head_used, 1)
                    dve.wait_ge(head_used, 2 + (b * H + h) * 2 + i + 1)

            def finish(b):
                nc.vector.tensor_copy(den[:, 0:1], den[:, 1:2]).then_inc(acc_ready, 1)
                dve.wait_ge(sig_ready, b + 1)
                chain.link(nc.vector.tensor_scalar(sig[:], sig[:], 1.0, None, ALU.add))
                chain.link(nc.vector.reciprocal(sig[:], sig[:]))
                nc.vector.tensor_tensor(x_all[:, bass.ds(b * T, T), :], x_all[:, bass.ds(b * T, T), :], sig[:],
                                        ALU.add).then_inc(x1_ready, 1)

            start = 2
            chain.turn(start, 0, 0)
            stage0(0)
            stage2(0)
            stage3(0)
            for jt in range(T):
                values(0, jt)
            start += chain.k
            turns_links = 2 + 1 + 2 + H * 4 + 2
            with dve.Fori(0, B - 1) as b:
                chain.turn(start, b, turns_links)
                for h in range(H):
                    weights(b, h)
                    if h == 0:
                        stage0(b + 1)
                    if h > 0:
                        collect(b, h - 1)
                    if h == 2:
                        stage2(b + 1)
                    if h == 3:
                        stage3(b + 1)
                    if h >= 5:
                        values(b + 1, h - 5)
                collect(b, H - 1)
                values(b + 1, T - 1)
                finish(b)
                assert chain.k == turns_links, chain.k
            chain.turn(start, B - 1, turns_links)
            for h in range(H):
                weights(B - 1, h)
                if h > 0:
                    collect(B - 1, h - 1)
            collect(B - 1, H - 1)
            finish(B - 1)



def route_tokens(nc, t, stage, x_all, expert_in, slot_of, share, ident, ident_bf, ones, neg_half, psum):
    def sb(name, shape, dt=F32):
        return stage.enter_context(nc.sbuf_tensor(name, shape, dt))

    def sem(name):
        return stage.enter_context(nc.semaphore(name))

    NT = B * T
    gate_w = sb("gate_w", [P, E])
    gate_b = sb("gate_b", [P, E])
    stats = sb("r_stats", [P, T, 6])
    mv_slot = sb("r_mv_slot", [P, T, 2])
    mv = sb("r_mv", [P, NT, 2])
    rstd = sb("r_rstd", [P, NT])
    wait_spot = sb("r_wait_spot", [P, 1])
    xn = sb("r_xn", [P, NT, D])
    xn_slot = sb("r_xn_slot", [P, 2, T, D])
    xnT = sb("r_xnT", [P, 2, N])
    upper = sb("upper", [P, P], BF16)
    all_ones = sb("all_ones", [P, P], BF16)
    logit = sb("logit", [P, NT, E])
    prob = sb("prob", [P, NT, E])
    top = sb("top", [P, NT])
    total = sb("total", [P, NT])
    rank = sb("rank", [P, NT, E])
    first = sb("first", [P, NT, E])
    hot = sb("hot", [P, NT, E])
    hot_bf = sb("hot_bf", [P, NT, E], BF16)
    before = sb("before", [P, E, NT + 1])
    place = sb("place", [P, NT])
    queue = sb("queue", [P, NT])
    kept = sb("kept", [P, NT])
    spare_i = sb("spare_i", [P, NT], mybir.dt.int32)
    spare = sb("spare", [P, NT])
    dest = sb("dest", [P, NT])
    dest_u = sb("dest_u", [P, NT], U32)
    zero = sb("zero", [P, CAP])

    w_in = sem("r_w_in")
    zero_ready = sem("zero_ready")
    zeroed = sem("zeroed")
    stats_ready = sem("r_stats_ready")
    rstd_ready = sem("r_rstd_ready")
    xn_ready = sem("r_xn_ready")
    xn_copied = sem("r_xn_copied")
    xnT_pe = sem("r_xnT_pe")
    xnT_ready = sem("r_xnT_ready")
    logit_pe = sem("logit_pe")
    chain_v = sem("r_vec_chain")
    chain_p = sem("r_pool_chain")
    consts_ready = sem("r_consts_ready")
    top_ready = sem("top_ready")
    prob_ready = sem("prob_ready")
    hot_ready = sem("hot_ready")
    count_pe = sem("count_pe")
    dest_ready = sem("dest_ready")
    scattered = sem("scattered")

    with nc.Block() as block:
        @block.sync
        def _(sp):
            sp.dma_start(gate_w[:], t["L0_ffn_gate_w"]).then_inc(w_in, 16)
            sp.dma_start(gate_b[:], t["L0_ffn_gate_b"].rearrange("(a n) -> a n", a=1).broadcast_to([P, E]))\
              .then_inc(w_in, 16)
            sp.wait_ge(zero_ready, 1)
            for e in range(E):
                sp.dma_start(expert_in[e * CAP:(e + 1) * CAP].rearrange("(p c) d -> p (c d)", p=P), zero[:])\
                  .then_inc(zeroed, 16)
            sp.wait_ge(zeroed, E * 16)

        @block.gpsimd
        def _(pool):
            nc.gpsimd.memset(zero[:], 0.0).then_inc(zero_ready, 1)
            chain = Chain(pool, chain_p)
            chain.link(nc.gpsimd.memset(upper[:], 1.0))
            nc.gpsimd.affine_select(out=upper[:], in_=upper[:], compare_op=ALU.is_ge, fill=0.0, base=0,
                                    pattern=[[1, P]], channel_multiplier=-1)
            nc.gpsimd.memset(all_ones[:], 1.0)
            for e in range(E):
                nc.gpsimd.memset(rank[:, :, e], float(E - e))
                nc.gpsimd.memset(first[:, :, e], float(e * CAP))
            chain.link(nc.gpsimd.iota(spare_i[:], pattern=[[P, NT]], base=E * CAP, channel_multiplier=1))
            nc.gpsimd.tensor_copy(spare[:], spare_i[:]).then_inc(consts_ready, 1)
            pool.wait_ge(stats_ready, 1)
            for k in range(4):
                n = slice(k * NT // 4, (k + 1) * NT // 4)
                m = nc.gpsimd.tensor_tensor(rstd[:, n], mv[:, n, 1], neg_half[:, 0:NT // 4], ALU.pow)
            m.then_inc(rstd_ready, 1)
            pool.wait_ge(dest_ready, 1)
            pool.wait_ge(zeroed, E * 16)
            for n in range(NT):
                nc.gpsimd.indirect_dma_start(out=expert_in[:, :], out_offset=bass.IndirectOffsetOnAxis(ap=dest_u[:, n:n + 1], axis=0),
                                             in_=xn[:, n, :], in_offset=None).then_inc(scattered, 16)
            pool.wait_ge(scattered, NT * 16)

        @block.scalar
        def _(act):
            with act.Fori(0, B // 2) as pair:
                for s in range(2):
                    b = pair * 2 + s
                    act.wait_ge(xn_ready, b + 1)
                    nc.scalar.activation(xn[:, bass.ds(b * T, T), :], xn_slot[:, s], ACT.Copy).then_inc(xn_copied, 1)
                    act.wait_ge(xnT_pe, b + 1)
                    nc.scalar.activation(xnT[:, s, :], psum.banks[s], ACT.Copy).then_inc(xnT_ready, 1)
            act.wait_ge(top_ready, 1)
            nc.scalar.activation(prob[:], prob[:], ACT.Exp).then_inc(prob_ready, 1)

        @block.tensor
        def _(pe):
            pe.wait_ge(w_in, 32)

            with pe.Fori(0, B // 2) as pair:
                for s in range(2):
                    b = pair * 2 + s
                    pe.wait_ge(xn_ready, b + 1)
                    for it in range(T):
                        m = nc.tensor.transpose(psum.banks[s][:, it * P:(it + 1) * P], xn_slot[:, s, it, :], ident[:])
                    m.then_inc(xnT_pe, 1)
                    pe.wait_ge(xnT_ready, b + 1)
                    for it in range(T):
                        m = nc.tensor.matmul(psum.logit[:, bass.ds((b * T + it) * E, E)],
                                             xnT[:, s, it * P:(it + 1) * P], gate_w[:], start=True, stop=True)
                    m.then_inc(logit_pe, 1)
            pe.wait_ge(consts_ready, 1)
            pe.wait_ge(hot_ready, 1)
            nc.tensor.matmul(psum.place[:, :], upper[:], hot_bf[:].rearrange("p n e -> p (n e)"), start=True, stop=True)
            nc.tensor.matmul(psum.count[:, :], all_ones[:], hot_bf[:].rearrange("p n e -> p (n e)"), start=True, stop=True)\
              .then_inc(count_pe, 1)

        @block.vector
        def _(dve):
            chain = Chain(dve, chain_v)
            with dve.Fori(0, B) as b:
                chain.turn(0, b, 3)
                for it in range(T):
                    m = nc.vector.bn_stats(stats[:, it, :], x_all[:, b * T + it, :])
                chain.link(m)
                nc.vector.memset(wait_spot[:], 0.0)
                for it in range(T):
                    m = nc.vector.bn_aggr(mv_slot[:, it, :], stats[:, it, :])
                chain.link(m)
                chain.link(nc.vector.tensor_copy(mv[:, bass.ds(b * T, T), :], mv_slot[:]))
            chain.turn(3 * B, 0, 0)
            chain.link(nc.vector.memset(wait_spot[:], 0.0))
            nc.vector.tensor_scalar(mv[:, :, 1], mv[:, :, 1], 1e-5, None, ALU.add).then_inc(stats_ready, 1)
            dve.wait_ge(rstd_ready, 1)

            def normalise(b, s):
                for it in range(T):
                    m = nc.vector.tensor_scalar(xn_slot[:, s, it, :], x_all[:, b * T + it, :], mv[:, b * T + it, 0:1],
                                                rstd[:, bass.ds(b * T + it, 1)], ALU.subtract, ALU.mult)
                m.then_inc(xn_ready, 1)

            normalise(0, 0)
            normalise(1, 1)
            with dve.Fori(1, B // 2) as pair:
                for s in range(2):
                    dve.wait_ge(xnT_ready, pair * 2 + s - 1)
                    normalise(pair * 2 + s, s)
            dve.wait_ge(w_in, 32)
            dve.wait_ge(consts_ready, 1)
            dve.wait_ge(logit_pe, B)
            chain.link(nc.vector.tensor_tensor(logit[:], psum.logit[:, :].rearrange("p (n e) -> p n e", e=E),
                                               gate_b[:].unsqueeze(1).broadcast_to([P, NT, E]), ALU.add))
            chain.link(nc.vector.tensor_reduce(top[:], logit[:], AX, ALU.max))
            top_e = top[:].unsqueeze(2).broadcast_to([P, NT, E])
            nc.vector.tensor_tensor(prob[:], logit[:], top_e, ALU.subtract).then_inc(top_ready, 1)
            chain.link(nc.vector.tensor_tensor(hot[:], logit[:], top_e, ALU.is_equal))
            chain.link(nc.vector.tensor_tensor(hot[:], hot[:], rank[:], ALU.mult))
            chain.link(nc.vector.tensor_reduce(total[:], hot[:], AX, ALU.max))
            chain.link(nc.vector.tensor_tensor(hot[:], hot[:], total[:].unsqueeze(2).broadcast_to([P, NT, E]), ALU.is_equal))
            nc.vector.tensor_copy(hot_bf[:], hot[:]).then_inc(hot_ready, 1)
            dve.wait_ge(prob_ready, 1)
            chain.link(nc.vector.tensor_reduce(total[:], prob[:], AX, ALU.add))
            chain.link(nc.vector.reciprocal(share[:], total[:]))
            dve.wait_ge(count_pe, 1)
            chain.link(nc.vector.memset(before[:], 0.0))
            counts = psum.count[:, :].rearrange("p (n e) -> p e n", e=E)
            for e in range(E):
                m = nc.vector.tensor_tensor_scan(before[:, e, 1:NT + 1], ones[:, 0:NT], counts[:, e, :], 0.0,
                                                 ALU.mult, ALU.add)
            chain.link(m)
            chain.link(nc.vector.tensor_tensor(prob[:], psum.place[:, :].rearrange("p (n e) -> p n e", e=E),
                                               before[:, :, 0:NT].rearrange("p e n -> p n e"), ALU.add))
            chain.link(nc.vector.tensor_tensor(prob[:], prob[:], hot[:], ALU.mult))
            chain.link(nc.vector.tensor_reduce(place[:], prob[:], AX, ALU.add))
            chain.link(nc.vector.tensor_tensor(prob[:], first[:], hot[:], ALU.mult))
            chain.link(nc.vector.tensor_reduce(queue[:], prob[:], AX, ALU.add))
            chain.link(nc.vector.tensor_scalar(kept[:], place[:], float(CAP), None, ALU.is_le))
            chain.link(nc.vector.tensor_scalar(dest[:], place[:], float(CAP), -1.0, ALU.min, ALU.add))
            chain.link(nc.vector.tensor_tensor(dest[:], dest[:], queue[:], ALU.add))
            nc.vector.tensor_copy(slot_of[:], dest[:])
            nc.vector.tensor_tensor(share[:], share[:], kept[:], ALU.mult)
            chain.link(nc.vector.tensor_tensor(dest[:], dest[:], spare[:], ALU.subtract))
            chain.link(nc.vector.tensor_tensor(dest[:], dest[:], kept[:], ALU.mult))
            chain.link(nc.vector.tensor_tensor(dest[:], dest[:], spare[:], ALU.add))
            nc.vector.tensor_copy(dest_u[:], dest[:]).then_inc(dest_ready, 1)


def run_experts(nc, t, stage, expert_in, expert_out, ident, psum):
    def sb(name, shape, dt=F32):
        return stage.enter_context(nc.sbuf_tensor(name, shape, dt))

    def sem(name):
        return stage.enter_context(nc.semaphore(name))

    C = CAP // P
    FK = F // P
    w1 = sb("w1", [P, 2, F])
    w2 = sb("w2", [P, E, FK, D])
    b1 = sb("b1", [P, E, FK])
    b2 = sb("b2", [P, E, D])
    rows = sb("rows", [P, 2, C, D])
    rowsT = sb("rowsT", [P, 2, C * P])
    hidden = sb("hidden", [P, 2, FK, C * P])
    y = sb("y", [P, 2, C, D])
    CHUNKS = [(0, 4), (4, 8), (8, C)]

    b1_in = sem("b1_in")
    w2_in = sem("w2_in")
    rows_in = sem("rows_in")
    rowsT_pe = sem("rowsT_pe")
    rowsT_ready = sem("rowsT_ready")
    hidden_pe = sem("hidden_pe")
    hidden_ready = sem("hidden_ready")
    y_pe = sem("y_pe")
    y_ready = sem("y_ready")
    y_stored = sem("y_stored")

    bank_t, bank_h, bank_y = psum.banks[0:3], psum.banks[3:6], [psum.banks[6], psum.banks[7], psum.banks[6]]
    in_v = expert_in[0:E * CAP].rearrange("(e p c) d -> e p c d", e=E, p=P)
    out_v = expert_out.rearrange("(e p c) d -> e p c d", e=E, p=P)

    with nc.Block() as block:
        @block.sync
        def _(sp):
            sp.dma_start(rows[:, 0], in_v[0]).then_inc(rows_in, 16)
            sp.dma_start(w1[:, 0], t["L0_ffn_w1"][0]).then_inc(rows_in, 16)
            with nc.allow_non_contiguous_dma("small biases"):
                sp.dma_start(b1[:], t["L0_ffn_b1"].rearrange("e (k p) -> p e k", p=P)).then_inc(b1_in, 16)
            sp.dma_start(w2[:], t["L0_ffn_w2"].rearrange("e (k p) d -> p e k d", p=P)).then_inc(w2_in, 16)
            sp.dma_start(b2[:], t["L0_ffn_b2"].rearrange("(a e) d -> a e d", a=1).broadcast_to([P, E, D])).then_inc(w2_in, 16)
            sp.wait_ge(rows_in, 32)
            sp.dma_start(rows[:, 1], in_v[1]).then_inc(rows_in, 16)
            sp.dma_start(w1[:, 1], t["L0_ffn_w1"][1]).then_inc(rows_in, 16)
            with sp.Fori(2, E) as e:
                sp.wait_ge(rows_in, e * 32)
                sp.wait_ge(hidden_pe, e * 12 - 12)
                sp.dma_start(rows[:, e % 2], in_v[e]).then_inc(rows_in, 16)
                sp.dma_start(w1[:, e % 2], t["L0_ffn_w1"][e]).then_inc(rows_in, 16)

        @block.gpsimd
        def _(pool):
            def store(e):
                pool.wait_ge(y_ready, (e + 1) * 3)
                if later(e):
                    pool.wait_ge(y_stored, e * 16)
                nc.gpsimd.dma_start(out_v[e], y[:, e % 2]).then_inc(y_stored, 16)

            store(0)
            with pool.Fori(1, E) as e:
                store(e)
            pool.wait_ge(y_stored, E * 16)

        @block.scalar
        def _(act):
            act.wait_ge(b1_in, 16)

            def turn(e):
                for k, (lo, hi) in enumerate(CHUNKS):
                    act.wait_ge(rowsT_pe, e * 3 + k + 1)
                    nc.scalar.activation(rowsT[:, e % 2, lo * P:hi * P], bank_t[k][:, 0:(hi - lo) * P], ACT.Copy)\
                      .then_inc(rowsT_ready, 1)

            def relu(e):
                for f in range(FK):
                    for k, (lo, hi) in enumerate(CHUNKS):
                        act.wait_ge(hidden_pe, e * 12 + f * 3 + k + 1)
                        nc.scalar.activation(hidden[:, e % 2, f, lo * P:hi * P], bank_h[k][:, 0:(hi - lo) * P], ACT.Relu,
                                             bias=b1[:, e, f:f + 1]).then_inc(hidden_ready, 1)

            turn(0)
            with act.Fori(0, E - 1) as e:
                relu(e)
                turn(e + 1)
            relu(E - 1)

        @block.tensor
        def _(pe):
            def turn(e, s):
                pe.wait_ge(rows_in, (e + 1) * 32)
                for k, (lo, hi) in enumerate(CHUNKS):
                    for c in range(lo, hi):
                        m = nc.tensor.transpose(bank_t[k][:, (c - lo) * P:(c - lo + 1) * P], rows[:, s, c, :], ident[:])
                    m.then_inc(rowsT_pe, 1)

            def up(e, s):
                for f in range(FK):
                    for k, (lo, hi) in enumerate(CHUNKS):
                        if f == 0:
                            pe.wait_ge(rowsT_ready, e * 3 + k + 1)
                        if f > 0 or later(e):
                            pe.wait_ge(hidden_ready, e * 12 + f * 3 + k - 2)
                        nc.tensor.matmul(bank_h[k][:, 0:(hi - lo) * P], w1[:, s, f * P:(f + 1) * P],
                                         rowsT[:, s, lo * P:hi * P], start=True, stop=True).then_inc(hidden_pe, 1)

            def down(e, s):
                pe.wait_ge(hidden_ready, (e + 1) * 12)
                for k, (lo, hi) in enumerate(CHUNKS):
                    if k == 2:
                        pe.wait_ge(y_ready, e * 3 + 1)
                    elif later(e):
                        pe.wait_ge(y_ready, e * 3)
                    for c in range(lo, hi):
                        for f in range(FK):
                            m = nc.tensor.matmul(bank_y[k][:, (c - lo) * D:(c - lo + 1) * D],
                                                 hidden[:, s, f, c * P:(c + 1) * P], w2[:, e, f, :],
                                                 start=(f == 0), stop=(f == FK - 1))
                    m.then_inc(y_pe, 1)

            turn(0, 0)
            up(0, 0)
            turn(1, 1)
            pe.wait_ge(w2_in, 32)
            down(0, 0)
            with pe.Fori(0, E // 2 - 1) as pair:
                for s in (1, 0):
                    e = pair * 2 + 2 - s
                    up(e, s)
                    turn(e + 1, 1 - s)
                    down(e, s)
            up(E - 1, 1)
            down(E - 1, 1)

        @block.vector
        def _(dve):
            dve.wait_ge(w2_in, 32)

            def turn(e):
                for k, (lo, hi) in enumerate(CHUNKS):
                    dve.wait_ge(y_pe, e * 3 + k + 1)
                    if later(e - 1):
                        dve.wait_ge(y_stored, e * 16 - 16)
                    nc.vector.tensor_tensor(y[:, e % 2, lo:hi, :],
                                            bank_y[k][:, 0:(hi - lo) * D].rearrange("p (c d) -> p c d", d=D),
                                            b2[:, bass.ds(e, 1), :].broadcast_to([P, hi - lo, D]), ALU.add).then_inc(y_ready, 1)

            turn(0)
            turn(1)
            with dve.Fori(2, E) as e:
                turn(e)


def gcn_layer(nc, t, stage, x_all, adjT, deg, expert_out, slot_of, share, ident, ident_bf, neg_half, psum):
    def sb(name, shape, dt=F32):
        return stage.enter_context(nc.sbuf_tensor(name, shape, dt))

    def sem(name):
        return stage.enter_context(nc.semaphore(name))

    NT = B * T
    w = sb("g_w", [P, D])
    wT = sb("g_wT", [P, D])
    bias = sb("g_bias", [P, D])
    y_in = sb("y_in", [P, NT, D])
    y_ok = sb("y_ok", [P, 2, T, D])
    same = sb("same", [P, 2, T, D])
    finite = sb("finite", [P, 2, T, D], U32)
    stats = sb("g_stats", [P, T, 6])
    mv_slot = sb("g_mv_slot", [P, T, 2])
    y_w = sb("y_w", [P, 2, T, D])
    mv = sb("g_mv", [P, NT, 2])
    rstd = sb("g_rstd", [P, NT])
    dinv = sb("dinv", [P, NT])
    scale = sb("g_scale", [P, NT])
    wait_spot = sb("g_wait_spot", [P, 1])
    u = sb("u", [P, 2, T, D])
    u_part = sb("u_part", [P, 2, 3, T, D], BF16)
    hT = sb("hT", [P, 2, N])
    msg = sb("msg", [P, 2, T, D])

    w_in = sem("g_w_in")
    wT_pe = sem("g_wT_pe")
    wT_ready = sem("g_wT_ready")
    gathered = [sem(f"gathered{q}") for q in range(4)]
    y_weighted = sem("y_weighted")
    y_checked = sem("y_checked")
    chain_v = sem("g_vec_chain")
    chain_p = sem("g_pool_chain")
    x2_ready = sem("x2_ready")
    stats_ready = sem("g_stats_ready")
    dinv_ready = sem("dinv_ready")
    u_ready = sem("u_ready")
    high_ready = sem("high_ready")
    rest_ready = sem("rest_ready")
    mid_ready = sem("mid_ready")
    parts_ready = sem("parts_ready")
    agg_pe = sem("agg_pe")
    hT_ready = sem("hT_ready")
    out_pe = sem("g_out_pe")
    out_used = sem("g_out_used")

    with nc.Block() as block:
        @block.sync
        def _(sp):
            sp.dma_start(w[:], t["L1_gnn_W"]).then_inc(w_in, 16)
            sp.dma_start(bias[:], t["L1_gnn_b"].rearrange("(a n) -> a n", a=1).broadcast_to([P, D])).then_inc(w_in, 16)

        @block.gpsimd
        def _(pool):
            chain = Chain(pool, chain_p)
            for q in range(4):
                for n in range(q * NT // 4, (q + 1) * NT // 4):
                    nc.gpsimd.indirect_dma_start(out=y_in[:, n, :], out_offset=None, in_=expert_out[:, :],
                                                 in_offset=bass.IndirectOffsetOnAxis(ap=slot_of[:, n:n + 1], axis=0))\
                      .then_inc(gathered[q], 16)

            def check(b, s):
                pool.wait_ge(y_weighted, b + 1)
                nc.gpsimd.tensor_tensor(y_ok[:, s], y_ok[:, s], same[:, s], ALU.mult).then_inc(y_checked, 1)

            check(0, 0)
            check(1, 1)
            with pool.Fori(1, B // 2) as pair:
                for s in range(2):
                    check(pair * 2 + s, s)
            pool.wait_ge(stats_ready, 1)
            for k in range(4):
                n = slice(k * NT // 4, (k + 1) * NT // 4)
                nc.gpsimd.tensor_tensor(rstd[:, n], mv[:, n, 1], neg_half[:, 0:NT // 4], ALU.pow)
                m = nc.gpsimd.tensor_tensor(dinv[:, n], deg[:, n], neg_half[:, 0:NT // 4], ALU.pow)
            chain.link(m)
            nc.gpsimd.tensor_tensor(scale[:], rstd[:], dinv[:], ALU.mult).then_inc(dinv_ready, 1)

        @block.scalar
        def _(act):
            act.wait_ge(wT_pe, 1)
            nc.scalar.activation(wT[:], psum.banks[7][:, 0:D], ACT.Copy).then_inc(wT_ready, 1)

            def turn(b):
                act.wait_ge(u_ready, b + 1)
                nc.scalar.activation(u_part[:, b % 2, 0], u[:, b % 2], ACT.Copy).then_inc(high_ready, 1)
                act.wait_ge(rest_ready, b + 1)
                nc.scalar.activation(u_part[:, b % 2, 1], u[:, b % 2], ACT.Copy).then_inc(mid_ready, 1)

            def move(b):
                act.wait_ge(agg_pe, b + 1)
                nc.scalar.activation(hT[:, b % 2, :], psum.whole[:, b % 2, :], ACT.Copy).then_inc(hT_ready, 1)

            turn(0)
            with act.Fori(0, B - 1) as b:
                turn(b + 1)
                move(b)
            move(B - 1)

        @block.tensor
        def _(pe):
            pe.wait_ge(w_in, 32)
            nc.tensor.transpose(psum.banks[7][:, 0:D], w[:], ident[:]).then_inc(wT_pe, 1)
            pe.wait_ge(wT_ready, 1)

            def aggregate(b):
                pe.wait_ge(parts_ready, b + 1)
                for part in range(3):
                    for jt in range(T):
                        nc.tensor.matmul(psum.whole[:, b % 2, :], u_part[:, b % 2, part, jt, :], adjT[:, b, jt, :],
                                         start=(part == 0 and jt == 0), stop=False, skip_group_check=True)
                        m = nc.tensor.matmul(psum.whole[:, b % 2, jt * P:(jt + 1) * P], u_part[:, b % 2, part, jt, :],
                                             ident_bf[:], start=False, stop=(part == 2 and jt == T - 1),
                                             skip_group_check=True)
                m.then_inc(agg_pe, 1)

            def project(b, s):
                pe.wait_ge(hT_ready, b + 1)
                if later(b - 1):
                    pe.wait_ge(out_used, b - 1)
                for it in range(T):
                    m = nc.tensor.matmul(psum.whole[:, 2 + s, it * P:(it + 1) * P], hT[:, s, it * P:(it + 1) * P],
                                         wT[:], start=True, stop=True)
                m.then_inc(out_pe, 1)

            aggregate(0)
            aggregate(1)
            project(0, 0)
            aggregate(2)
            project(1, 1)
            with pe.Fori(1, B // 2 - 1) as pair:
                for s in range(2):
                    aggregate(pair * 2 + s + 1)
                    project(pair * 2 + s, s)
            aggregate(B - 1)
            project(B - 2, 0)
            project(B - 1, 1)

        @block.vector
        def _(dve):
            chain = Chain(dve, chain_v)
            chain.link(nc.vector.tensor_scalar(deg[:], deg[:], 1.0, None, ALU.add))
            dve.wait_ge(w_in, 32)

            def weigh(b, s):
                chain.link(nc.vector.tensor_tensor(y_w[:, s], y_in[:, bass.ds(b * T, T), :],
                                                   share[:, bass.ds(b * T, T)].unsqueeze(2).broadcast_to([P, T, D]),
                                                   ALU.mult))
                nc.vector.tensor_scalar(y_ok[:, s], y_w[:, s], 1e4, -1e4, ALU.min, ALU.max)
                nc.vector.tensor_tensor(same[:, s], y_w[:, s], y_w[:, s], ALU.is_equal)
                nc.vector.tensor_scalar(finite[:, s], y_w[:, s], 0.0, 0.0, ALU.mult, ALU.is_equal).then_inc(y_weighted, 1)
                dve.wait_ge(y_weighted, b + 1)

            def add(b, s):
                dve.wait_ge(y_checked, b + 1)
                chain.link(nc.vector.copy_predicated(y_ok[:, s], finite[:, s], y_w[:, s]))
                xb = x_all[:, bass.ds(b * T, T), :]
                nc.vector.tensor_tensor(xb, xb, y_ok[:, s], ALU.add).then_inc(x2_ready, 1)
                dve.wait_ge(x2_ready, b + 1)
                for it in range(T):
                    m = nc.vector.bn_stats(stats[:, it, :], x_all[:, b * T + it, :])
                chain.link(m)
                nc.vector.memset(wait_spot[:], 0.0)
                for it in range(T):
                    m = nc.vector.bn_aggr(mv_slot[:, it, :], stats[:, it, :])
                chain.link(m)
                chain.link(nc.vector.tensor_copy(mv[:, bass.ds(b * T, T), :], mv_slot[:]))

            dve.wait_ge(gathered[0], NT // 4 * 16)
            weigh(0, 0)
            start = chain.k
            for q in range(4):
                with dve.Fori(q * B // 8, (q + 1) * B // 8 - 1) as pair:
                    for s in range(2):
                        chain.turn(start, pair * 2 + s, 5)
                        weigh(pair * 2 + s + 1, 1 - s)
                        add(pair * 2 + s, s)
                b = (q + 1) * B // 4 - 2
                chain.turn(start, b, 5)
                weigh(b + 1, 1)
                add(b, 0)
                chain.turn(start, b + 1, 5)
                if q < 3:
                    dve.wait_ge(gathered[q + 1], NT // 4 * 16)
                    weigh(b + 2, 0)
                add(b + 1, 1)
            chain.turn(start + chain.k, B - 1, 5)
            chain.k = 0
            chain.link(nc.vector.memset(wait_spot[:], 0.0))
            nc.vector.tensor_scalar(mv[:, :, 1], mv[:, :, 1], 1e-5, None, ALU.add).then_inc(stats_ready, 1)
            dve.wait_ge(dinv_ready, 1)
            start = 1 + 3 * B + 1

            def split(b):
                if not isinstance(b, int):
                    dve.wait_ge(agg_pe, b - 1)
                for it in range(T):
                    m = nc.vector.tensor_scalar(u[:, b % 2, it, :], x_all[:, b * T + it, :], mv[:, b * T + it, 0:1],
                                                scale[:, bass.ds(b * T + it, 1)], ALU.subtract, ALU.mult)
                m.then_inc(u_ready, 1)
                dve.wait_ge(high_ready, b + 1)
                nc.vector.tensor_tensor(u[:, b % 2], u[:, b % 2], u_part[:, b % 2, 0], ALU.subtract).then_inc(rest_ready, 1)
                dve.wait_ge(mid_ready, b + 1)
                nc.vector.tensor_tensor(u_part[:, b % 2, 2], u[:, b % 2], u_part[:, b % 2, 1], ALU.subtract).then_inc(parts_ready, 1)

            def update(b):
                dve.wait_ge(out_pe, b + 1)
                for it in range(T):
                    m = nc.vector.scalar_tensor_tensor(out=msg[:, b % 2, it, :], in0=psum.whole[:, 2 + b % 2, it * P:(it + 1) * P],
                                                       scalar=dinv[:, bass.ds(b * T + it, 1)], in1=bias[:],
                                                       op0=ALU.mult, op1=ALU.add)
                m.then_inc(out_used, 1)
                dve.wait_ge(out_used, b + 1)
                xb = x_all[:, bass.ds(b * T, T), :]
                nc.vector.scalar_tensor_tensor(out=xb, in0=msg[:, b % 2], scalar=0.0, in1=xb, op0=ALU.max, op1=ALU.add)

            split(0)
            split(1)
            with dve.Fori(0, B - 2) as b:
                update(b)
                split(b + 2)
            update(B - 2)
            update(B - 1)


NH, NX, HD = 4, 4, 32
GROUPS = [(sc, tc) for sc in range(T) for tc in range(sc + 1)]
MAX_PARTS = [(0, (0, 1, 2, 3)), (1, (0, 1)), (1, (2, 3))] + [(sc, (e,)) for sc in (2, 3) for e in range(NX)]


def attention_schedule(pre, post):
    beside = {}

    def put(at, *jobs):
        beside.setdefault(at, []).extend(jobs)

    put(0, ("max_split", 1))
    for sc, at in ((1, (0, 0, 1, 1)), (2, (5, 6, 7, 8)), (3, (11, 11, 13, 13))):
        for n in range(NH):
            put(at[n], ("negmax", n, sc))
    if pre:
        put(1, ("norm_x",))
        put(2, ("scale_x",))
        put(3, ("xT", 0), ("xT", 1))
        put(4, ("sx",))
        for e in range(NX):
            put(5 + e, ("q", e))
            put(6 + e, ("mid", e))
        put(9, ("k",), ("v",))
        put(10, ("mid", NX))
        for k, job in enumerate(MAX_JOBS):
            put(18 + k // 2, job)
        put(26, ("max_split", 0))
        for n in range(NH):
            put(32 + 2 * n, ("negmax", n, 0))
    if post:
        put(2, ("tok", 3), ("gate", 3))
        put(3, ("mix_logits",))
        put(10, ("mix",), ("norm_mix",))
        put(12, ("scale_mix",))
    put(14, ("tok", 0), ("gate", 0))
    if post:
        put(14, ("fxT",))
        put(15, ("fc1",))
        put(16, ("fc2",), ("norm_out",))
    put(17, ("tok", 1), ("gate", 1))
    if post:
        put(18, ("scale_out",))
        put(19, ("foT",))
        put(20, ("fgate",))
        put(21, ("leave",))
    put(29, ("tok", 2), ("gate", 2))
    order = []
    for g, (sc, tc) in enumerate(GROUPS):
        for n in range(NH):
            order.append(("score", g, n))
            if n == NH - 1:
                order += after_values(g - 1) if g > 0 else [("begin",)]
            order += beside.get(4 * g + n, [])
    return order + after_values(len(GROUPS) - 1)


def after_values(g):
    sc, tc = GROUPS[g]
    return [("values", g)] + ([("collect", sc)] if tc == sc else [])


SIDE_JOBS = ("xT", "sx", "q", "k", "v", "max", "negmax", "tok", "gate", "fxT", "fc1", "fc2", "foT", "fgate")
MAX_JOBS = [("max", n, k) for k in range(len(MAX_PARTS)) for n in range(NH)]
FIRST_MAXIMA = sum(MAX_PARTS[job[2]][0] < T // 2 for job in MAX_JOBS)
PRE_JOBS = [("norm_x",), ("scale_x",), ("xT", 0), ("xT", 1), ("sx",)] \
    + [job for e in range(NX) for job in (("q", e), ("mid", e))] + [("k",), ("mid", NX), ("v",)] \
    + MAX_JOBS[:FIRST_MAXIMA] + [("max_split", 0)] + MAX_JOBS[FIRST_MAXIMA:] + [("negmax", n, 0) for n in range(NH)]
POST_JOBS = [("tok", 3), ("gate", 3), ("mix_logits",), ("mix",), ("norm_mix",), ("scale_mix",), ("fxT",), ("fc1",),
             ("fc2",), ("norm_out",), ("scale_out",), ("foT",), ("fgate",), ("leave",)]


def side_count(order):
    return sum(job[0] in SIDE_JOBS for job in order)


class SideUse:

    def __init__(self):
        self.base, self.k = 0, 0

    def turn(self, each):
        self.base, self.k = each, 0

    def use(self):
        bank, nth = self.k % 2, self.k // 2 + 1
        self.k += 1
        return bank, self.base + nth


def attention_layer(nc, t, stage, x_all, out, ident, ident_bf, ones, neg_half, psum):
    def sb(name, shape, dt=F32):
        return stage.enter_context(nc.sbuf_tensor(name, shape, dt))

    def sem(name):
        return stage.enter_context(nc.semaphore(name))

    SCALE = float(HD) ** 0.5
    LOADS = 7 * NH + 10
    VEC_LINKS = 54
    NAT = 9
    prob = sb("a_prob", [P, 2, NH, NX * P])
    whole = prob[:].rearrange("p a n s -> p (a n s)").rearrange("p (k c) -> p k c", c=P)
    nat, nat_gate, nat_fgate = whole[:, 0:NAT, :], whole[0:NH * NX, NAT:NAT + NX, :], whole[0:NH, NAT + NX, :]
    turned = sb("turned", [P, NAT, P])
    gate_w = sb("a_gate_w", [P, NX, NH * NX])
    fgate_w = sb("a_fgate_w", [P, NH])
    hl_b = sb("hl_b", [P, 1])
    hl_b_row = sb("hl_b_row", [P, P])
    gate_b = sb("a_gate_b", [P, NH * NX])
    ln_g, ln_b, fn_g, fn_b, fc2_b = (sb(n, [P, HD]) for n in ("ln_g", "ln_b", "fn_g", "fn_b", "fc2_b"))
    fc1_b = sb("fc1_b", [P, 1])
    wq_t, wk_t, wv_t, fc1_t, fc2_t, hl_t = turned[:, 0:4, :], turned[:, 4, :], turned[:, 5, :], turned[:, 6, :], \
        turned[:, 7, :], turned[:, 8, :]
    mask_qk = sb("mask_qk", [P, P], BF16)
    mask_kq = sb("mask_kq", [P, NX, P], BF16)

    stats = sb("a_stats", [P, T, 6])
    mv = sb("a_mv", [P, T, 2])
    rstd = sb("a_rstd", [P, T])
    spot = sb("a_spot", [P, 1])
    xn = sb("a_xn", [P, T, D])
    xnT = sb("a_xnT", [P, N])
    sxT = sb("sxT", [P, N])
    not_pad = sb("not_pad", [P, 2, N], BF16)
    resid = sb("resid", [P, T, D])
    q_hi = sb("q_hi", [P, NX, N], BF16)
    q_mid = sb("q_mid", [P, NX, N], BF16)
    q_lo = sb("q_lo", [P, NX, N], BF16)
    q_rest = sb("q_rest", [P, NX, N])
    k_hi = sb("k_hi", [P, N], BF16)
    k_mid = sb("k_mid", [P, N], BF16)
    k_lo = sb("k_lo", [P, N], BF16)
    k_rest = sb("k_rest", [P, N])
    q1 = sb("q1", [P, 2, NH, NX, N], BF16)
    q2 = sb("q2", [P, 2, NH, NX, N], BF16)
    k1 = sb("k1", [P, 2, NH, N], BF16)
    k2 = sb("k2", [P, 2, NH, N], BF16)
    v_next = sb("v_next", [P, T, D])
    v_now = sb("v_now", [P, T, D])
    top = sb("a_top", [P, T, NH, NX])
    neg_top = sb("neg_top", [P, NH * T * NX])
    neg_part = sb("neg_part", [P, NH * T * NX, HD], BF16)
    den = sb("a_den", [P, NX, P])
    att = sb("att", [P, 2, NX, P])
    tok = sb("tok", [P, T, NX, P])
    glog = sb("glog", [P, T, NH, NX])
    gprod = sb("gprod", [P, NX, NH, NX])
    rden = sb("a_rden", [P, T, NX, NH])
    gl = sb("gl", [P, T, NH, NX])
    gtop = sb("gtop", [P, T, NH])
    mixw = sb("mixw", [P, NX, P])
    y = sb("a_y", [P, T, D])
    yc = sb("a_yc", [P, T, D])
    sq = mixw
    s16 = sb("s16", [P, T * NH])
    r16 = sb("r16", [P, T * NH])
    hn = sb("hn", [P, T, D])
    fxT = sb("fxT", [P, N])
    h1 = mixw[:].rearrange("p e c -> p (e c)")
    fo, foT = y, fxT
    fl = gtop
    fmax = sb("fmax", [P, T])

    w_in = sem("a_w_in")
    zeroed = sem("a_zeroed")
    w_pe = sem("a_w_pe")
    w_ready = sem("a_w_ready")
    masks_ready = sem("masks_ready")
    chain_v = sem("a_vec_chain")
    chain_p = sem("a_pool_chain")
    chain_a = sem("a_act_chain")
    side_full = [sem("side_full0"), sem("side_full1")]
    var_ready = sem("a_var_ready")
    rstd_ready = sem("a_rstd_ready")
    xn_ready = sem("a_xn_ready")
    xnT_ready = sem("a_xnT_ready")
    sxT_ready = sem("sxT_ready")
    hi_ready = sem("hi_ready")
    rest_ready = sem("a_rest_ready")
    mid_ready = sem("a_mid_ready")
    lo_ready = sem("lo_ready")
    stack_in = sem("stack_in")
    top_split = sem("top_split")
    negmax_ready = sem("negmax_ready")
    v_ready = sem("v_ready")
    v_now_ready = sem("v_now_ready")
    score_pe = [sem(f"score_pe{n}") for n in range(NH)]
    prob_ready = [sem(f"prob_ready{n}") for n in range(NH)]
    values_pe = sem("values_pe")
    banks_left = sem("banks_left")
    att_ready = sem("att_ready")
    den_ready = sem("den_ready")
    resid_ready = sem("resid_ready")
    top_ready = sem("a_top_ready")
    tok_copied = sem("tok_copied")
    tok_ready = sem("tok_ready")
    y_biased = sem("y_biased")
    gl_ready = sem("gl_ready")
    gexp_ready = sem("gexp_ready")
    sum_ready = sem("sum_ready")
    pow_ready = sem("pow_ready")
    hn_ready = sem("hn_ready")
    fxT_ready = sem("fxT_ready")
    h1_ready = sem("h1_ready")
    h1m_ready = sem("h1m_ready")
    fo_ready = sem("fo_ready")
    foT_ready = sem("foT_ready")
    fl_ready = sem("fl_ready")
    fexp_ready = sem("fexp_ready")
    x4_ready = sem("x4_ready")
    stored = sem("stored")

    side = psum.banks[6:8]
    STACK_DMAS = NH * 12
    FIRST, MID, LAST = (attention_schedule(*f) for f in ((True, False), (True, True), (False, True)))
    NG = len(GROUPS)
    NEG = NH * T
    RES_JOBS = [job for _ in range(NH) for job in (("xT", 0), ("xT", 1), ("sx",))]
    BEFORE = side_count(RES_JOBS) + side_count(PRE_JOBS)
    assert side_count(RES_JOBS) % 2 == 0 and side_count(MID) % 2 == 0 and (BEFORE + side_count(FIRST)) % 2 == 0

    def run_turns(eng, handle, chain=None, links=0, begins=None):
        side_use = SideUse()
        for r in range(NH):
            for job in [("norm_x",), ("scale_x",), ("xT", 0), ("xT", 1), ("resid",)]:
                handle(job, r - NH, side_use.use() if job[0] in SIDE_JOBS + ("resid",) else None)

        def turn(order, b):
            for job in order:
                graph = b + 1 if job in PRE_JOBS else b - 1 if job in POST_JOBS else b
                handle(job, graph, side_use.use() if job[0] in SIDE_JOBS else None)

        turn(PRE_JOBS, -1)
        turn(FIRST, 0)
        if chain:
            start = chain.k
        each = (BEFORE + side_count(FIRST)) // 2
        with eng.Fori(1, B - 1) as b:
            if begins:
                begins(b)
            side_use.turn((b - 1) * (side_count(MID) // 2) + each)
            if chain:
                chain.turn(start, b - 1, links)
            turn(MID, b)
            if chain:
                assert chain.k == links, chain.k
        if begins:
            begins(B - 1)
        side_use.turn((B - 2) * (side_count(MID) // 2) + each)
        if chain:
            chain.turn(start, B - 2, links)
        turn(LAST, B - 1)
        turn(POST_JOBS, B)

    def slot(b):
        return b % 2

    def read(job, b):
        name, arg = job[0], job[1:]
        if name == "max":
            return top_ready, b * len(MAX_JOBS) + MAX_JOBS.index(job) + 1
        if name == "negmax":
            return negmax_ready, b * NEG + arg[1] * NH + arg[0] + 1
        if name in ("q", "k"):
            return rest_ready, b * (NX + 1) + (arg[0] if arg else NX) + 1
        if name in ("tok", "gate"):
            return {"tok": tok_copied, "gate": tok_ready}[name], b * T + arg[0] + 1
        if name == "xT":
            return xnT_ready, (b + NH) * 2 + arg[0] + 1
        if name == "resid":
            return resid_ready, b + NH + 1
        return {"sx": sxT_ready, "v": v_ready, "fxT": fxT_ready, "fc1": h1_ready, "fc2": y_biased, "foT": foT_ready,
                "fgate": fl_ready}[name], b + 1

    with nc.Block() as block:
        @block.sync
        def _(sp):
            sp.wait_ge(zeroed, 1)
            loads = []
            for n in range(NH):
                d = slice(n * HD, (n + 1) * HD)
                loads += [(nat[d, 0:NX, d], t["L1_ffn_wq"][n].rearrange("e o d -> o e d")),
                          (nat[d, 4, d], t["L1_ffn_wk"][n]),
                          (nat[d, 5, d], t["L1_ffn_wv"][n]),
                          (nat[d, 6, d], t["L1_ffn_fc1_w"]),
                          (nat[d, 7, d], t["L1_ffn_fc2_w"]),
                          (nat_gate[n * NX:(n + 1) * NX, :, d], t["L1_ffn_gate_w"][n].rearrange("g (e d) -> g e d", e=NX)),
                          (fc1_b[d, :], t["L1_ffn_fc1_b"].rearrange("(p a) -> p a", a=1))]

            def row(src, width):
                return src.rearrange("(a n) -> a n", a=1).broadcast_to([P, width])

            loads += [(nat[:, 8, :], t["L1_ffn_hl_w"].rearrange("n d h -> (n d) h")),
                      (nat_fgate, t["L1_ffn_fgate_w"]),
                      (hl_b[:], t["L1_ffn_hl_b"].rearrange("n (d a) -> (n d) a", a=1)),
                      (hl_b_row[:], row(t["L1_ffn_hl_b"].rearrange("n d -> (n d)"), P)),
                      (gate_b[:], row(t["L1_ffn_gate_b"].rearrange("n e -> (n e)"), NH * NX)),
                      (ln_g[:], row(t["L1_ffn_ln_g"], HD)), (ln_b[:], row(t["L1_ffn_ln_b"], HD)),
                      (fn_g[:], row(t["L1_ffn_fnorm_g"], HD)), (fn_b[:], row(t["L1_ffn_fnorm_b"], HD)),
                      (fc2_b[:], row(t["L1_ffn_fc2_b"], HD))]
            assert len(loads) == LOADS
            for dst, src in loads:
                with nc.allow_non_contiguous_dma("small weights"):
                    sp.dma_start(dst, src).then_inc(w_in, 16)

            def place(b, placed):
                for n in range(NH):
                    d = slice(n * HD, (n + 1) * HD)
                    for dst, g, part in placed:
                        sp.dma_start(dst[g * HD:(g + 1) * HD, slot(b), n], part[d]).then_inc(stack_in, 16)

            def stack(b):
                sp.wait_ge(hi_ready, (b + 1) * (NX + 1))
                place(b, ((q1, 0, q_hi), (k1, 0, k_hi), (q1, 1, q_hi), (k1, 2, k_hi), (q2, 0, q_hi), (k2, 1, k_hi)))
                sp.wait_ge(mid_ready, (b + 1) * (NX + 1))
                place(b, ((q1, 2, q_mid), (k1, 1, k_mid), (q1, 3, q_mid)))
                sp.wait_ge(lo_ready, (b + 1) * (NX + 1))
                place(b, ((k1, 3, k_mid), (k2, 0, k_lo), (q2, 1, q_lo)))

            out_v = out.rearrange("b (t p) d -> b p t d", p=P)

            def store(b):
                sp.wait_ge(x4_ready, b + 1)
                sp.dma_start(out_v[b], x_all[:, bass.ds(b * T, T), :]).then_inc(stored, 16)

            stack(0)
            stack(1)
            with sp.Fori(1, B - 1) as b:
                stack(b + 1)
                store(b - 1)
            store(B - 2)
            store(B - 1)
            sp.wait_ge(stored, B * 16)

        @block.gpsimd
        def _(pool):
            nc.gpsimd.memset(whole[:, 0:NAT + NX, :], 0.0).then_inc(zeroed, 1)
            chain = Chain(pool, chain_p)
            nc.gpsimd.memset(mask_qk[:], 0.0)
            nc.gpsimd.memset(neg_part[:], 0.0)
            chain.link(nc.gpsimd.memset(mask_kq[:], 0.0))
            nc.gpsimd.affine_select(out=mask_qk[:], in_=mask_qk[:], compare_op=ALU.is_ge, fill=-1e30, base=0,
                                    pattern=[[-1, P]], channel_multiplier=1)
            for e in range(NX):
                m = nc.gpsimd.affine_select(out=mask_kq[:, e, :], in_=mask_kq[:, e, :], compare_op=ALU.is_ge, fill=-1e30,
                                            base=0, pattern=[[1, P]], channel_multiplier=-1)
            m.then_inc(masks_ready, 1)

            def handle(job, b, use):
                if job[0] == "norm_x":
                    pool.wait_ge(var_ready, b + NH + 1)
                    nc.gpsimd.tensor_tensor(rstd[:], mv[:, :, 1], neg_half[:, 0:T], ALU.pow).then_inc(rstd_ready, 1)
                if job[0] == "mid":
                    e = job[1]
                    pool.wait_ge(mid_ready, b * (NX + 1) + e + 1)
                    lo, rest, mid = (x[:, e, :] for x in (q_lo, q_rest, q_mid)) if e < NX else (k_lo[:], k_rest[:], k_mid[:])
                    nc.gpsimd.tensor_tensor(lo, rest, mid, ALU.subtract).then_inc(lo_ready, 1)
                if job[0] in ("norm_mix", "norm_out"):
                    pool.wait_ge(sum_ready, b * 2 + (2 if job[0] == "norm_out" else 1))
                    nc.gpsimd.tensor_tensor(r16[:], s16[:], neg_half[:, 0:T * NH], ALU.pow).then_inc(pow_ready, 1)

            run_turns(pool, handle)

        @block.scalar
        def _(act):
            def copied(bank, nth, dst, src, signal, func=ACT.Copy, **kw):
                act.wait_ge(side_full[bank], nth)
                nc.scalar.activation(dst, src, func, **kw).then_inc(signal, 1)

            def handle(job, b, use):
                name, arg = job[0], job[1:]
                if use:
                    bank, nth = use
                    ps = side[bank]
                if name == "begin":
                    act.wait_ge(v_ready, b + 1)
                    if later(b):
                        act.wait_ge(values_pe, b * NG)
                    nc.scalar.activation(v_now[:], v_next[:], ACT.Copy).then_inc(v_now_ready, 1)
                elif name == "score":
                    g, n = arg
                    act.wait_ge(score_pe[n], b * NG + g + 1)
                    if later(b) or g > 1:
                        act.wait_ge(values_pe, b * NG + g - 1)
                    nc.scalar.activation(prob[:, g % 2, n, :], psum.banks[n], ACT.Exp, scale=SCALE)\
                      .then_inc(prob_ready[n], 1)
                elif name == "xT":
                    h = arg[0]
                    copied(bank, nth, xnT[:, h * 256:(h + 1) * 256], ps[:, 0:256], xnT_ready)
                elif name == "sx":
                    copied(bank, nth, sxT[:], ps, sxT_ready, ACT.Identity, bias=hl_b[:, 0:1])
                elif name in ("q", "k"):
                    e = arg[0] if arg else NX
                    act.wait_ge(side_full[bank], nth)
                    if e == 0 and later(b):
                        act.wait_ge(stack_in, b * STACK_DMAS * 16)
                    nc.scalar.activation(q_hi[:, e, :] if arg else k_hi[:], ps, ACT.Copy).then_inc(hi_ready, 1)
                elif name == "v":
                    copied(bank, nth, v_next[:], ps, v_ready)
                elif name == "mid":
                    e = arg[0]
                    act.wait_ge(rest_ready, b * (NX + 1) + e + 1)
                    mid, rest = (q_mid[:, e, :], q_rest[:, e, :]) if e < NX else (k_mid[:], k_rest[:])
                    nc.scalar.activation(mid, rest, ACT.Copy).then_inc(mid_ready, 1)
                elif name == "collect":
                    sc = arg[0]
                    act.wait_ge(values_pe, b * NG + GROUPS.index((sc, sc)) + 1)
                    if later(b) or sc > 0:
                        act.wait_ge(tok_ready, b * T + sc)
                    nc.scalar.activation(den[:], psum.banks[5].rearrange("p (e s) -> p e s", e=NX), ACT.Copy)\
                      .then_inc(den_ready, 1)
                elif name == "negmax":
                    n, sc = arg
                    copied(bank, nth, q2[96:128, slot(b), n, :, sc * P:(sc + 1) * P],
                           ps[96:128, :].rearrange("p (e s) -> p e s", e=NX), negmax_ready)
                elif name == "tok":
                    if arg[0] == 0 and later(b):
                        act.wait_ge(sum_ready, b * 2 - 1)
                    copied(bank, nth, tok[:, arg[0]], ps.rearrange("p (e c) -> p e c", e=NX), tok_copied)
                elif name == "mix_logits":
                    act.wait_ge(gl_ready, b + 1)
                    nc.scalar.activation(gl[:], gl[:], ACT.Exp).then_inc(gexp_ready, 1)
                elif name == "fxT":
                    copied(bank, nth, fxT[:], ps, fxT_ready)
                elif name == "fc1":
                    copied(bank, nth, h1, ps, h1_ready, ACT.Relu, bias=fc1_b[:, 0:1])
                elif name == "foT":
                    copied(bank, nth, foT[:], ps, foT_ready)
                elif name == "leave":
                    act.wait_ge(fl_ready, b + 1)
                    nc.scalar.activation(fl[:], fl[:], ACT.Exp).then_inc(fexp_ready, 1)

            act.wait_ge(w_in, LOADS * 16)
            run_turns(act, handle)

        @block.tensor
        def _(pe):
            pe.wait_ge(w_in, LOADS * 16)
            pe.wait_ge(masks_ready, 1)
            for k in range(NAT):
                nc.tensor.transpose(psum.banks[k // 4][:, (k % 4) * P:(k % 4 + 1) * P], nat[:, k, :], ident[:])
            for e in range(NX):
                nc.tensor.transpose(psum.banks[3][:, e * 16:(e + 1) * 16], nat_gate[:, e, :], ident[0:16, 0:16])
            nc.tensor.transpose(psum.banks[3][:, 64:64 + NH], nat_fgate, ident[0:NH, 0:NH]).then_inc(w_pe, 1)
            pe.wait_ge(w_ready, 1)
            held = [None, None]
            pick = ident[:].rearrange("p (n d) -> p n d", d=HD)[:, :, 0]

            def begins(b):
                left = [job for job in MID if job[0] in SIDE_JOBS][-2:]
                assert all(job in PRE_JOBS for job in left)
                held[:] = [(job, b) for job in left]

            def handle(job, b, use):
                name, arg = job[0], job[1:]
                if use:
                    bank, nth = use
                    ps = side[bank]
                    if held[bank]:
                        pe.wait_ge(*read(*held[bank]))
                    held[bank] = (job, b)
                if name == "score":
                    g, n = arg
                    sc, tc = GROUPS[g]
                    if tc == 0:
                        pe.wait_ge(negmax_ready, b * NEG + sc * NH + n + 1)
                    if later(b) or g > 0:
                        pe.wait_ge(prob_ready[n], b * NG + g)
                    s, k = slice(sc * P, (sc + 1) * P), slice(tc * P, (tc + 1) * P)
                    dst = psum.banks[n]
                    nc.tensor.matmul(dst, k1[:, slot(b), n, k], q1[:, slot(b), n, :, s], start=True, stop=False)
                    m = nc.tensor.matmul(dst, k2[:, slot(b), n, k], q2[:, slot(b), n, :, s], start=False, stop=(sc != tc))
                    if sc == tc:
                        m = nc.tensor.matmul(dst, ident_bf[:], mask_kq[:], start=False, stop=True)
                    m.then_inc(score_pe[n], 1)
                elif name == "values":
                    g = arg[0]
                    sc, tc = GROUPS[g]
                    if g == 0:
                        pe.wait_ge(v_now_ready, b + 1)
                    if tc == 0 and (later(b) or sc > 0):
                        pe.wait_ge(att_ready, b * T + sc)
                        pe.wait_ge(den_ready, b * T + sc)
                    for n in range(NH):
                        pe.wait_ge(prob_ready[n], b * NG + g + 1)
                        d = slice(n * HD, (n + 1) * HD)
                        nc.tensor.matmul(psum.banks[4][d, :], v_now[:, tc, d], prob[:, g % 2, n, :],
                                         start=(tc == 0), stop=(tc == sc))
                    for n in range(NH):
                        d = slice(n * HD, (n + 1) * HD)
                        m = nc.tensor.matmul(psum.banks[5][d, :], ones[:, 0:HD], prob[:, g % 2, n, :],
                                             start=(tc == 0), stop=(tc == sc))
                    m.then_inc(values_pe, 1)
                elif name == "xT":
                    h = arg[0]
                    pe.wait_ge(xn_ready, b + NH + 1)
                    for i in range(2):
                        m = nc.tensor.transpose(ps[:, i * P:(i + 1) * P], xn[:, 2 * h + i, :], ident[:])
                    m.then_inc(side_full[bank], 1)
                elif name == "resid":
                    r = b + NH
                    pe.wait_ge(xnT_ready, (r + 1) * 2)
                    for it in range(T):
                        m = nc.tensor.matmul(ps[:, it * HD:(it + 1) * HD], xnT[:, it * P:(it + 1) * P],
                                             hl_t[:, r * HD:(r + 1) * HD], start=True, stop=True)
                    m.then_inc(side_full[bank], 1)
                elif name == "sx":
                    pe.wait_ge(xnT_ready, (b + NH + 1) * 2)
                    nc.tensor.matmul(ps, hl_t, xnT[:], start=True, stop=True).then_inc(side_full[bank], 1)
                elif name in ("q", "k"):
                    pe.wait_ge(sxT_ready, b + 1)
                    nc.tensor.matmul(ps, wq_t[:, arg[0], :] if arg else wk_t, sxT[:], start=True, stop=True)\
                      .then_inc(side_full[bank], 1)
                elif name == "v":
                    for it in range(T):
                        m = nc.tensor.matmul(ps[:, it * P:(it + 1) * P], sxT[:, it * P:(it + 1) * P], wv_t,
                                             start=True, stop=True)
                    m.then_inc(side_full[bank], 1)
                elif name == "max":
                    n, part = arg
                    sc, experts = MAX_PARTS[part]
                    if n == 0 and part == 0:
                        pe.wait_ge(stack_in, (b + 1) * STACK_DMAS * 16)
                    width = (sc + 1) * P
                    for i, e in enumerate(experts):
                        nc.tensor.matmul(ps[:, i * width:(i + 1) * width], q1[:, slot(b), n, e, sc * P:(sc + 1) * P],
                                         k1[:, slot(b), n, 0:width], start=True, stop=False)
                        m = nc.tensor.matmul(ps[:, (i + 1) * width - P:(i + 1) * width], ident_bf[:], mask_qk[:],
                                             start=False, stop=True)
                    m.then_inc(side_full[bank], 1)
                elif name == "negmax":
                    n, sc = arg
                    pe.wait_ge(top_split, b * 2 + sc // 2 + 1)
                    for e in range(NX):
                        m = nc.tensor.matmul(ps[96:128, e * P:(e + 1) * P], neg_part[:, (sc * NH + n) * NX + e, :],
                                             ident_bf[:], start=True, stop=True)
                    m.then_inc(side_full[bank], 1)
                elif name == "tok":
                    sc = arg[0]
                    pe.wait_ge(att_ready, b * T + sc + 1)
                    for e in range(NX):
                        m = nc.tensor.transpose(ps[:, e * P:(e + 1) * P], att[:, sc % 2, e, :], ident[:])
                    m.then_inc(side_full[bank], 1)
                elif name == "gate":
                    sc = arg[0]
                    for e in range(NX):
                        nc.tensor.matmul(ps[:, e * NH * NX:(e + 1) * NH * NX], att[:, sc % 2, e, :], gate_w[:, e, :],
                                         start=True, stop=True)
                    pe.wait_ge(den_ready, b * T + sc + 1)
                    at = NX * NH * NX
                    for e in range(NX):
                        m = nc.tensor.matmul(ps[:, at + e * NH:at + (e + 1) * NH], den[:, e, :], pick,
                                             start=True, stop=True)
                    m.then_inc(side_full[bank], 1)
                elif name == "fxT":
                    pe.wait_ge(hn_ready, b + 1)
                    for it in range(T):
                        m = nc.tensor.transpose(ps[:, it * P:(it + 1) * P], hn[:, it, :], ident[:])
                    m.then_inc(side_full[bank], 1)
                elif name == "fc1":
                    pe.wait_ge(fxT_ready, b + 1)
                    nc.tensor.matmul(ps, fc1_t, fxT[:], start=True, stop=True).then_inc(side_full[bank], 1)
                elif name == "fc2":
                    pe.wait_ge(h1m_ready, b + 1)
                    for it in range(T):
                        m = nc.tensor.matmul(ps[:, it * P:(it + 1) * P], h1[:, it * P:(it + 1) * P], fc2_t,
                                             start=True, stop=True)
                    m.then_inc(side_full[bank], 1)
                elif name == "foT":
                    pe.wait_ge(fo_ready, b + 1)
                    for it in range(T):
                        m = nc.tensor.transpose(ps[:, it * P:(it + 1) * P], fo[:, it, :], ident[:])
                    m.then_inc(side_full[bank], 1)
                elif name == "fgate":
                    pe.wait_ge(foT_ready, b + 1)
                    for it in range(T):
                        m = nc.tensor.matmul(ps[:, it * NH:(it + 1) * NH], foT[:, it * P:(it + 1) * P], fgate_w[:],
                                             start=True, stop=True)
                    m.then_inc(side_full[bank], 1)

            run_turns(pe, handle, begins=begins)

        @block.vector
        def _(dve):
            chain = Chain(dve, chain_v)
            nc.vector.memset(q2[64:128].rearrange("p a n e s -> p (a n e s)").bitcast(F32), 0.0)
            chain.link(nc.vector.memset(k2[64:128].rearrange("p a n s -> p (a n s)").bitcast(F32), 0.0))
            nc.vector.memset(k2[96:99], 1.0)
            dve.wait_ge(w_in, LOADS * 16)
            dve.wait_ge(w_pe, 1)
            for k in range(NAT):
                nc.vector.tensor_copy(turned[:, k, :], psum.banks[k // 4][:, (k % 4) * P:(k % 4 + 1) * P])
            nc.vector.tensor_copy(gate_w[:], psum.banks[3][:, 0:64].rearrange("p (e g) -> p e g", e=NX))
            nc.vector.tensor_copy(fgate_w[:], psum.banks[3][:, 64:64 + NH]).then_inc(w_ready, 1)

            def heads(x):
                return x.rearrange("p t (n d) -> p (t n) d", d=HD)

            def each(x):
                return x.unsqueeze(2).broadcast_to([P, T * NH, HD])

            def row(x):
                return x[:].unsqueeze(1).broadcast_to([P, T * NH, HD])

            def norm_heads():
                chain.link(nc.vector.tensor_reduce(s16[:], heads(y[:]), AX, ALU.add))
                chain.link(nc.vector.tensor_scalar(s16[:], s16[:], -1.0 / HD, None, ALU.mult))
                chain.link(nc.vector.tensor_tensor(heads(yc[:]), heads(y[:]), each(s16[:]), ALU.add))
                chain.link(nc.vector.tensor_tensor(sq[:], yc[:], yc[:], ALU.mult))
                chain.link(nc.vector.tensor_reduce(s16[:], heads(sq[:]), AX, ALU.add))
                nc.vector.tensor_scalar(s16[:], s16[:], 1.0 / HD, 1e-8, ALU.mult, ALU.add).then_inc(sum_ready, 1)

            def scale_heads(dst, gain, bias, count, ready):
                dve.wait_ge(pow_ready, count)
                chain.link(nc.vector.tensor_tensor(heads(yc[:]), heads(yc[:]), each(r16[:]), ALU.mult))
                chain.link(nc.vector.tensor_tensor(heads(yc[:]), heads(yc[:]), row(gain), ALU.mult))
                nc.vector.tensor_tensor(heads(dst[:]), heads(yc[:]), row(bias), ALU.add).then_inc(ready, 1)

            def handle(job, b, use):
                name, arg = job[0], job[1:]
                if use:
                    bank, nth = use
                    ps = side[bank]
                if name == "norm_x":
                    m_th = b + NH
                    g = b + NH if isinstance(b, int) and b < 0 else b
                    for it in range(T):
                        m = nc.vector.bn_stats(stats[:, it, :], x_all[:, g * T + it, :])
                    chain.link(m)
                    nc.vector.memset(spot[:], 0.0)
                    for it in range(T):
                        m = nc.vector.bn_aggr(mv[:, it, :], stats[:, it, :])
                    chain.link(m)
                    nc.vector.tensor_scalar(mv[:, :, 1], mv[:, :, 1], 1e-5, None, ALU.add).then_inc(var_ready, 1)
                elif name == "scale_x":
                    m_th = b + NH
                    g = b + NH if isinstance(b, int) and b < 0 else b
                    dve.wait_ge(rstd_ready, m_th + 1)
                    if later(m_th):
                        dve.wait_ge(xnT_ready, m_th * 2)
                    for it in range(T):
                        m = nc.vector.tensor_scalar(xn[:, it, :], x_all[:, g * T + it, :], mv[:, it, 0:1],
                                                    rstd[:, it:it + 1], ALU.subtract, ALU.mult)
                    m.then_inc(xn_ready, 1)
                elif name == "resid":
                    r = b + NH
                    d = slice(r * HD, (r + 1) * HD)
                    dve.wait_ge(side_full[bank], nth)
                    nc.vector.tensor_tensor(resid[:, :, d], ps[:, 0:T * HD].rearrange("p (t d) -> p t d", t=T),
                                            hl_b_row[:, d].unsqueeze(1).broadcast_to([P, T, HD]), ALU.add)\
                      .then_inc(resid_ready, 1)
                elif name == "sx":
                    dve.wait_ge(sxT_ready, b + 1)
                    nc.vector.tensor_scalar(not_pad[:, slot(b), :], sxT[:], 0.0, None, ALU.not_equal)
                elif name in ("q", "k"):
                    e = arg[0] if arg else NX
                    dve.wait_ge(hi_ready, b * (NX + 1) + e + 1)
                    if e == 0 and later(b):
                        dve.wait_ge(lo_ready, b * (NX + 1))
                    hi, rest = (q_hi[:, e, :], q_rest[:, e, :]) if arg else (k_hi[:], k_rest[:])
                    nc.vector.tensor_tensor(rest, ps, hi, ALU.subtract).then_inc(rest_ready, 1)
                elif name == "max":
                    n, part = arg
                    sc, experts = MAX_PARTS[part]
                    width = (sc + 1) * P * len(experts)
                    dve.wait_ge(side_full[bank], nth)
                    nc.vector.tensor_reduce(top[:, sc, n, experts[0]:experts[-1] + 1],
                                            ps[:, 0:width].rearrange("p (e k) -> p e k", e=len(experts)), AX, ALU.max)\
                      .then_inc(top_ready, 1)
                elif name == "max_split":
                    half = arg[0]
                    done = FIRST_MAXIMA if half == 0 else len(MAX_JOBS)
                    dve.wait_ge(top_ready, b * len(MAX_JOBS) + done)
                    if later(b):
                        dve.wait_ge(negmax_ready, b * NEG)
                    i = slice(half * NEG // 2 * NX, (half + 1) * NEG // 2 * NX)
                    neg = neg_top[:, i]
                    chain.link(nc.vector.tensor_scalar(neg, top[:].rearrange("p s n e -> p (s n e)")[:, i], -1.0, None,
                                                       ALU.mult))
                    chain.link(nc.vector.tensor_copy(neg_part[:, i, 0], neg))
                    chain.link(nc.vector.tensor_tensor(neg, neg, neg_part[:, i, 0], ALU.subtract))
                    chain.link(nc.vector.tensor_copy(neg_part[:, i, 1], neg))
                    nc.vector.tensor_tensor(neg_part[:, i, 2], neg, neg_part[:, i, 1], ALU.subtract)\
                      .then_inc(top_split, 1)
                elif name == "collect":
                    sc = arg[0]
                    g = GROUPS.index((sc, sc))
                    dve.wait_ge(values_pe, b * NG + g + 1)
                    nc.vector.tensor_tensor(att[:, sc % 2], psum.banks[4].rearrange("p (e s) -> p e s", e=NX),
                                            not_pad[:, slot(b), sc * P:(sc + 1) * P].unsqueeze(1)
                                            .broadcast_to([P, NX, P]), ALU.mult).then_inc(att_ready, 1)
                elif name == "gate":
                    sc = arg[0]
                    dve.wait_ge(side_full[bank], nth)
                    at = NX * NH * NX
                    chain.link(nc.vector.reciprocal(rden[:, sc], ps[:, at:at + NX * NH].rearrange("p (e n) -> p e n", e=NX)))
                    chain.link(nc.vector.tensor_tensor(gprod[:], ps[:, 0:at].rearrange("p (e n g) -> p e n g", e=NX, n=NH),
                                                       rden[:, sc].unsqueeze(3).broadcast_to([P, NX, NH, NX]), ALU.mult))
                    nc.vector.tensor_reduce(glog[:, sc], gprod[:].rearrange("p e n g -> p n g e"), AX, ALU.add)\
                      .then_inc(tok_ready, 1)
                elif name == "mix_logits":
                    dve.wait_ge(tok_ready, (b + 1) * T)
                    chain.link(nc.vector.tensor_tensor(gl[:], glog[:],
                                                       gate_b[:].rearrange("p (n e) -> p n e", n=NH).unsqueeze(1)
                                                       .broadcast_to([P, T, NH, NX]), ALU.add))
                    chain.link(nc.vector.tensor_reduce(gtop[:], gl[:], AX, ALU.max))
                    nc.vector.tensor_tensor(gl[:], gl[:], gtop[:].unsqueeze(3).broadcast_to([P, T, NH, NX]),
                                            ALU.subtract).then_inc(gl_ready, 1)
                elif name == "mix":
                    dve.wait_ge(gexp_ready, b + 1)
                    chain.link(nc.vector.tensor_reduce(gtop[:], gl[:], AX, ALU.add))
                    chain.link(nc.vector.reciprocal(gtop[:], gtop[:]))
                    chain.link(nc.vector.tensor_tensor(gl[:], gl[:], gtop[:].unsqueeze(3).broadcast_to([P, T, NH, NX]),
                                                       ALU.mult))
                    chain.link(nc.vector.tensor_tensor(gl[:], gl[:], rden[:].rearrange("p t e n -> p t n e"), ALU.mult))
                    dve.wait_ge(tok_copied, (b + 1) * T)
                    for sc in range(T):
                        chain.link(nc.vector.tensor_tensor(
                            mixw[:].rearrange("p e (n d) -> p e n d", n=NH),
                            tok[:, sc].rearrange("p e (n d) -> p e n d", n=NH),
                            gl[:, sc].rearrange("p n e -> p e n").unsqueeze(3).broadcast_to([P, NX, NH, HD]), ALU.mult))
                        chain.link(nc.vector.tensor_reduce(y[:, sc, :], mixw[:].rearrange("p e c -> p c e"), AX, ALU.add))
                    chain.link(nc.vector.tensor_tensor(y[:], y[:], resid[:], ALU.add))
                elif name in ("norm_mix", "norm_out"):
                    norm_heads()
                elif name == "scale_mix":
                    scale_heads(hn, ln_g, ln_b, b * 2 + 1, hn_ready)
                elif name == "fc1":
                    dve.wait_ge(h1_ready, b + 1)
                    nc.vector.scalar_tensor_tensor(out=h1, in0=fxT[:], scalar=0.0, in1=h1, op0=ALU.not_equal,
                                                   op1=ALU.mult).then_inc(h1m_ready, 1)
                elif name == "fc2":
                    dve.wait_ge(side_full[bank], nth)
                    nc.vector.tensor_tensor(heads(y[:]), ps.rearrange("p (a d) -> p a d", d=HD), row(fc2_b), ALU.add)\
                      .then_inc(y_biased, 1)
                    dve.wait_ge(y_biased, b + 1)
                    chain.link(nc.vector.scalar_tensor_tensor(out=y[:], in0=hn[:], scalar=0.0, in1=y[:],
                                                              op0=ALU.not_equal, op1=ALU.mult))
                    chain.link(nc.vector.tensor_tensor(y[:], y[:], hn[:], ALU.add))
                elif name == "scale_out":
                    scale_heads(fo, fn_g, fn_b, b * 2 + 2, fo_ready)
                elif name == "fgate":
                    dve.wait_ge(side_full[bank], nth)
                    logits = ps[:, 0:T * NH].rearrange("p (t n) -> p t n", t=T)
                    chain.link(nc.vector.tensor_reduce(fmax[:], logits, AX, ALU.max))
                    nc.vector.tensor_tensor(fl[:], logits, fmax[:].unsqueeze(2).broadcast_to([P, T, NH]),
                                            ALU.subtract).then_inc(fl_ready, 1)
                elif name == "leave":
                    dve.wait_ge(fexp_ready, b + 1)
                    chain.link(nc.vector.tensor_reduce(fmax[:], fl[:], AX, ALU.add))
                    chain.link(nc.vector.reciprocal(fmax[:], fmax[:]))
                    chain.link(nc.vector.tensor_tensor(fl[:], fl[:], fmax[:].unsqueeze(2).broadcast_to([P, T, NH]), ALU.mult))
                    chain.link(nc.vector.tensor_tensor(heads(yc[:]), heads(fo[:]), each(fl[:].rearrange("p t n -> p (t n)")),
                                                       ALU.mult))
                    xb = x_all[:, bass.ds(b * T, T), :]
                    nc.vector.tensor_tensor(xb, xb, yc[:], ALU.add).then_inc(x4_ready, 1)

            run_turns(dve, handle, chain, VEC_LINKS)


_INS = ["x", "adj",
        "L0_gnn_fc_w", "L0_gnn_fc_b", "L0_gnn_q_w", "L0_gnn_q_b", "L0_gnn_k_w", "L0_gnn_k_b", "L0_gnn_fp_w",
        "L0_gnn_fp_b", "L0_ffn_gate_w", "L0_ffn_gate_b", "L0_ffn_w1", "L0_ffn_b1", "L0_ffn_w2", "L0_ffn_b2",
        "L1_gnn_W", "L1_gnn_b", "L1_ffn_hl_w", "L1_ffn_hl_b", "L1_ffn_wq", "L1_ffn_wk", "L1_ffn_wv",
        "L1_ffn_gate_w", "L1_ffn_gate_b", "L1_ffn_ln_g", "L1_ffn_ln_b", "L1_ffn_fc1_w", "L1_ffn_fc1_b",
        "L1_ffn_fc2_w", "L1_ffn_fc2_b", "L1_ffn_fnorm_g", "L1_ffn_fnorm_b", "L1_ffn_fgate_w"]


def kernel(**inputs):
    import numpy as _np
    import concourse.bacc as _bacc
    from concourse import mybir as _mybir
    from concourse.bass_utils import run_bass_kernel_spmd as _run

    nc = _bacc.Bacc("TRN2", target_bir_lowering=False, num_devices=1)
    arrays, args = {}, {}
    for name in _INS:
        a = _np.ascontiguousarray(inputs[name])
        arrays[f"in_{name}_dram"] = a
        args[name] = nc.dram_tensor(f"in_{name}_dram", a.shape, _mybir.dt.from_np(a.dtype), kind="ExternalInput").ap()
    out = nc.dram_tensor("out_0_dram", (16, 512, 128), _mybir.dt.float32, kind="ExternalOutput").ap()
    build(nc, args, out)
    r = _run(nc, [arrays], core_ids=[0])
    return r.results[0]["out_0_dram"]
```

```python
from contextlib import ExitStack

import concourse.bass as bass
from concourse import mybir

F32 = mybir.dt.float32
BF16 = mybir.dt.bfloat16
U32 = mybir.dt.uint32
ACT = mybir.ActivationFunctionType
ALU = mybir.AluOpType
AX = mybir.AxisListType.X

P = 128
B, N, D = 16, 512, 128
T = N // P
H = 8
E, F = 8, 512
CAP = B * N * 5 // 4 // E
SLOPE = 0.01


class Chain:

    def __init__(self, eng, sem):
        self.eng, self.sem, self.base, self.k = eng, sem, 0, 0

    def turn(self, start, turn, steps):
        self.base, self.k = turn * steps + start, 0

    def link(self, ins):
        self.k += 1
        ins.then_inc(self.sem, 1)
        self.eng.wait_ge(self.sem, self.base + self.k)


def later(turn):
    return not isinstance(turn, int) or turn > 0


class Banks:

    def __init__(self, whole):
        self.whole = whole
        self.banks = [whole[:, i, :] for i in range(8)]
        self.logit, self.place, self.count = self.banks[2:5]


def build(nc, t, out):
    ctx = ExitStack()
    with ctx:
        def sb(name, shape, dt=F32):
            return ctx.enter_context(nc.sbuf_tensor(name, shape, dt))

        def sem(name):
            return ctx.enter_context(nc.semaphore(name))

        x_all = sb("x_all", [P, B * T, D])
        deg = sb("deg", [P, B * T])
        ident = sb("ident", [P, P])
        ident_bf = sb("ident_bf", [P, P], BF16)
        dinv = sb("dinv", [P, B * T])
        ones = sb("ones", [P, P])
        ones_bf = sb("ones_bf", [P, 1], BF16)
        neg_half = sb("neg_half", [P, 16])
        slot_of = sb("slot_of", [P, B * T], U32)
        share = sb("share", [P, B * T])
        expert_in = nc.dram_tensor("expert_in", [E * CAP + B * N, D], F32, kind="Internal").ap()
        expert_out = nc.dram_tensor("expert_out", [E * CAP, D], F32, kind="Internal").ap()

        psum = Banks(ctx.enter_context(nc.psum_tensor("banks", [P, 8, 512], F32)))

        const_ready = sem("const_ready")

        with ExitStack() as graphs:
            adjT = graphs.enter_context(nc.sbuf_tensor("adjT", [P, B, T, N], BF16))
            with ExitStack() as stage:
                gat_layer(nc, t, stage, x_all, adjT, deg, ident, ident_bf, ones, ones_bf, neg_half, psum.banks,
                          const_ready)
            with ExitStack() as stage:
                route_tokens(nc, t, stage, x_all, expert_in, slot_of, share, ident, ident_bf, ones, neg_half, psum)
            with ExitStack() as stage:
                run_experts(nc, t, stage, expert_in, expert_out, deg, dinv, ident, neg_half, psum)
            with ExitStack() as stage:
                gcn_layer(nc, t, stage, x_all, adjT, dinv, expert_out, slot_of, share, ident, ident_bf, neg_half, psum)
        with ExitStack() as stage:
            attention_layer(nc, t, stage, x_all, out, ident, ident_bf, ones, neg_half, psum)


def gat_layer(nc, t, stage, x_all, adjT, deg, ident, ident_bf, ones, ones_bf, neg_half, psum, const_ready):
    def sb(name, shape, dt=F32):
        return stage.enter_context(nc.sbuf_tensor(name, shape, dt))

    def sem(name):
        return stage.enter_context(nc.semaphore(name))

    fc_b = sb("fc_b", [P, H])
    qk_w = sb("qk_w", [P, 2])
    qk_b = sb("qk_b", [P, 2])
    fp_b = sb("fp_b", [P, D])
    value_w = sb("value_w", [P, H, D])
    mean_w = sb("mean_w", [P, D])
    head_qk = sb("head_qk", [P, H, 2])
    q_rep = sb("q_rep", [P, H, P])
    qk_sum = sb("qk_sum", [P, 2])
    logit_b = sb("logit_b", [P, H])
    out_b = sb("out_b", [P, D])

    adj_in = sb("adj_in", [P, T, N])
    adj_bf = sb("adj_bf", [P, T, N], BF16)
    xn = sb("xn", [P, T, D])
    xnT = sb("xnT", [P, N])
    stats = sb("stats", [P, T, 6])
    mv = sb("mv", [P, T, 2])
    rstd = sb("rstd", [P, T])
    wait_spot = sb("wait_spot", [P, 1])
    kmax = sb("kmax", [H, 1])
    kmax_diag = sb("kmax_diag", [H, H])
    kmax_all = sb("kmax_all", [P, H])
    relu_b = sb("relu_b", [P, H])
    kd = sb("kd", [P, T, H])
    k_steep = sb("k_steep", [P, 2, T, H])
    k_flat = sb("k_flat", [P, T, H])
    xsum = sb("xsum", [P, 1])
    xsum_rep = sb("xsum_rep", [P, P])
    lone = sb("lone", [P, 2, T])
    acc = sb("acc", [P, 2, T, D])
    value = sb("value", [P, 2, T, H, D + 1])
    q_relu = sb("q_relu", [P, 2, N])
    q_row = sb("q_row", [P, H, N])
    weight = sb("weight", [P, 2, T, N])
    fc_w = weight[:, 0, 0:2, :].rearrange("p a (h d) -> p (a h) d", d=D)
    fp_w = weight[:, 0, 2:4, :].rearrange("p a (h d) -> p (a h) d", d=D)
    fc_wT = weight[:, 1, 0:2, :].rearrange("p a (h d) -> p (a h) d", d=D)
    den = sb("den", [P, T])
    rden = sb("rden", [P, T])
    sig = sb("sig", [P, T, D])

    fc_b_rep = q_row[:, :, 0:P]

    w_in = sem("w_in")
    in_ready = sem("in_ready")
    adj_cast = sem("adj_cast")
    pe_w = sem("pe_w")
    w_done = sem("w_done")
    vec_chain = sem("gat_vec_chain")
    pool_chain = sem("gat_pool_chain")
    act_chain = sem("gat_act_chain")
    var_ready = sem("var_ready")
    rstd_ready = sem("rstd_ready")
    xn_ready = sem("xn_ready")
    adjT_pe = sem("adjT_pe")
    adjT_ready = sem("adjT_ready")
    xnT_pe = sem("xnT_pe")
    xnT_ready = sem("xnT_ready")
    k_pe = sem("k_pe")
    kdiag_ready = sem("kdiag_ready")
    kmax_pe = sem("kmax_pe")
    kd_ready = sem("kd_ready")
    kexp_ready = sem("kexp_ready")
    small_used = sem("small_used")
    value_pe = sem("value_pe")
    value_ready = sem("value_ready")
    q_pe = sem("q_pe")
    q_relu_ready = sem("q_relu_ready")
    q_row_ready = sem("q_row_ready")
    weight_ready = sem("weight_ready")
    head_pe = sem("head_pe")
    head_used = sem("head_used")
    sig_ready = sem("sig_ready")
    x1_ready = sem("x1_ready")

    bank_t = psum[0:2]
    bank_s = psum[2]
    bank_k = psum[3]
    bank_q = psum[4:6]
    bank_o = psum[6:8]
    k_tok = bank_s[:, 0:T * H].rearrange("p (t h) -> p t h", t=T)
    deg_ps = bank_s[:, 64:64 + T]
    kmax_ps = bank_s[:, 128:128 + H]
    mean_ps = bank_s[:, 256:256 + D]
    o_ps = [bank_o[i][:, 0:2 * (D + 1)].rearrange("p (t c) -> p t c", t=2) for i in range(2)]

    adj = t["adj"].rearrange("b (t p) j -> b p t j", p=P)
    x_in = t["x"].rearrange("b (t p) d -> b p t d", p=P)

    with nc.Block() as block:
        @block.sync
        def _(sp):
            def load(b):
                sp.dma_start(x_all[:, bass.ds(b * T, T), :], x_in[b]).then_inc(in_ready, 16)
                sp.dma_start(adj_in[:], adj[b]).then_inc(in_ready, 16)

            load(0)
            for dst, src in ((fc_w, t["L0_gnn_fc_w"].rearrange("d (h c) -> d h c", h=H)),
                             (fp_w, t["L0_gnn_fp_w"].rearrange("(h c) o -> c h o", h=H)),
                             (fc_b[:], t["L0_gnn_fc_b"].rearrange("(h c) -> c h", h=H)),
                             (qk_w[:, 0:1], t["L0_gnn_q_w"]),
                             (qk_w[:, 1:2], t["L0_gnn_k_w"]),
                             (qk_b[:, 0:1], t["L0_gnn_q_b"].rearrange("(a n) -> a n", a=1).broadcast_to([P, 1])),
                             (qk_b[:, 1:2], t["L0_gnn_k_b"].rearrange("(a n) -> a n", a=1).broadcast_to([P, 1])),
                             (fp_b[:], t["L0_gnn_fp_b"].rearrange("(a n) -> a n", a=1).broadcast_to([P, D]))):
                with nc.allow_non_contiguous_dma("small weights"):
                    sp.dma_start(dst, src).then_inc(w_in, 16)
            with sp.Fori(1, B) as b:
                sp.wait_ge(in_ready, b * 32)
                sp.wait_ge(adj_cast, b)
                load(b)

        @block.gpsimd
        def _(pool):
            chain = Chain(pool, pool_chain)
            nc.gpsimd.memset(neg_half[:], -0.5)
            nc.gpsimd.memset(ones[:], 1.0).then_inc(const_ready, 1)
            nc.gpsimd.memset(ones_bf[:], 1.0).then_inc(const_ready, 1)
            chain.link(nc.gpsimd.memset(ident[:], 0.0))
            chain.link(nc.gpsimd.affine_select(out=ident[:], in_=ident[:], compare_op=ALU.not_equal, fill=1.0,
                                               base=0, pattern=[[-1, P]], channel_multiplier=1))
            nc.gpsimd.tensor_copy(ident_bf[:], ident[:]).then_inc(const_ready, 1)

            def prepare(b):
                pool.wait_ge(var_ready, b + 1)
                nc.gpsimd.tensor_tensor(rstd[:], mv[:, :, 1], neg_half[:, 0:T], ALU.pow).then_inc(rstd_ready, 1)

            prepare(0)
            with pool.Fori(0, B - 1) as b:
                prepare(b + 1)

        @block.scalar
        def _(act):
            def stage0(b):
                act.wait_ge(in_ready, (b + 1) * 32)
                if later(b):
                    act.wait_ge(adjT_pe, b * 2)
                nc.scalar.activation(adj_bf[:], adj_in[:], ACT.Copy).then_inc(adj_cast, 1)

            def stage1(b):
                for i in range(2):
                    act.wait_ge(adjT_pe, b * 2 + i + 1)
                    src = bank_t[i][:, :].bitcast(BF16).rearrange("p (t n) -> p t n", t=2)
                    nc.scalar.activation(adjT[:, b, 2 * i:2 * i + 2, :], src, ACT.Copy).then_inc(adjT_ready, 1)
                act.wait_ge(xnT_pe, b + 1)
                nc.scalar.activation(xnT[:], bank_t[0][:, :], ACT.Copy).then_inc(xnT_ready, 1)

            def stage3(b):
                act.wait_ge(kd_ready, b + 1)
                nc.scalar.activation(k_flat[:], kd[:], ACT.Exp, scale=SLOPE)
                nc.scalar.activation(k_steep[:, b % 2], kd[:], ACT.Exp, scale=1.0 - SLOPE).then_inc(kexp_ready, 1)

            def q_rows(b, h):
                act.wait_ge(q_pe, b * H + h + 1)
                act.wait_ge(kd_ready, b + 1)
                nc.scalar.activation(q_relu[:, h % 2, :], bank_q[h % 2][:, :], ACT.Relu,
                                     bias=relu_b[:, h:h + 1]).then_inc(q_relu_ready, 1)
                act.wait_ge(q_relu_ready, b * H + h + 1)
                if later(b):
                    act.wait_ge(weight_ready, (b - 1) * H + h + 1)
                nc.scalar.activation(q_row[:, h, :], q_relu[:, h % 2, :], ACT.Exp,
                                     scale=-(1.0 - SLOPE)).then_inc(q_row_ready, 1)

            def finish(b):
                act.wait_ge(head_used, 2 + (b + 1) * H * 2)
                nc.scalar.activation(sig[:], acc[:, b % 2], ACT.Exp, scale=-1.0).then_inc(sig_ready, 1)

            stage0(0)
            stage1(0)
            stage3(0)
            for h in range(H):
                q_rows(0, h)
            with act.Fori(0, B - 1) as b:
                stage0(b + 1)
                stage1(b + 1)
                stage3(b + 1)
                for h in range(H):
                    q_rows(b + 1, h)
                finish(b)
            finish(B - 1)

        @block.tensor
        def _(pe):
            pe.wait_ge(w_in, 8 * 16)
            pe.wait_ge(const_ready, 3)
            for h in range(H):
                m = nc.tensor.transpose(psum[h // 4][:, (h % 4) * D:(h % 4 + 1) * D], fc_w[:, h, :], ident[:])
            m.then_inc(pe_w, 1)
            pe.wait_ge(w_done, 1)
            for h in range(H):
                m = nc.tensor.matmul(psum[2 + h // 4][:, (h % 4) * D:(h % 4 + 1) * D], fc_wT[:, h, :], fp_w[:, h, :],
                                     start=True, stop=True)
            for h in range(H):
                m = nc.tensor.matmul(psum[4][:, 2 * h:2 * h + 2], fc_wT[:, h, :], qk_w[:], start=True, stop=True)
            for h in range(H):
                m = nc.tensor.matmul(psum[4][:, 32 + h:33 + h], fc_b_rep[:, h, :], qk_sum[:, 0:1], start=True, stop=True)
            for h in range(H):
                m = nc.tensor.matmul(psum[5][:, 0:D], fc_b_rep[:, h, :], fp_w[:, h, :], start=(h == 0), stop=(h == H - 1))
            m.then_inc(pe_w, 1)
            pe.wait_ge(w_done, 2)

            def stage1(b):
                pe.wait_ge(adj_cast, b + 1)
                if later(b):
                    pe.wait_ge(value_ready, b * T * 2)
                for jt in range(T):
                    dst = bank_t[jt // 2][:, :].bitcast(BF16).rearrange("p (t n) -> p t n", t=2)
                    for it in range(T):
                        m = nc.tensor.transpose(dst[:, jt % 2, it * P:(it + 1) * P],
                                                adj_bf[:, it, jt * P:(jt + 1) * P], ident_bf[:])
                    if jt % 2:
                        m.then_inc(adjT_pe, 1)
                pe.wait_ge(xn_ready, b + 1)
                pe.wait_ge(adjT_ready, b * 2 + 1)
                for it in range(T):
                    m = nc.tensor.transpose(bank_t[0][:, it * P:(it + 1) * P], xn[:, it, :], ident[:])
                m.then_inc(xnT_pe, 1)

            def stage2(b):
                pe.wait_ge(xnT_ready, b + 1)
                pe.wait_ge(adjT_ready, b * 2 + 2)
                if later(b):
                    pe.wait_ge(small_used, b)
                m = nc.tensor.matmul(bank_k[0:H, :], head_qk[:, :, 1], xnT[:], start=True, stop=True)
                for jt in range(T):
                    nc.tensor.matmul(k_tok[:, jt, :], xnT[:, jt * P:(jt + 1) * P], head_qk[:, :, 1],
                                     start=True, stop=True)
                for it in range(T):
                    for jt in range(T):
                        m = nc.tensor.matmul(deg_ps[:, it:it + 1], adjT[:, b, jt, it * P:(it + 1) * P],
                                             ones_bf[:], start=(jt == 0), stop=(jt == T - 1))
                m.then_inc(k_pe, 1)

            def stage3(b):
                pe.wait_ge(kdiag_ready, b + 1)
                nc.tensor.matmul(kmax_ps, ones[0:H, :], kmax_diag[:], start=True, stop=True)
                nc.tensor.matmul(mean_ps, xsum_rep[:], mean_w[:], start=True, stop=True).then_inc(kmax_pe, 1)

            def values(b, jt):
                if jt == 0:
                    pe.wait_ge(xnT_ready, b + 1)
                    pe.wait_ge(adjT_ready, b * 2 + 2)
                for i in range(2):
                    if jt > 0:
                        pe.wait_ge(value_ready, (b * T + jt - 1) * 2 + i + 1)
                    nc.tensor.matmul(bank_t[i][:, :], xnT[:, jt * P:(jt + 1) * P], value_w[:, 4 * i:4 * i + 4, :],
                                     start=True, stop=True).then_inc(value_pe, 1)

            def q_rows(b, h):
                if h >= 2:
                    pe.wait_ge(q_relu_ready, b * H + h - 1)
                nc.tensor.matmul(bank_q[h % 2][:, :], q_rep[:, h, :], xnT[:], start=True, stop=True).then_inc(q_pe, 1)

            def attend(b, h):
                pe.wait_ge(weight_ready, b * H + h + 1)
                if h == 0:
                    pe.wait_ge(value_ready, (b + 1) * T * 2)
                for i in range(2):
                    pe.wait_ge(head_used, (b * H + h) * 2 + i + 1)
                    for it in (2 * i, 2 * i + 1):
                        for jt in range(T):
                            m = nc.tensor.matmul(o_ps[i][:, it % 2, :], weight[:, h % 2, jt, it * P:(it + 1) * P],
                                                 value[:, b % 2, jt, h, :], start=(jt == 0), stop=(jt == T - 1))
                    m.then_inc(head_pe, 1)

            stage1(0)
            stage2(0)
            stage3(0)
            for jt in range(T):
                values(0, jt)
            for h in range(H):
                q_rows(0, h)
            with pe.Fori(0, B - 1) as b:
                for h in range(H):
                    if h >= 4:
                        values(b + 1, h - 4)
                    attend(b, h)
                    if h == 0:
                        stage1(b + 1)
                    if h == 1:
                        stage2(b + 1)
                    if h == 2:
                        stage3(b + 1)
                    if h >= 4:
                        q_rows(b + 1, 2 * h - 8)
                        q_rows(b + 1, 2 * h - 7)
            for h in range(H):
                attend(B - 1, h)

        @block.vector
        def _(dve):
            chain = Chain(dve, vec_chain)
            nc.vector.memset(den[:], 0.0).then_inc(head_used, 2)
            dve.wait_ge(w_in, 8 * 16)
            dve.wait_ge(const_ready, 3)
            nc.vector.tensor_tensor(qk_sum[:, 0:1], qk_w[:, 0:1], qk_w[:, 1:2], ALU.add)
            nc.vector.tensor_tensor(qk_sum[:, 1:2], qk_b[:, 0:1], qk_b[:, 1:2], ALU.add)
            nc.vector.tensor_copy(fc_b_rep, fc_b[:].unsqueeze(2).broadcast_to([P, H, P]))
            dve.wait_ge(pe_w, 1)
            nc.vector.tensor_copy(fc_wT[:, 0:4, :], bank_t[0][:, :].rearrange("p (h d) -> p h d", h=4))
            nc.vector.tensor_copy(fc_wT[:, 4:8, :], bank_t[1][:, :].rearrange("p (h d) -> p h d", h=4)).then_inc(w_done, 1)
            dve.wait_ge(pe_w, 2)
            nc.vector.tensor_copy(value_w[:, 0:4, :], psum[2][:, :].rearrange("p (h d) -> p h d", h=4))
            nc.vector.tensor_copy(value_w[:, 4:8, :], psum[3][:, :].rearrange("p (h d) -> p h d", h=4))
            nc.vector.tensor_copy(head_qk[:], psum[4][:, 0:2 * H].rearrange("p (h c) -> p h c", c=2))
            nc.vector.tensor_copy(q_rep[:], psum[4][:, 0:2 * H:2].unsqueeze(2).broadcast_to([P, H, P]))
            nc.vector.tensor_scalar(logit_b[:], psum[4][:, 32:32 + H], qk_sum[:, 1:2], None, ALU.add)
            chain.link(nc.vector.tensor_tensor(out_b[:], psum[5][:, 0:D], fp_b[:], ALU.add))
            chain.link(nc.vector.tensor_reduce(mean_w[:], value_w[:].rearrange("p h o -> p o h"), AX, ALU.add))
            nc.vector.tensor_scalar(mean_w[:], mean_w[:], 1.0 / N, None, ALU.mult).then_inc(w_done, 1)

            def stage0(b):
                dve.wait_ge(in_ready, (b + 1) * 32)
                for it in range(T):
                    m = nc.vector.bn_stats(stats[:, it, :], x_all[:, b * T + it, :])
                chain.link(m)
                nc.vector.memset(wait_spot[:], 0.0)
                for it in range(T):
                    m = nc.vector.bn_aggr(mv[:, it, :], stats[:, it, :])
                chain.link(m)
                nc.vector.tensor_scalar(mv[:, :, 1], mv[:, :, 1], 1e-5, None, ALU.add).then_inc(var_ready, 1)
                dve.wait_ge(rstd_ready, b + 1)
                if later(b):
                    dve.wait_ge(xnT_pe, b)
                for it in range(T):
                    m = nc.vector.tensor_scalar(xn[:, it, :], x_all[:, b * T + it, :], mv[:, it, 0:1],
                                                rstd[:, it:it + 1], ALU.subtract, ALU.mult)
                m.then_inc(xn_ready, 1)

            def stage2(b):
                dve.wait_ge(k_pe, b + 1)
                nc.vector.tensor_copy(deg[:, bass.ds(b * T, T)], deg_ps)
                nc.vector.tensor_scalar(lone[:, b % 2, :], deg_ps, 0.0, None, ALU.is_equal)
                nc.vector.tensor_reduce(kmax[:], bank_k[0:H, :], AX, ALU.max)
                chain.link(nc.vector.tensor_reduce(xsum[:], xnT[:], AX, ALU.add))
                if later(b):
                    dve.wait_ge(kmax_pe, b)
                nc.vector.tensor_scalar(kmax_diag[:], ident[0:H, 0:H], kmax[:, 0:1], None, ALU.mult)
                nc.vector.tensor_scalar(xsum_rep[:], ones[:], xsum[:, 0:1], None, ALU.mult).then_inc(kdiag_ready, 1)

            def stage3(b):
                dve.wait_ge(kmax_pe, b + 1)
                chain.link(nc.vector.tensor_copy(kmax_all[:], kmax_ps))
                if later(b):
                    dve.wait_ge(kexp_ready, b)
                if later(b):
                    dve.wait_ge(q_relu_ready, b * H)
                nc.vector.tensor_tensor(kd[:], k_tok, kmax_all[:].unsqueeze(1).broadcast_to([P, T, H]), ALU.subtract)
                nc.vector.tensor_tensor(relu_b[:], kmax_all[:], logit_b[:], ALU.add).then_inc(kd_ready, 1)
                chain.link(nc.vector.tensor_tensor(acc[:, b % 2], xn[:], out_b[:].unsqueeze(1).broadcast_to([P, T, D]), ALU.add))
                for it in range(T):
                    m = nc.vector.scalar_tensor_tensor(out=acc[:, b % 2, it, :], in0=mean_ps,
                                                       scalar=lone[:, b % 2, it:it + 1], in1=acc[:, b % 2, it, :],
                                                       op0=ALU.mult, op1=ALU.add)
                m.then_inc(small_used, 1)
                dve.wait_ge(kexp_ready, b + 1)
                nc.vector.tensor_copy(value[:, b % 2, :, :, D], k_flat[:])

            def values(b, jt):
                for i in range(2):
                    dve.wait_ge(value_pe, (b * T + jt) * 2 + i + 1)
                    nc.vector.tensor_tensor(value[:, b % 2, jt, 4 * i:4 * i + 4, 0:D],
                                            bank_t[i][:, :].rearrange("p (h d) -> p h d", h=4),
                                            k_flat[:, jt, 4 * i:4 * i + 4].unsqueeze(2).broadcast_to([P, 4, D]),
                                            ALU.mult).then_inc(value_ready, 1)

            def weights(b, h):
                dve.wait_ge(q_row_ready, b * H + h + 1)
                for jt in range(T):
                    m = nc.vector.scalar_tensor_tensor(out=weight[:, h % 2, jt, :], in0=q_row[:, h, :],
                                                       scalar=k_steep[:, b % 2, jt, h:h + 1], in1=adjT[:, b, jt, :],
                                                       op0=ALU.max, op1=ALU.mult)
                m.then_inc(weight_ready, 1)

            def collect(b, h):
                for i in range(2):
                    dve.wait_ge(head_pe, (b * H + h) * 2 + i + 1)
                    its = slice(2 * i, 2 * i + 2)
                    chain.link(nc.vector.tensor_tensor(den[:, its], o_ps[i][:, :, D], lone[:, b % 2, its], ALU.add))
                    chain.link(nc.vector.reciprocal(rden[:, its], den[:, its]))
                    for it in (2 * i, 2 * i + 1):
                        m = nc.vector.scalar_tensor_tensor(out=acc[:, b % 2, it, :], in0=o_ps[i][:, it % 2, 0:D],
                                                           scalar=rden[:, it:it + 1], in1=acc[:, b % 2, it, :],
                                                           op0=ALU.mult, op1=ALU.add)
                    m.then_inc(head_used, 1)
                    dve.wait_ge(head_used, 2 + (b * H + h) * 2 + i + 1)

            def leave(b, it):
                dve.wait_ge(sig_ready, b + 1)
                chain.link(nc.vector.tensor_scalar(sig[:, it, :], sig[:, it, :], 1.0, None, ALU.add))
                chain.link(nc.vector.reciprocal(sig[:, it, :], sig[:, it, :]))
                xb = x_all[:, bass.ds(b * T + it, 1), :]
                nc.vector.tensor_tensor(xb, xb, sig[:, it:it + 1, :], ALU.add).then_inc(x1_ready, 1)

            def turn(b):
                for h in range(1, H + 1):
                    last = isinstance(b, int) and b == B - 1
                    if h < H:
                        weights(b, h)
                    elif not last:
                        weights(b + 1, 0)
                    if h == 1 and not last:
                        stage0(b + 1)
                    collect(b, h - 1)
                    if h == 2 and not last:
                        stage2(b + 1)
                    if h == 3 and not last:
                        stage3(b + 1)
                    if h <= T and later(b):
                        leave(b - 1, h - 1)
                    if 4 <= h < 4 + T and not last:
                        values(b + 1, h - 4)

            start = 2
            chain.turn(start, 0, 0)
            stage0(0)
            stage2(0)
            stage3(0)
            for jt in range(T):
                values(0, jt)
            weights(0, 0)
            turn(0)
            start += chain.k
            turns_links = 2 + 1 + 2 + H * 4 + 2 * T
            with dve.Fori(1, B - 1) as b:
                chain.turn(start, b - 1, turns_links)
                turn(b)
                assert chain.k == turns_links, chain.k
            chain.turn(start, B - 2, turns_links)
            turn(B - 1)
            for it in range(T):
                leave(B - 1, it)


def route_tokens(nc, t, stage, x_all, expert_in, slot_of, share, ident, ident_bf, ones, neg_half, psum):
    def sb(name, shape, dt=F32):
        return stage.enter_context(nc.sbuf_tensor(name, shape, dt))

    def sem(name):
        return stage.enter_context(nc.semaphore(name))

    NT = B * T
    gate_w = sb("gate_w", [P, E])
    gate_b = sb("gate_b", [P, E])
    stats = sb("r_stats", [P, T, 6])
    mv_slot = sb("r_mv_slot", [P, T, 2])
    mv = sb("r_mv", [P, NT, 2])
    rstd = sb("r_rstd", [P, NT])
    wait_spot = sb("r_wait_spot", [P, 1])
    xn = sb("r_xn", [P, NT, D])
    xn_slot = sb("r_xn_slot", [P, 2, T, D])
    xnT = sb("r_xnT", [P, 2, N])
    upper = sb("upper", [P, P], BF16)
    all_ones = sb("all_ones", [P, P], BF16)
    logit = sb("logit", [P, NT, E])
    prob = sb("prob", [P, NT, E])
    top = sb("top", [P, NT])
    total = sb("total", [P, NT])
    rank = sb("rank", [P, NT, E])
    first = sb("first", [P, NT, E])
    hot = sb("hot", [P, NT, E])
    hot_bf = sb("hot_bf", [P, NT, E], BF16)
    before = sb("before", [P, E, NT + 1])
    place = sb("place", [P, NT])
    queue = sb("queue", [P, NT])
    kept = sb("kept", [P, NT])
    spare_i = sb("spare_i", [P, NT], mybir.dt.int32)
    spare = sb("spare", [P, NT])
    dest = sb("dest", [P, NT])
    dest_u = sb("dest_u", [P, NT], U32)
    zero = sb("zero", [P, CAP])
    offset = sb("offset", [P, NT, E])

    w_in = sem("r_w_in")
    zero_ready = sem("zero_ready")
    zeroed = sem("zeroed")
    stats_ready = sem("r_stats_ready")
    rstd_ready = sem("r_rstd_ready")
    xn_ready = sem("r_xn_ready")
    xn_copied = sem("r_xn_copied")
    xnT_pe = sem("r_xnT_pe")
    xnT_ready = sem("r_xnT_ready")
    logit_pe = sem("logit_pe")
    chain_v = sem("r_vec_chain")
    chain_s = sem("r_stats_chain")
    chain_p = sem("r_pool_chain")
    consts_ready = sem("r_consts_ready")
    top_ready = sem("top_ready")
    prob_ready = sem("prob_ready")
    hot_ready = sem("hot_ready")
    count_pe = sem("count_pe")
    dest_ready = sem("dest_ready")
    scattered = sem("scattered")

    QUARTERS = 4

    def tiles(q):
        return slice(q * NT // QUARTERS, (q + 1) * NT // QUARTERS)

    def pairs(q):
        return q * B // 2 // QUARTERS, (q + 1) * B // 2 // QUARTERS

    with nc.Block() as block:
        @block.sync
        def _(sp):
            sp.dma_start(gate_w[:], t["L0_ffn_gate_w"]).then_inc(w_in, 16)
            sp.dma_start(gate_b[:], t["L0_ffn_gate_b"].rearrange("(a n) -> a n", a=1).broadcast_to([P, E]))\
              .then_inc(w_in, 16)
            sp.wait_ge(zero_ready, 1)
            for e in range(E):
                sp.dma_start(expert_in[e * CAP:(e + 1) * CAP].rearrange("(p c) d -> p (c d)", p=P), zero[:])\
                  .then_inc(zeroed, 16)
            sp.wait_ge(zeroed, E * 16)

        @block.gpsimd
        def _(pool):
            nc.gpsimd.memset(zero[:], 0.0).then_inc(zero_ready, 1)
            chain = Chain(pool, chain_p)
            chain.link(nc.gpsimd.memset(upper[:], 1.0))
            nc.gpsimd.affine_select(out=upper[:], in_=upper[:], compare_op=ALU.is_ge, fill=0.0, base=0,
                                    pattern=[[1, P]], channel_multiplier=-1)
            nc.gpsimd.memset(all_ones[:], 1.0)
            for e in range(E):
                nc.gpsimd.memset(rank[:, :, e], float(E - e))
                nc.gpsimd.memset(first[:, :, e], float(e * CAP))
            chain.link(nc.gpsimd.iota(spare_i[:], pattern=[[P, NT]], base=E * CAP, channel_multiplier=1))
            nc.gpsimd.tensor_copy(spare[:], spare_i[:]).then_inc(consts_ready, 1)

            def deviations(q):
                pool.wait_ge(stats_ready, q + 1)
                nc.gpsimd.tensor_tensor(rstd[:, tiles(q)], mv[:, tiles(q), 1], neg_half[:, 0:NT // QUARTERS], ALU.pow)\
                  .then_inc(rstd_ready, 1)

            def scatter(q):
                pool.wait_ge(dest_ready, q + 1)
                for n in range(q * NT // QUARTERS, (q + 1) * NT // QUARTERS):
                    nc.gpsimd.indirect_dma_start(out=expert_in[:, :],
                                                 out_offset=bass.IndirectOffsetOnAxis(ap=dest_u[:, n:n + 1], axis=0),
                                                 in_=xn[:, n, :], in_offset=None).then_inc(scattered, 16)

            deviations(0)
            deviations(1)
            deviations(2)
            pool.wait_ge(zeroed, E * 16)
            scatter(0)
            deviations(3)
            scatter(1)
            scatter(2)
            scatter(3)
            pool.wait_ge(scattered, NT * 16)

        @block.scalar
        def _(act):
            for q in range(QUARTERS):
                with act.Fori(*pairs(q)) as pair:
                    for s in range(2):
                        b = pair * 2 + s
                        act.wait_ge(xn_ready, b + 1)
                        nc.scalar.activation(xn[:, bass.ds(b * T, T), :], xn_slot[:, s], ACT.Copy).then_inc(xn_copied, 1)
                        act.wait_ge(xnT_pe, b + 1)
                        nc.scalar.activation(xnT[:, s, :], psum.banks[s], ACT.Copy).then_inc(xnT_ready, 1)
                act.wait_ge(top_ready, q + 1)
                nc.scalar.activation(prob[:, tiles(q)], prob[:, tiles(q)], ACT.Exp).then_inc(prob_ready, 1)

        @block.tensor
        def _(pe):
            pe.wait_ge(w_in, 32)
            for q in range(QUARTERS):
                with pe.Fori(*pairs(q)) as pair:
                    for s in range(2):
                        b = pair * 2 + s
                        pe.wait_ge(xn_ready, b + 1)
                        for it in range(T):
                            m = nc.tensor.transpose(psum.banks[s][:, it * P:(it + 1) * P], xn_slot[:, s, it, :], ident[:])
                        m.then_inc(xnT_pe, 1)
                    for s in range(2):
                        b = pair * 2 + s
                        pe.wait_ge(xnT_ready, b + 1)
                        for it in range(T):
                            m = nc.tensor.matmul(psum.logit[:, bass.ds((b * T + it) * E, E)],
                                                 xnT[:, s, it * P:(it + 1) * P], gate_w[:], start=True, stop=True)
                        m.then_inc(logit_pe, 1)
                if q == 0:
                    pe.wait_ge(consts_ready, 1)
                pe.wait_ge(hot_ready, q + 1)
                hot_q = hot_bf[:, tiles(q)].rearrange("p n e -> p (n e)")
                cols = slice(q * NT * E // QUARTERS, (q + 1) * NT * E // QUARTERS)
                nc.tensor.matmul(psum.place[:, cols], upper[:], hot_q, start=True, stop=True)
                nc.tensor.matmul(psum.count[:, cols], all_ones[:], hot_q, start=True, stop=True).then_inc(count_pe, 1)

        @block.vector
        def _(dve):
            chain = Chain(dve, chain_v)
            stats_chain = Chain(dve, chain_s)

            def statistics(q):
                with dve.Fori(q * B // QUARTERS, (q + 1) * B // QUARTERS) as b:
                    stats_chain.turn(0, b, 3)
                    for it in range(T):
                        m = nc.vector.bn_stats(stats[:, it, :], x_all[:, b * T + it, :])
                    stats_chain.link(m)
                    nc.vector.memset(wait_spot[:], 0.0)
                    for it in range(T):
                        m = nc.vector.bn_aggr(mv_slot[:, it, :], stats[:, it, :])
                    stats_chain.link(m)
                    stats_chain.link(nc.vector.tensor_copy(mv[:, bass.ds(b * T, T), :], mv_slot[:]))
                chain.link(nc.vector.memset(wait_spot[:], 0.0))
                nc.vector.tensor_scalar(mv[:, tiles(q), 1], mv[:, tiles(q), 1], 1e-5, None, ALU.add).then_inc(stats_ready, 1)

            def normalise(q):
                dve.wait_ge(rstd_ready, q + 1)

                def one(b, s):
                    for it in range(T):
                        m = nc.vector.tensor_scalar(xn_slot[:, s, it, :], x_all[:, b * T + it, :],
                                                    mv[:, b * T + it, 0:1], rstd[:, bass.ds(b * T + it, 1)],
                                                    ALU.subtract, ALU.mult)
                    m.then_inc(xn_ready, 1)

                lo, hi = pairs(q)
                if q == 0:
                    one(0, 0)
                    one(1, 1)
                    lo = 1
                with dve.Fori(lo, hi) as pair:
                    for s in range(2):
                        dve.wait_ge(xnT_ready, pair * 2 + s - 1)
                        one(pair * 2 + s, s)

            def route(q):
                lo, hi = q * NT // QUARTERS, (q + 1) * NT // QUARTERS
                n, width = tiles(q), hi - lo
                dve.wait_ge(logit_pe, (q + 1) * B // QUARTERS)
                chain.link(nc.vector.tensor_tensor(logit[:, n], psum.logit.rearrange("p (n e) -> p n e", e=E)[:, n],
                                                   gate_b[:].unsqueeze(1).broadcast_to([P, width, E]), ALU.add))
                chain.link(nc.vector.tensor_reduce(top[:, n], logit[:, n], AX, ALU.max))
                top_e = top[:, n].unsqueeze(2).broadcast_to([P, width, E])
                nc.vector.tensor_tensor(prob[:, n], logit[:, n], top_e, ALU.subtract).then_inc(top_ready, 1)
                chain.link(nc.vector.tensor_tensor(hot[:, n], logit[:, n], top_e, ALU.is_equal))
                chain.link(nc.vector.tensor_tensor(hot[:, n], hot[:, n], rank[:, n], ALU.mult))
                chain.link(nc.vector.tensor_reduce(total[:, n], hot[:, n], AX, ALU.max))
                chain.link(nc.vector.tensor_tensor(hot[:, n], hot[:, n], total[:, n].unsqueeze(2).broadcast_to([P, width, E]),
                                                   ALU.is_equal))
                nc.vector.tensor_copy(hot_bf[:, n], hot[:, n]).then_inc(hot_ready, 1)
                chain.link(nc.vector.tensor_tensor(offset[:, n], first[:, n], hot[:, n], ALU.mult))
                nc.vector.tensor_reduce(queue[:, n], offset[:, n], AX, ALU.add)
                dve.wait_ge(prob_ready, q + 1)
                chain.link(nc.vector.tensor_reduce(total[:, n], prob[:, n], AX, ALU.add))
                chain.link(nc.vector.reciprocal(share[:, n], total[:, n]))
                dve.wait_ge(count_pe, q + 1)
                counts = psum.count.rearrange("p (n e) -> p e n", e=E)
                for e in range(E):
                    m = nc.vector.tensor_tensor_scan(before[:, e, 1:hi + 1], ones[:, 0:hi], counts[:, e, 0:hi], 0.0,
                                                     ALU.mult, ALU.add)
                chain.link(m)
                chain.link(nc.vector.tensor_tensor(prob[:, n], psum.place.rearrange("p (n e) -> p n e", e=E)[:, n],
                                                   before[:, :, n].rearrange("p e n -> p n e"), ALU.add))
                chain.link(nc.vector.tensor_tensor(prob[:, n], prob[:, n], hot[:, n], ALU.mult))
                chain.link(nc.vector.tensor_reduce(place[:, n], prob[:, n], AX, ALU.add))
                nc.vector.tensor_scalar(kept[:, n], place[:, n], float(CAP), None, ALU.is_le)
                chain.link(nc.vector.tensor_scalar(dest[:, n], place[:, n], float(CAP), -1.0, ALU.min, ALU.add))
                chain.link(nc.vector.tensor_tensor(dest[:, n], dest[:, n], queue[:, n], ALU.add))
                nc.vector.tensor_copy(slot_of[:, n], dest[:, n])
                nc.vector.tensor_tensor(share[:, n], share[:, n], kept[:, n], ALU.mult)
                chain.link(nc.vector.tensor_tensor(dest[:, n], dest[:, n], spare[:, n], ALU.subtract))
                chain.link(nc.vector.tensor_tensor(dest[:, n], dest[:, n], kept[:, n], ALU.mult))
                chain.link(nc.vector.tensor_tensor(dest[:, n], dest[:, n], spare[:, n], ALU.add))
                nc.vector.tensor_copy(dest_u[:, n], dest[:, n]).then_inc(dest_ready, 1)

            chain.link(nc.vector.memset(before[:], 0.0))
            statistics(0)
            statistics(1)
            normalise(0)
            statistics(2)
            dve.wait_ge(w_in, 32)
            dve.wait_ge(consts_ready, 1)
            route(0)
            normalise(1)
            statistics(3)
            route(1)
            normalise(2)
            route(2)
            normalise(3)
            route(3)


def run_experts(nc, t, stage, expert_in, expert_out, deg, dinv, ident, neg_half, psum):
    def sb(name, shape, dt=F32):
        return stage.enter_context(nc.sbuf_tensor(name, shape, dt))

    def sem(name):
        return stage.enter_context(nc.semaphore(name))

    C = CAP // P
    FK = F // P
    w1 = sb("w1", [P, 2, F])
    w2 = sb("w2", [P, E, FK, D])
    b1 = sb("b1", [P, E, FK])
    b2 = sb("b2", [P, E, D])
    rows = sb("rows", [P, 2, C, D])
    rowsT = sb("rowsT", [P, 2, C * P])
    hidden = sb("hidden", [P, 2, FK, C * P])
    y = sb("y", [P, 2, C, D])
    CHUNKS = [(0, 4), (4, 8), (8, C)]

    b1_in = sem("b1_in")
    deg_ready = sem("deg_ready")
    w2_in = sem("w2_in")
    rows_in = sem("rows_in")
    rowsT_pe = sem("rowsT_pe")
    rowsT_ready = sem("rowsT_ready")
    hidden_pe = sem("hidden_pe")
    hidden_ready = sem("hidden_ready")
    y_pe = sem("y_pe")
    y_ready = sem("y_ready")
    y_stored = sem("y_stored")

    bank_t, bank_h, bank_y = psum.banks[0:3], psum.banks[3:6], [psum.banks[6], psum.banks[7], psum.banks[6]]
    in_v = expert_in[0:E * CAP].rearrange("(e p c) d -> e p c d", e=E, p=P)
    out_v = expert_out.rearrange("(e p c) d -> e p c d", e=E, p=P)

    with nc.Block() as block:
        @block.sync
        def _(sp):
            sp.dma_start(rows[:, 0], in_v[0]).then_inc(rows_in, 16)
            sp.dma_start(w1[:, 0], t["L0_ffn_w1"][0]).then_inc(rows_in, 16)
            with nc.allow_non_contiguous_dma("small biases"):
                sp.dma_start(b1[:], t["L0_ffn_b1"].rearrange("e (k p) -> p e k", p=P)).then_inc(b1_in, 16)
            sp.dma_start(w2[:], t["L0_ffn_w2"].rearrange("e (k p) d -> p e k d", p=P)).then_inc(w2_in, 16)
            sp.dma_start(b2[:], t["L0_ffn_b2"].rearrange("(a e) d -> a e d", a=1).broadcast_to([P, E, D])).then_inc(w2_in, 16)
            sp.wait_ge(rows_in, 32)
            sp.dma_start(rows[:, 1], in_v[1]).then_inc(rows_in, 16)
            sp.dma_start(w1[:, 1], t["L0_ffn_w1"][1]).then_inc(rows_in, 16)
            with sp.Fori(2, E) as e:
                sp.wait_ge(rows_in, e * 32)
                sp.wait_ge(hidden_pe, e * 12 - 12)
                sp.dma_start(rows[:, e % 2], in_v[e]).then_inc(rows_in, 16)
                sp.dma_start(w1[:, e % 2], t["L0_ffn_w1"][e]).then_inc(rows_in, 16)

        @block.gpsimd
        def _(pool):
            pool.wait_ge(deg_ready, 1)
            for k in range(B * T // 16):
                n = slice(k * 16, (k + 1) * 16)
                nc.gpsimd.tensor_tensor(dinv[:, n], deg[:, n], neg_half[:], ALU.pow)

            def store(e):
                pool.wait_ge(y_ready, (e + 1) * 3)
                if later(e):
                    pool.wait_ge(y_stored, e * 16)
                nc.gpsimd.dma_start(out_v[e], y[:, e % 2]).then_inc(y_stored, 16)

            store(0)
            with pool.Fori(1, E) as e:
                store(e)
            pool.wait_ge(y_stored, E * 16)

        @block.scalar
        def _(act):
            act.wait_ge(b1_in, 16)

            def turn(e):
                for k, (lo, hi) in enumerate(CHUNKS):
                    act.wait_ge(rowsT_pe, e * 3 + k + 1)
                    nc.scalar.activation(rowsT[:, e % 2, lo * P:hi * P], bank_t[k][:, 0:(hi - lo) * P], ACT.Copy)\
                      .then_inc(rowsT_ready, 1)

            def relu(e):
                for f in range(FK):
                    for k, (lo, hi) in enumerate(CHUNKS):
                        act.wait_ge(hidden_pe, e * 12 + f * 3 + k + 1)
                        nc.scalar.activation(hidden[:, e % 2, f, lo * P:hi * P], bank_h[k][:, 0:(hi - lo) * P], ACT.Relu,
                                             bias=b1[:, e, f:f + 1]).then_inc(hidden_ready, 1)

            turn(0)
            with act.Fori(0, E - 1) as e:
                relu(e)
                turn(e + 1)
            relu(E - 1)

        @block.tensor
        def _(pe):
            def turn(e, s):
                pe.wait_ge(rows_in, (e + 1) * 32)
                for k, (lo, hi) in enumerate(CHUNKS):
                    for c in range(lo, hi):
                        m = nc.tensor.transpose(bank_t[k][:, (c - lo) * P:(c - lo + 1) * P], rows[:, s, c, :], ident[:])
                    m.then_inc(rowsT_pe, 1)

            def up(e, s):
                for f in range(FK):
                    for k, (lo, hi) in enumerate(CHUNKS):
                        if f == 0:
                            pe.wait_ge(rowsT_ready, e * 3 + k + 1)
                        if f > 0 or later(e):
                            pe.wait_ge(hidden_ready, e * 12 + f * 3 + k - 2)
                        nc.tensor.matmul(bank_h[k][:, 0:(hi - lo) * P], w1[:, s, f * P:(f + 1) * P],
                                         rowsT[:, s, lo * P:hi * P], start=True, stop=True).then_inc(hidden_pe, 1)

            def down(e, s):
                pe.wait_ge(hidden_ready, (e + 1) * 12)
                for k, (lo, hi) in enumerate(CHUNKS):
                    if k == 2:
                        pe.wait_ge(y_ready, e * 3 + 1)
                    elif later(e):
                        pe.wait_ge(y_ready, e * 3)
                    for c in range(lo, hi):
                        for f in range(FK):
                            m = nc.tensor.matmul(bank_y[k][:, (c - lo) * D:(c - lo + 1) * D],
                                                 hidden[:, s, f, c * P:(c + 1) * P], w2[:, e, f, :],
                                                 start=(f == 0), stop=(f == FK - 1))
                    m.then_inc(y_pe, 1)

            turn(0, 0)
            up(0, 0)
            turn(1, 1)
            pe.wait_ge(w2_in, 32)
            down(0, 0)
            with pe.Fori(0, E // 2 - 1) as pair:
                for s in (1, 0):
                    e = pair * 2 + 2 - s
                    up(e, s)
                    turn(e + 1, 1 - s)
                    down(e, s)
            up(E - 1, 1)
            down(E - 1, 1)

        @block.vector
        def _(dve):
            nc.vector.tensor_scalar(deg[:], deg[:], 1.0, None, ALU.add).then_inc(deg_ready, 1)
            dve.wait_ge(w2_in, 32)

            def turn(e):
                for k, (lo, hi) in enumerate(CHUNKS):
                    dve.wait_ge(y_pe, e * 3 + k + 1)
                    if later(e - 1):
                        dve.wait_ge(y_stored, e * 16 - 16)
                    nc.vector.tensor_tensor(y[:, e % 2, lo:hi, :],
                                            bank_y[k][:, 0:(hi - lo) * D].rearrange("p (c d) -> p c d", d=D),
                                            b2[:, bass.ds(e, 1), :].broadcast_to([P, hi - lo, D]), ALU.add).then_inc(y_ready, 1)

            turn(0)
            turn(1)
            with dve.Fori(2, E) as e:
                turn(e)


def gcn_layer(nc, t, stage, x_all, adjT, dinv, expert_out, slot_of, share, ident, ident_bf, neg_half, psum):
    def sb(name, shape, dt=F32):
        return stage.enter_context(nc.sbuf_tensor(name, shape, dt))

    def sem(name):
        return stage.enter_context(nc.semaphore(name))

    NT = B * T
    w = sb("g_w", [P, D])
    wT = sb("g_wT", [P, D])
    bias = sb("g_bias", [P, D])
    y_in = sb("y_in", [P, NT, D])
    y_ok = sb("y_ok", [P, 2, T, D])
    same = sb("same", [P, 2, T, D])
    finite = sb("finite", [P, 2, T, D], U32)
    stats = sb("g_stats", [P, T, 6])
    mv_slot = sb("g_mv_slot", [P, T, 2])
    y_w = sb("y_w", [P, 2, T, D])
    mv = sb("g_mv", [P, NT, 2])
    rstd = sb("g_rstd", [P, NT])
    scale = sb("g_scale", [P, NT])
    wait_spot = sb("g_wait_spot", [P, 1])
    u = sb("u", [P, 2, T, D])
    u_part = sb("u_part", [P, 2, 3, T, D], BF16)
    hT = sb("hT", [P, 2, N])
    msg = sb("msg", [P, 2, T, D])

    w_in = sem("g_w_in")
    wT_pe = sem("g_wT_pe")
    wT_ready = sem("g_wT_ready")
    gathered = [sem(f"gathered{q}") for q in range(4)]
    y_weighted = sem("y_weighted")
    chain_v = sem("g_vec_chain")
    chain_p = sem("g_pool_chain")
    x2_ready = sem("x2_ready")
    stats_ready = sem("g_stats_ready")
    scale_ready = sem("scale_ready")
    u_ready = sem("u_ready")
    high_ready = sem("high_ready")
    rest_ready = sem("rest_ready")
    mid_ready = sem("mid_ready")
    parts_ready = sem("parts_ready")
    agg_pe = sem("agg_pe")
    hT_ready = sem("hT_ready")
    out_pe = sem("g_out_pe")
    out_used = sem("g_out_used")

    with nc.Block() as block:
        @block.sync
        def _(sp):
            sp.dma_start(w[:], t["L1_gnn_W"]).then_inc(w_in, 16)
            sp.dma_start(bias[:], t["L1_gnn_b"].rearrange("(a n) -> a n", a=1).broadcast_to([P, D])).then_inc(w_in, 16)

        @block.gpsimd
        def _(pool):
            chain = Chain(pool, chain_p)

            def gather(q):
                for n in range(q * NT // 4, (q + 1) * NT // 4):
                    nc.gpsimd.indirect_dma_start(out=y_in[:, n, :], out_offset=None, in_=expert_out[:, :],
                                                 in_offset=bass.IndirectOffsetOnAxis(ap=slot_of[:, n:n + 1], axis=0))\
                      .then_inc(gathered[q], 16)

            def scales(q):
                pool.wait_ge(stats_ready, q + 1)
                n = slice(q * NT // 4, (q + 1) * NT // 4)
                chain.link(nc.gpsimd.tensor_tensor(rstd[:, n], mv[:, n, 1], neg_half[:, 0:NT // 4], ALU.pow))
                nc.gpsimd.tensor_tensor(scale[:, n], rstd[:, n], dinv[:, n], ALU.mult).then_inc(scale_ready, 1)

            gather(0)
            gather(1)
            scales(0)
            gather(2)
            scales(1)
            gather(3)
            scales(2)
            scales(3)

        @block.scalar
        def _(act):
            act.wait_ge(wT_pe, 1)
            nc.scalar.activation(wT[:], psum.banks[7][:, 0:D], ACT.Copy).then_inc(wT_ready, 1)

            def turn(b):
                act.wait_ge(u_ready, b + 1)
                nc.scalar.activation(u_part[:, b % 2, 0], u[:, b % 2], ACT.Copy).then_inc(high_ready, 1)
                act.wait_ge(rest_ready, b + 1)
                nc.scalar.activation(u_part[:, b % 2, 1], u[:, b % 2], ACT.Copy).then_inc(mid_ready, 1)

            def move(b):
                act.wait_ge(agg_pe, b + 1)
                nc.scalar.activation(hT[:, b % 2, :], psum.whole[:, b % 2, :], ACT.Copy).then_inc(hT_ready, 1)

            turn(0)
            with act.Fori(0, B - 1) as b:
                turn(b + 1)
                move(b)
            move(B - 1)

        @block.tensor
        def _(pe):
            pe.wait_ge(w_in, 32)
            nc.tensor.transpose(psum.banks[7][:, 0:D], w[:], ident[:]).then_inc(wT_pe, 1)
            pe.wait_ge(wT_ready, 1)

            def aggregate(b):
                pe.wait_ge(parts_ready, b + 1)
                for part in range(3):
                    for jt in range(T):
                        nc.tensor.matmul(psum.whole[:, b % 2, :], u_part[:, b % 2, part, jt, :], adjT[:, b, jt, :],
                                         start=(part == 0 and jt == 0), stop=False, skip_group_check=True)
                        m = nc.tensor.matmul(psum.whole[:, b % 2, jt * P:(jt + 1) * P], u_part[:, b % 2, part, jt, :],
                                             ident_bf[:], start=False, stop=(part == 2 and jt == T - 1),
                                             skip_group_check=True)
                m.then_inc(agg_pe, 1)

            def project(b, s):
                pe.wait_ge(hT_ready, b + 1)
                if later(b - 1):
                    pe.wait_ge(out_used, b - 1)
                for it in range(T):
                    m = nc.tensor.matmul(psum.whole[:, 2 + s, it * P:(it + 1) * P], hT[:, s, it * P:(it + 1) * P],
                                         wT[:], start=True, stop=True)
                m.then_inc(out_pe, 1)

            aggregate(0)
            aggregate(1)
            project(0, 0)
            aggregate(2)
            project(1, 1)
            with pe.Fori(1, B // 2 - 1) as pair:
                for s in range(2):
                    aggregate(pair * 2 + s + 1)
                    project(pair * 2 + s, s)
            aggregate(B - 1)
            project(B - 2, 0)
            project(B - 1, 1)

        @block.vector
        def _(dve):
            chain = Chain(dve, chain_v)
            dve.wait_ge(w_in, 32)

            def weigh(b, s):
                chain.link(nc.vector.tensor_tensor(y_w[:, s], y_in[:, bass.ds(b * T, T), :],
                                                   share[:, bass.ds(b * T, T)].unsqueeze(2).broadcast_to([P, T, D]),
                                                   ALU.mult))
                nc.vector.tensor_scalar(y_ok[:, s], y_w[:, s], 1e4, -1e4, ALU.min, ALU.max)
                nc.vector.tensor_tensor(same[:, s], y_w[:, s], y_w[:, s], ALU.is_equal)
                nc.vector.tensor_scalar(finite[:, s], y_w[:, s], 0.0, 0.0, ALU.mult, ALU.is_equal).then_inc(y_weighted, 1)
                dve.wait_ge(y_weighted, b + 1)

            def add(b, s):
                chain.link(nc.vector.tensor_tensor(y_ok[:, s], y_ok[:, s], same[:, s], ALU.mult))
                chain.link(nc.vector.copy_predicated(y_ok[:, s], finite[:, s], y_w[:, s]))
                xb = x_all[:, bass.ds(b * T, T), :]
                nc.vector.tensor_tensor(xb, xb, y_ok[:, s], ALU.add).then_inc(x2_ready, 1)
                dve.wait_ge(x2_ready, b + 1)
                for it in range(T):
                    m = nc.vector.bn_stats(stats[:, it, :], x_all[:, b * T + it, :])
                chain.link(m)
                nc.vector.memset(wait_spot[:], 0.0)
                for it in range(T):
                    m = nc.vector.bn_aggr(mv_slot[:, it, :], stats[:, it, :])
                chain.link(m)
                chain.link(nc.vector.tensor_copy(mv[:, bass.ds(b * T, T), :], mv_slot[:]))

            def scaled(b):
                if not isinstance(b, int) or b > 1:
                    dve.wait_ge(agg_pe, b - 1)
                for it in range(T):
                    m = nc.vector.tensor_scalar(u[:, b % 2, it, :], x_all[:, b * T + it, :], mv[:, b * T + it, 0:1],
                                                scale[:, bass.ds(b * T + it, 1)], ALU.subtract, ALU.mult)
                m.then_inc(u_ready, 1)

            def rest(b):
                dve.wait_ge(high_ready, b + 1)
                nc.vector.tensor_tensor(u[:, b % 2], u[:, b % 2], u_part[:, b % 2, 0], ALU.subtract).then_inc(rest_ready, 1)

            def low(b):
                dve.wait_ge(mid_ready, b + 1)
                nc.vector.tensor_tensor(u_part[:, b % 2, 2], u[:, b % 2], u_part[:, b % 2, 1], ALU.subtract).then_inc(parts_ready, 1)

            def message(b):
                dve.wait_ge(out_pe, b + 1)
                for it in range(T):
                    m = nc.vector.scalar_tensor_tensor(out=msg[:, b % 2, it, :], in0=psum.whole[:, 2 + b % 2, it * P:(it + 1) * P],
                                                       scalar=dinv[:, bass.ds(b * T + it, 1)], in1=bias[:],
                                                       op0=ALU.mult, op1=ALU.add)
                m.then_inc(out_used, 1)

            def update(b):
                dve.wait_ge(out_used, b + 1)
                xb = x_all[:, bass.ds(b * T, T), :]
                nc.vector.scalar_tensor_tensor(out=xb, in0=msg[:, b % 2], scalar=0.0, in1=xb, op0=ALU.max, op1=ALU.add)

            def convolve(lo, hi):
                with dve.Fori(lo, hi) as b:
                    scaled(b + 2)
                    message(b - 1)
                    rest(b + 2)
                    update(b - 1)
                    low(b + 2)

            dve.wait_ge(gathered[0], NT // 4 * 16)
            weigh(0, 0)
            start = chain.k
            for q in range(4):
                with dve.Fori(q * B // 8, (q + 1) * B // 8 - 1) as pair:
                    for s in range(2):
                        chain.turn(start, pair * 2 + s, 6)
                        weigh(pair * 2 + s + 1, 1 - s)
                        add(pair * 2 + s, s)
                b = (q + 1) * B // 4 - 2
                chain.turn(start, b, 6)
                weigh(b + 1, 1)
                add(b, 0)
                chain.turn(start, b + 1, 6)
                if q < 3:
                    dve.wait_ge(gathered[q + 1], NT // 4 * 16)
                    weigh(b + 2, 0)
                add(b + 1, 1)
                n = slice(q * NT // 4, (q + 1) * NT // 4)
                nc.vector.tensor_scalar(mv[:, n, 1], mv[:, n, 1], 1e-5, None, ALU.add).then_inc(stats_ready, 1)
                if q > 0:
                    dve.wait_ge(scale_ready, q)
                    if q == 1:
                        for b in range(3):
                            scaled(b)
                            rest(b)
                            low(b)
                    convolve(max(1, B // 4 * (q - 1) - 2), B // 4 * q - 2)
            dve.wait_ge(scale_ready, 4)
            convolve(B // 4 * 3 - 2, B - 2)
            for b in (B - 3, B - 2, B - 1):
                message(b)
                update(b)


NH, NX, HD = 4, 4, 32
GROUPS = [(sc, tc) for sc in range(T) for tc in range(sc + 1)]
MAX_PARTS = [(0, (0, 1, 2, 3)), (1, (0, 1)), (1, (2, 3))] + [(sc, (e,)) for sc in (2, 3) for e in range(NX)]


MAX_AT = 20


def attention_schedule(pre, post):
    beside = {}

    def put(at, *jobs):
        beside.setdefault(at, []).extend(jobs)

    put(0, ("max_split", 1))
    for sc, at in ((1, (0, 0, 1, 1)), (2, (6, 7, 8, 9)), (3, (11, 12, 13, 15))):
        for n in range(NH):
            put(at[n], ("negmax", n, sc))
    if pre:
        put(0, ("norm_x",))
        put(1, ("scale_x",))
        put(3, ("xT", 0), ("xT", 1))
        put(4, ("sx",))
        for e in range(NX):
            put(5 + e, ("q", e))
            put(6 + e, ("mid", e))
        put(9, ("k",), ("v",))
        put(10, ("mid", NX))
        for k, job in enumerate(MAX_JOBS):
            put(MAX_AT + k * (40 - MAX_AT) // len(MAX_JOBS), job)
        put(28, ("max_split", 0))
        for n in range(NH):
            put(33 + 2 * n, ("negmax", n, 0))
    if post:
        put(2, ("tok", 3), ("gate", 3))
        put(3, ("mix_logits",))
        put(4, ("mix_weights",))
        for sc in range(T):
            put(5 + sc, ("mix", sc))
        put(8, ("norm_mix",))
    put(14, ("tok", 0), ("gate", 0))
    if post:
        put(16, ("fxT",))
        put(17, ("fc1",))
        put(18, ("fc2",), ("norm_out",))
    put(18, ("tok", 1), ("gate", 1))
    if post:
        put(24, ("foT",))
        put(25, ("fgate",))
        put(26, ("leave",))
    put(29, ("tok", 2), ("gate", 2))
    order = []
    for g, (sc, tc) in enumerate(GROUPS):
        for n in range(NH):
            order.append(("score", g, n))
            if n == NH - 1:
                order += after_values(g - 1) if g > 0 else [("begin",)]
            order += beside.get(4 * g + n, [])
    return order + after_values(len(GROUPS) - 1)


def after_values(g):
    sc, tc = GROUPS[g]
    return [("values", g)] + ([("collect", sc)] if tc == sc else [])


SIDE_JOBS = ("xT", "sx", "q", "k", "v", "max", "negmax", "tok", "gate", "fxT", "fc1", "fc2", "foT", "fgate")
MAX_JOBS = [("max", n, k) for k in range(len(MAX_PARTS)) for n in range(NH)]
FIRST_MAXIMA = sum(MAX_PARTS[job[2]][0] < T // 2 for job in MAX_JOBS)
PRE_JOBS = [("norm_x",), ("scale_x",), ("xT", 0), ("xT", 1), ("sx",)] \
    + [job for e in range(NX) for job in (("q", e), ("mid", e))] + [("k",), ("mid", NX), ("v",)] \
    + MAX_JOBS[:FIRST_MAXIMA] + [("max_split", 0)] + MAX_JOBS[FIRST_MAXIMA:] + [("negmax", n, 0) for n in range(NH)]
POST_JOBS = [("tok", 3), ("gate", 3), ("mix_logits",), ("mix_weights",)] + [("mix", sc) for sc in range(T)] \
    + [("norm_mix",), ("fxT",), ("fc1",), ("fc2",), ("norm_out",), ("foT",), ("fgate",), ("leave",)]


def side_count(order):
    return sum(job[0] in SIDE_JOBS for job in order)


class SideUse:

    def __init__(self):
        self.base, self.k = 0, 0

    def turn(self, each):
        self.base, self.k = each, 0

    def use(self):
        bank, nth = self.k % 2, self.k // 2 + 1
        self.k += 1
        return bank, self.base + nth


def attention_layer(nc, t, stage, x_all, out, ident, ident_bf, ones, neg_half, psum):
    def sb(name, shape, dt=F32):
        return stage.enter_context(nc.sbuf_tensor(name, shape, dt))

    def sem(name):
        return stage.enter_context(nc.semaphore(name))

    SCALE = float(HD) ** 0.5
    LOADS = 7 * NH + 10
    VEC_LINKS, POOL_LINKS = 48, 7
    NAT = 9
    prob = sb("a_prob", [P, 2, NH, NX * P])
    whole = prob[:].rearrange("p a n s -> p (a n s)").rearrange("p (k c) -> p k c", c=P)
    nat, nat_gate, nat_fgate = whole[:, 0:NAT, :], whole[0:NH * NX, NAT:NAT + NX, :], whole[0:NH, NAT + NX, :]
    turned = sb("turned", [P, NAT, P])
    gate_w = sb("a_gate_w", [P, NX, NH * NX])
    fgate_w = sb("a_fgate_w", [P, NH])
    hl_b = sb("hl_b", [P, 1])
    hl_b_row = sb("hl_b_row", [P, P])
    gate_b = sb("a_gate_b", [P, NH * NX])
    ln_g, ln_b, fn_g, fn_b, fc2_b = (sb(n, [P, HD]) for n in ("ln_g", "ln_b", "fn_g", "fn_b", "fc2_b"))
    fc1_b = sb("fc1_b", [P, 1])
    wq_t, wk_t, wv_t, fc1_t, fc2_t, hl_t = turned[:, 0:4, :], turned[:, 4, :], turned[:, 5, :], turned[:, 6, :], \
        turned[:, 7, :], turned[:, 8, :]
    mask_qk = sb("mask_qk", [P, P], BF16)
    mask_kq = sb("mask_kq", [P, NX, P], BF16)

    stats = sb("a_stats", [P, T, 6])
    mv = sb("a_mv", [P, T, 2])
    rstd = sb("a_rstd", [P, T])
    spot = sb("a_spot", [P, 1])
    xn = sb("a_xn", [P, T, D])
    xnT = sb("a_xnT", [P, N])
    sxT = sb("sxT", [P, N])
    not_pad = sb("not_pad", [P, 2, N], BF16)
    resid = sb("resid", [P, T, D])
    q_hi = sb("q_hi", [P, NX, N], BF16)
    q_mid = sb("q_mid", [P, NX, N], BF16)
    q_lo = sb("q_lo", [P, NX, N], BF16)
    q_rest = sb("q_rest", [P, NX, N])
    k_hi = sb("k_hi", [P, N], BF16)
    k_mid = sb("k_mid", [P, N], BF16)
    k_lo = sb("k_lo", [P, N], BF16)
    k_rest = sb("k_rest", [P, N])
    q1 = sb("q1", [P, 2, NH, NX, N], BF16)
    q2 = sb("q2", [P, 2, NH, NX, N], BF16)
    k1 = sb("k1", [P, 2, NH, N], BF16)
    k2 = sb("k2", [P, 2, NH, N], BF16)
    v_next = sb("v_next", [P, T, D])
    v_now = sb("v_now", [P, T, D])
    top = sb("a_top", [P, T, NH, NX])
    neg_top = sb("neg_top", [P, NH * T * NX])
    neg_part = sb("neg_part", [P, NH * T * NX, HD], BF16)
    den = sb("a_den", [P, NX, P])
    att = sb("att", [P, 2, NX, P])
    tok = sb("tok", [P, T, NX, P])
    glog = sb("glog", [P, T, NH, NX])
    gprod = sb("gprod", [P, NX, NH, NX])
    rden = sb("a_rden", [P, T, NX, NH])
    gl = sb("gl", [P, T, NH, NX])
    gtop = sb("gtop", [P, T, NH])
    mixw = sb("mixw", [P, NX, P])
    y = sb("a_y", [P, T, D])
    yc = sb("a_yc", [P, T, D])
    sq = mixw
    s16 = sb("s16", [P, T * NH])
    r16 = sb("r16", [P, T * NH])
    hn = sb("hn", [P, T, D])
    fxT = sb("fxT", [P, N])
    h1 = mixw[:].rearrange("p e c -> p (e c)")
    fo, foT = y, fxT
    fl = gtop
    fmax = sb("fmax", [P, T])

    w_in = sem("a_w_in")
    zeroed = sem("a_zeroed")
    w_pe = sem("a_w_pe")
    w_ready = sem("a_w_ready")
    masks_ready = sem("masks_ready")
    chain_v = sem("a_vec_chain")
    chain_p = sem("a_pool_chain")
    chain_a = sem("a_act_chain")
    side_full = [sem("side_full0"), sem("side_full1")]
    var_ready = sem("a_var_ready")
    rstd_ready = sem("a_rstd_ready")
    xn_ready = sem("a_xn_ready")
    xnT_ready = sem("a_xnT_ready")
    sxT_ready = sem("sxT_ready")
    hi_ready = sem("hi_ready")
    rest_ready = sem("a_rest_ready")
    mid_ready = sem("a_mid_ready")
    lo_ready = sem("lo_ready")
    stack1_in = sem("stack1_in")
    stack2_in = sem("stack2_in")
    top_split = sem("top_split")
    negmax_ready = sem("negmax_ready")
    v_ready = sem("v_ready")
    v_now_ready = sem("v_now_ready")
    score_pe = [sem(f"score_pe{n}") for n in range(NH)]
    prob_ready = [sem(f"prob_ready{n}") for n in range(NH)]
    values_pe = sem("values_pe")
    banks_left = sem("banks_left")
    att_ready = sem("att_ready")
    den_ready = sem("den_ready")
    resid_ready = sem("resid_ready")
    top_ready = sem("a_top_ready")
    tok_copied = sem("tok_copied")
    tok_ready = sem("tok_ready")
    y_biased = sem("y_biased")
    gl_ready = sem("gl_ready")
    gexp_ready = sem("gexp_ready")
    sum_ready = sem("sum_ready")
    hn_ready = sem("hn_ready")
    fxT_ready = sem("fxT_ready")
    h1_ready = sem("h1_ready")
    h1m_ready = sem("h1m_ready")
    fo_ready = sem("fo_ready")
    foT_ready = sem("foT_ready")
    fl_ready = sem("fl_ready")
    fexp_ready = sem("fexp_ready")
    fl_scaled = sem("fl_scaled")
    x4_ready = sem("x4_ready")
    stored = sem("stored")

    side = psum.banks[6:8]
    STACK1_DMAS, STACK2_DMAS = NH * 8, NH * 4
    FIRST, MID, LAST = (attention_schedule(*f) for f in ((True, False), (True, True), (False, True)))
    NG = len(GROUPS)
    NEG = NH * T
    RES_JOBS = [job for _ in range(NH) for job in (("xT", 0), ("xT", 1), ("sx",))]
    BEFORE = side_count(RES_JOBS) + side_count(PRE_JOBS)
    assert side_count(RES_JOBS) % 2 == 0 and side_count(MID) % 2 == 0 and (BEFORE + side_count(FIRST)) % 2 == 0

    def run_turns(eng, handle, chain=None, links=0, begins=None):
        side_use = SideUse()
        handle(("norm_x",), -NH, None)
        handle(("scale_x",), -NH, None)
        for r in range(NH):
            if r < NH - 1:
                handle(("norm_x",), r + 1 - NH, None)
            for job in [("xT", 0), ("xT", 1)]:
                handle(job, r - NH, side_use.use())
            if r < NH - 1:
                handle(("scale_x",), r + 1 - NH, None)
            handle(("resid",), r - NH, side_use.use())

        def turn(order, b):
            for job in order:
                graph = b + 1 if job in PRE_JOBS else b - 1 if job in POST_JOBS else b
                handle(job, graph, side_use.use() if job[0] in SIDE_JOBS else None)

        turn(PRE_JOBS, -1)
        turn(FIRST, 0)
        if chain:
            start = chain.k
        each = (BEFORE + side_count(FIRST)) // 2
        with eng.Fori(1, B - 1) as b:
            if begins:
                begins(b)
            side_use.turn((b - 1) * (side_count(MID) // 2) + each)
            if chain:
                chain.turn(start, b - 1, links)
            turn(MID, b)
            if chain:
                assert chain.k == links, chain.k
        if begins:
            begins(B - 1)
        side_use.turn((B - 2) * (side_count(MID) // 2) + each)
        if chain:
            chain.turn(start, B - 2, links)
        turn(LAST, B - 1)
        turn(POST_JOBS, B)

    def heads(x):
        return x.rearrange("p t (n d) -> p (t n) d", d=HD)

    def each(x):
        return x.unsqueeze(2).broadcast_to([P, T * NH, HD])

    def row(x):
        return x[:].unsqueeze(1).broadcast_to([P, T * NH, HD])

    def slot(b):
        return b % 2

    def read(job, b):
        name, arg = job[0], job[1:]
        if name == "max":
            return top_ready, b * len(MAX_JOBS) + MAX_JOBS.index(job) + 1
        if name == "negmax":
            return negmax_ready, b * NEG + arg[1] * NH + arg[0] + 1
        if name in ("q", "k"):
            return rest_ready, b * (NX + 1) + (arg[0] if arg else NX) + 1
        if name in ("tok", "gate"):
            return {"tok": tok_copied, "gate": tok_ready}[name], b * T + arg[0] + 1
        if name == "xT":
            return xnT_ready, (b + NH) * 2 + arg[0] + 1
        if name == "resid":
            return resid_ready, b + NH + 1
        return {"sx": sxT_ready, "v": v_ready, "fxT": fxT_ready, "fc1": h1_ready, "fc2": y_biased, "foT": foT_ready,
                "fgate": fl_ready}[name], b + 1

    with nc.Block() as block:
        @block.sync
        def _(sp):
            sp.wait_ge(zeroed, 1)
            loads = []
            for n in range(NH):
                d = slice(n * HD, (n + 1) * HD)
                loads += [(nat[d, 0:NX, d], t["L1_ffn_wq"][n].rearrange("e o d -> o e d")),
                          (nat[d, 4, d], t["L1_ffn_wk"][n]),
                          (nat[d, 5, d], t["L1_ffn_wv"][n]),
                          (nat[d, 6, d], t["L1_ffn_fc1_w"]),
                          (nat[d, 7, d], t["L1_ffn_fc2_w"]),
                          (nat_gate[n * NX:(n + 1) * NX, :, d], t["L1_ffn_gate_w"][n].rearrange("g (e d) -> g e d", e=NX)),
                          (fc1_b[d, :], t["L1_ffn_fc1_b"].rearrange("(p a) -> p a", a=1))]

            def row(src, width):
                return src.rearrange("(a n) -> a n", a=1).broadcast_to([P, width])

            loads += [(nat[:, 8, :], t["L1_ffn_hl_w"].rearrange("n d h -> (n d) h")),
                      (nat_fgate, t["L1_ffn_fgate_w"]),
                      (hl_b[:], t["L1_ffn_hl_b"].rearrange("n (d a) -> (n d) a", a=1)),
                      (hl_b_row[:], row(t["L1_ffn_hl_b"].rearrange("n d -> (n d)"), P)),
                      (gate_b[:], row(t["L1_ffn_gate_b"].rearrange("n e -> (n e)"), NH * NX)),
                      (ln_g[:], row(t["L1_ffn_ln_g"], HD)), (ln_b[:], row(t["L1_ffn_ln_b"], HD)),
                      (fn_g[:], row(t["L1_ffn_fnorm_g"], HD)), (fn_b[:], row(t["L1_ffn_fnorm_b"], HD)),
                      (fc2_b[:], row(t["L1_ffn_fc2_b"], HD))]
            assert len(loads) == LOADS
            for dst, src in loads:
                with nc.allow_non_contiguous_dma("small weights"):
                    sp.dma_start(dst, src).then_inc(w_in, 16)

            def place(b, placed, arrived):
                for n in range(NH):
                    d = slice(n * HD, (n + 1) * HD)
                    for dst, g, part in placed:
                        sp.dma_start(dst[g * HD:(g + 1) * HD, slot(b), n], part[d]).then_inc(arrived, 16)

            def stack(b):
                sp.wait_ge(hi_ready, (b + 1) * (NX + 1))
                place(b, ((q1, 0, q_hi), (k1, 0, k_hi), (q1, 1, q_hi), (k1, 2, k_hi)), stack1_in)
                sp.wait_ge(mid_ready, (b + 1) * (NX + 1))
                place(b, ((q1, 2, q_mid), (k1, 1, k_mid), (q1, 3, q_mid)), stack1_in)
                sp.wait_ge(lo_ready, (b + 1) * (NX + 1))
                place(b, ((k1, 3, k_mid),), stack1_in)
                place(b, ((q2, 0, q_hi), (k2, 1, k_hi), (k2, 0, k_lo), (q2, 1, q_lo)), stack2_in)

            out_v = out.rearrange("b (t p) d -> b p t d", p=P)

            def store(b):
                sp.wait_ge(x4_ready, b + 1)
                sp.dma_start(out_v[b], x_all[:, bass.ds(b * T, T), :]).then_inc(stored, 16)

            stack(0)
            stack(1)
            with sp.Fori(1, B - 1) as b:
                stack(b + 1)
                store(b - 1)
            store(B - 2)
            store(B - 1)
            sp.wait_ge(stored, B * 16)

        @block.gpsimd
        def _(pool):
            nc.gpsimd.memset(whole[:, 0:NAT + NX, :], 0.0).then_inc(zeroed, 1)
            chain = Chain(pool, chain_p)
            nc.gpsimd.memset(mask_qk[:], 0.0)
            nc.gpsimd.memset(neg_part[:], 0.0)
            chain.link(nc.gpsimd.memset(mask_kq[:], 0.0))
            nc.gpsimd.affine_select(out=mask_qk[:], in_=mask_qk[:], compare_op=ALU.is_ge, fill=-1e30, base=0,
                                    pattern=[[-1, P]], channel_multiplier=1)
            for e in range(NX):
                m = nc.gpsimd.affine_select(out=mask_kq[:, e, :], in_=mask_kq[:, e, :], compare_op=ALU.is_ge, fill=-1e30,
                                            base=0, pattern=[[1, P]], channel_multiplier=-1)
            m.then_inc(masks_ready, 1)

            def handle(job, b, use):
                if job[0] == "norm_x":
                    pool.wait_ge(var_ready, b + NH + 1)
                    nc.gpsimd.tensor_tensor(rstd[:], mv[:, :, 1], neg_half[:, 0:T], ALU.pow).then_inc(rstd_ready, 1)
                if job[0] == "mid":
                    e = job[1]
                    pool.wait_ge(mid_ready, b * (NX + 1) + e + 1)
                    lo, rest, mid = (x[:, e, :] for x in (q_lo, q_rest, q_mid)) if e < NX else (k_lo[:], k_rest[:], k_mid[:])
                    nc.gpsimd.tensor_tensor(lo, rest, mid, ALU.subtract).then_inc(lo_ready, 1)
                if job[0] in ("norm_mix", "norm_out"):
                    first = job[0] == "norm_mix"
                    dst, gain, bias, ready = (hn, ln_g, ln_b, hn_ready) if first else (fo, fn_g, fn_b, fo_ready)
                    pool.wait_ge(sum_ready, b * 2 + (1 if first else 2))
                    chain.link(nc.gpsimd.tensor_tensor(r16[:], s16[:], neg_half[:, 0:T * NH], ALU.pow))
                    chain.link(nc.gpsimd.tensor_tensor(heads(yc[:]), heads(yc[:]), each(r16[:]), ALU.mult))
                    chain.link(nc.gpsimd.tensor_tensor(heads(yc[:]), heads(yc[:]), row(gain), ALU.mult))
                    nc.gpsimd.tensor_tensor(heads(dst[:]), heads(yc[:]), row(bias), ALU.add).then_inc(ready, 1)
                if job[0] == "leave":
                    pool.wait_ge(fl_scaled, b + 1)
                    chain.link(nc.gpsimd.tensor_tensor(heads(yc[:]), heads(fo[:]),
                                                       each(fl[:].rearrange("p t n -> p (t n)")), ALU.mult))
                    xb = x_all[:, bass.ds(b * T, T), :]
                    nc.gpsimd.tensor_tensor(xb, xb, yc[:], ALU.add).then_inc(x4_ready, 1)

            run_turns(pool, handle, chain, POOL_LINKS)

        @block.scalar
        def _(act):
            def copied(bank, nth, dst, src, signal, func=ACT.Copy, **kw):
                act.wait_ge(side_full[bank], nth)
                nc.scalar.activation(dst, src, func, **kw).then_inc(signal, 1)

            def handle(job, b, use):
                name, arg = job[0], job[1:]
                if use:
                    bank, nth = use
                    ps = side[bank]
                if name == "begin":
                    act.wait_ge(v_ready, b + 1)
                    if later(b):
                        act.wait_ge(values_pe, b * NG)
                    nc.scalar.activation(v_now[:], v_next[:], ACT.Copy).then_inc(v_now_ready, 1)
                elif name == "score":
                    g, n = arg
                    act.wait_ge(score_pe[n], b * NG + g + 1)
                    if later(b) or g > 1:
                        act.wait_ge(values_pe, b * NG + g - 1)
                    nc.scalar.activation(prob[:, g % 2, n, :], psum.banks[n], ACT.Exp, scale=SCALE)\
                      .then_inc(prob_ready[n], 1)
                elif name == "xT":
                    h = arg[0]
                    copied(bank, nth, xnT[:, h * 256:(h + 1) * 256], ps[:, 0:256], xnT_ready)
                elif name == "sx":
                    copied(bank, nth, sxT[:], ps, sxT_ready, ACT.Identity, bias=hl_b[:, 0:1])
                elif name in ("q", "k"):
                    e = arg[0] if arg else NX
                    act.wait_ge(side_full[bank], nth)
                    if e == 0 and later(b):
                        act.wait_ge(stack1_in, b * STACK1_DMAS * 16)
                        act.wait_ge(stack2_in, b * STACK2_DMAS * 16)
                    nc.scalar.activation(q_hi[:, e, :] if arg else k_hi[:], ps, ACT.Copy).then_inc(hi_ready, 1)
                elif name == "v":
                    copied(bank, nth, v_next[:], ps, v_ready)
                elif name == "mid":
                    e = arg[0]
                    act.wait_ge(rest_ready, b * (NX + 1) + e + 1)
                    mid, rest = (q_mid[:, e, :], q_rest[:, e, :]) if e < NX else (k_mid[:], k_rest[:])
                    nc.scalar.activation(mid, rest, ACT.Copy).then_inc(mid_ready, 1)
                elif name == "collect":
                    sc = arg[0]
                    act.wait_ge(values_pe, b * NG + GROUPS.index((sc, sc)) + 1)
                    if later(b) or sc > 0:
                        act.wait_ge(tok_ready, b * T + sc)
                    nc.scalar.activation(den[:], psum.banks[5].rearrange("p (e s) -> p e s", e=NX), ACT.Copy)\
                      .then_inc(den_ready, 1)
                elif name == "negmax":
                    n, sc = arg
                    copied(bank, nth, q2[96:128, slot(b), n, :, sc * P:(sc + 1) * P],
                           ps[96:128, :].rearrange("p (e s) -> p e s", e=NX), negmax_ready)
                elif name == "tok":
                    if arg[0] == 0 and later(b):
                        act.wait_ge(sum_ready, b * 2 - 1)
                    copied(bank, nth, tok[:, arg[0]], ps.rearrange("p (e c) -> p e c", e=NX), tok_copied)
                elif name == "mix_logits":
                    act.wait_ge(gl_ready, b + 1)
                    nc.scalar.activation(gl[:], gl[:], ACT.Exp).then_inc(gexp_ready, 1)
                elif name == "fxT":
                    copied(bank, nth, fxT[:], ps, fxT_ready)
                elif name == "fc1":
                    copied(bank, nth, h1, ps, h1_ready, ACT.Relu, bias=fc1_b[:, 0:1])
                elif name == "foT":
                    copied(bank, nth, foT[:], ps, foT_ready)
                elif name == "leave":
                    act.wait_ge(fl_ready, b + 1)
                    nc.scalar.activation(fl[:], fl[:], ACT.Exp).then_inc(fexp_ready, 1)

            act.wait_ge(w_in, LOADS * 16)
            run_turns(act, handle)

        @block.tensor
        def _(pe):
            pe.wait_ge(w_in, LOADS * 16)
            pe.wait_ge(masks_ready, 1)
            for k in range(NAT):
                nc.tensor.transpose(psum.banks[k // 4][:, (k % 4) * P:(k % 4 + 1) * P], nat[:, k, :], ident[:])
            for e in range(NX):
                nc.tensor.transpose(psum.banks[3][:, e * 16:(e + 1) * 16], nat_gate[:, e, :], ident[0:16, 0:16])
            nc.tensor.transpose(psum.banks[3][:, 64:64 + NH], nat_fgate, ident[0:NH, 0:NH]).then_inc(w_pe, 1)
            pe.wait_ge(w_ready, 1)
            held = [None, None]
            pick = ident[:].rearrange("p (n d) -> p n d", d=HD)[:, :, 0]

            def begins(b):
                left = [job for job in MID if job[0] in SIDE_JOBS][-2:]
                assert all(job in PRE_JOBS for job in left)
                held[:] = [(job, b) for job in left]

            def handle(job, b, use):
                name, arg = job[0], job[1:]
                if use:
                    bank, nth = use
                    ps = side[bank]
                    if held[bank]:
                        pe.wait_ge(*read(*held[bank]))
                    held[bank] = (job, b)
                if name == "score":
                    g, n = arg
                    sc, tc = GROUPS[g]
                    if g == 0 and n == 0:
                        pe.wait_ge(stack2_in, (b + 1) * STACK2_DMAS * 16)
                    if tc == 0:
                        pe.wait_ge(negmax_ready, b * NEG + sc * NH + n + 1)
                    if later(b) or g > 0:
                        pe.wait_ge(prob_ready[n], b * NG + g)
                    s, k = slice(sc * P, (sc + 1) * P), slice(tc * P, (tc + 1) * P)
                    dst = psum.banks[n]
                    nc.tensor.matmul(dst, k1[:, slot(b), n, k], q1[:, slot(b), n, :, s], start=True, stop=False)
                    m = nc.tensor.matmul(dst, k2[:, slot(b), n, k], q2[:, slot(b), n, :, s], start=False, stop=(sc != tc))
                    if sc == tc:
                        m = nc.tensor.matmul(dst, ident_bf[:], mask_kq[:], start=False, stop=True)
                    m.then_inc(score_pe[n], 1)
                elif name == "values":
                    g = arg[0]
                    sc, tc = GROUPS[g]
                    if g == 0:
                        pe.wait_ge(v_now_ready, b + 1)
                    if tc == 0 and (later(b) or sc > 0):
                        pe.wait_ge(att_ready, b * T + sc)
                        pe.wait_ge(den_ready, b * T + sc)
                    for n in range(NH):
                        pe.wait_ge(prob_ready[n], b * NG + g + 1)
                        d = slice(n * HD, (n + 1) * HD)
                        nc.tensor.matmul(psum.banks[4][d, :], v_now[:, tc, d], prob[:, g % 2, n, :],
                                         start=(tc == 0), stop=(tc == sc))
                    for n in range(NH):
                        d = slice(n * HD, (n + 1) * HD)
                        m = nc.tensor.matmul(psum.banks[5][d, :], ones[:, 0:HD], prob[:, g % 2, n, :],
                                             start=(tc == 0), stop=(tc == sc))
                    m.then_inc(values_pe, 1)
                elif name == "xT":
                    h = arg[0]
                    pe.wait_ge(xn_ready, b + NH + 1)
                    for i in range(2):
                        m = nc.tensor.transpose(ps[:, i * P:(i + 1) * P], xn[:, 2 * h + i, :], ident[:])
                    m.then_inc(side_full[bank], 1)
                elif name == "resid":
                    r = b + NH
                    pe.wait_ge(xnT_ready, (r + 1) * 2)
                    for it in range(T):
                        m = nc.tensor.matmul(ps[:, it * HD:(it + 1) * HD], xnT[:, it * P:(it + 1) * P],
                                             hl_t[:, r * HD:(r + 1) * HD], start=True, stop=True)
                    m.then_inc(side_full[bank], 1)
                elif name == "sx":
                    pe.wait_ge(xnT_ready, (b + NH + 1) * 2)
                    nc.tensor.matmul(ps, hl_t, xnT[:], start=True, stop=True).then_inc(side_full[bank], 1)
                elif name in ("q", "k"):
                    pe.wait_ge(sxT_ready, b + 1)
                    nc.tensor.matmul(ps, wq_t[:, arg[0], :] if arg else wk_t, sxT[:], start=True, stop=True)\
                      .then_inc(side_full[bank], 1)
                elif name == "v":
                    for it in range(T):
                        m = nc.tensor.matmul(ps[:, it * P:(it + 1) * P], sxT[:, it * P:(it + 1) * P], wv_t,
                                             start=True, stop=True)
                    m.then_inc(side_full[bank], 1)
                elif name == "max":
                    n, part = arg
                    sc, experts = MAX_PARTS[part]
                    if n == 0 and part == 0:
                        pe.wait_ge(stack1_in, (b + 1) * STACK1_DMAS * 16)
                    width = (sc + 1) * P
                    for i, e in enumerate(experts):
                        nc.tensor.matmul(ps[:, i * width:(i + 1) * width], q1[:, slot(b), n, e, sc * P:(sc + 1) * P],
                                         k1[:, slot(b), n, 0:width], start=True, stop=False)
                        m = nc.tensor.matmul(ps[:, (i + 1) * width - P:(i + 1) * width], ident_bf[:], mask_qk[:],
                                             start=False, stop=True)
                    m.then_inc(side_full[bank], 1)
                elif name == "negmax":
                    n, sc = arg
                    pe.wait_ge(top_split, b * 2 + sc // 2 + 1)
                    for e in range(NX):
                        m = nc.tensor.matmul(ps[96:128, e * P:(e + 1) * P], neg_part[:, (sc * NH + n) * NX + e, :],
                                             ident_bf[:], start=True, stop=True)
                    m.then_inc(side_full[bank], 1)
                elif name == "tok":
                    sc = arg[0]
                    pe.wait_ge(att_ready, b * T + sc + 1)
                    for e in range(NX):
                        m = nc.tensor.transpose(ps[:, e * P:(e + 1) * P], att[:, sc % 2, e, :], ident[:])
                    m.then_inc(side_full[bank], 1)
                elif name == "gate":
                    sc = arg[0]
                    for e in range(NX):
                        nc.tensor.matmul(ps[:, e * NH * NX:(e + 1) * NH * NX], att[:, sc % 2, e, :], gate_w[:, e, :],
                                         start=True, stop=True)
                    pe.wait_ge(den_ready, b * T + sc + 1)
                    at = NX * NH * NX
                    for e in range(NX):
                        m = nc.tensor.matmul(ps[:, at + e * NH:at + (e + 1) * NH], den[:, e, :], pick,
                                             start=True, stop=True)
                    m.then_inc(side_full[bank], 1)
                elif name == "fxT":
                    pe.wait_ge(hn_ready, b + 1)
                    for it in range(T):
                        m = nc.tensor.transpose(ps[:, it * P:(it + 1) * P], hn[:, it, :], ident[:])
                    m.then_inc(side_full[bank], 1)
                elif name == "fc1":
                    pe.wait_ge(fxT_ready, b + 1)
                    nc.tensor.matmul(ps, fc1_t, fxT[:], start=True, stop=True).then_inc(side_full[bank], 1)
                elif name == "fc2":
                    pe.wait_ge(h1m_ready, b + 1)
                    for it in range(T):
                        m = nc.tensor.matmul(ps[:, it * P:(it + 1) * P], h1[:, it * P:(it + 1) * P], fc2_t,
                                             start=True, stop=True)
                    m.then_inc(side_full[bank], 1)
                elif name == "foT":
                    pe.wait_ge(fo_ready, b + 1)
                    for it in range(T):
                        m = nc.tensor.transpose(ps[:, it * P:(it + 1) * P], fo[:, it, :], ident[:])
                    m.then_inc(side_full[bank], 1)
                elif name == "fgate":
                    pe.wait_ge(foT_ready, b + 1)
                    for it in range(T):
                        m = nc.tensor.matmul(ps[:, it * NH:(it + 1) * NH], foT[:, it * P:(it + 1) * P], fgate_w[:],
                                             start=True, stop=True)
                    m.then_inc(side_full[bank], 1)

            run_turns(pe, handle, begins=begins)

        @block.vector
        def _(dve):
            chain = Chain(dve, chain_v)
            nc.vector.memset(q2[64:128].rearrange("p a n e s -> p (a n e s)").bitcast(F32), 0.0)
            chain.link(nc.vector.memset(k2[64:128].rearrange("p a n s -> p (a n s)").bitcast(F32), 0.0))
            nc.vector.memset(k2[96:99], 1.0)
            dve.wait_ge(w_in, LOADS * 16)
            dve.wait_ge(w_pe, 1)
            for k in range(NAT):
                nc.vector.tensor_copy(turned[:, k, :], psum.banks[k // 4][:, (k % 4) * P:(k % 4 + 1) * P])
            nc.vector.tensor_copy(gate_w[:], psum.banks[3][:, 0:64].rearrange("p (e g) -> p e g", e=NX))
            nc.vector.tensor_copy(fgate_w[:], psum.banks[3][:, 64:64 + NH]).then_inc(w_ready, 1)

            def norm_heads():
                chain.link(nc.vector.tensor_reduce(s16[:], heads(y[:]), AX, ALU.add))
                chain.link(nc.vector.tensor_scalar(s16[:], s16[:], -1.0 / HD, None, ALU.mult))
                chain.link(nc.vector.tensor_tensor(heads(yc[:]), heads(y[:]), each(s16[:]), ALU.add))
                chain.link(nc.vector.tensor_tensor(sq[:], yc[:], yc[:], ALU.mult))
                chain.link(nc.vector.tensor_reduce(s16[:], heads(sq[:]), AX, ALU.add))
                nc.vector.tensor_scalar(s16[:], s16[:], 1.0 / HD, 1e-8, ALU.mult, ALU.add).then_inc(sum_ready, 1)

            def handle(job, b, use):
                name, arg = job[0], job[1:]
                if use:
                    bank, nth = use
                    ps = side[bank]
                if name == "norm_x":
                    m_th = b + NH
                    g = b + NH if isinstance(b, int) and b < 0 else b
                    for it in range(T):
                        m = nc.vector.bn_stats(stats[:, it, :], x_all[:, g * T + it, :])
                    chain.link(m)
                    nc.vector.memset(spot[:], 0.0)
                    for it in range(T):
                        m = nc.vector.bn_aggr(mv[:, it, :], stats[:, it, :])
                    chain.link(m)
                    nc.vector.tensor_scalar(mv[:, :, 1], mv[:, :, 1], 1e-5, None, ALU.add).then_inc(var_ready, 1)
                elif name == "scale_x":
                    m_th = b + NH
                    g = b + NH if isinstance(b, int) and b < 0 else b
                    dve.wait_ge(rstd_ready, m_th + 1)
                    if later(m_th):
                        dve.wait_ge(xnT_ready, m_th * 2)
                    for it in range(T):
                        m = nc.vector.tensor_scalar(xn[:, it, :], x_all[:, g * T + it, :], mv[:, it, 0:1],
                                                    rstd[:, it:it + 1], ALU.subtract, ALU.mult)
                    m.then_inc(xn_ready, 1)
                elif name == "resid":
                    r = b + NH
                    d = slice(r * HD, (r + 1) * HD)
                    dve.wait_ge(side_full[bank], nth)
                    nc.vector.tensor_tensor(resid[:, :, d], ps[:, 0:T * HD].rearrange("p (t d) -> p t d", t=T),
                                            hl_b_row[:, d].unsqueeze(1).broadcast_to([P, T, HD]), ALU.add)\
                      .then_inc(resid_ready, 1)
                elif name == "sx":
                    dve.wait_ge(sxT_ready, b + 1)
                    nc.vector.tensor_scalar(not_pad[:, slot(b), :], sxT[:], 0.0, None, ALU.not_equal)
                elif name in ("q", "k"):
                    e = arg[0] if arg else NX
                    dve.wait_ge(hi_ready, b * (NX + 1) + e + 1)
                    if e == 0 and later(b):
                        dve.wait_ge(lo_ready, b * (NX + 1))
                    hi, rest = (q_hi[:, e, :], q_rest[:, e, :]) if arg else (k_hi[:], k_rest[:])
                    nc.vector.tensor_tensor(rest, ps, hi, ALU.subtract).then_inc(rest_ready, 1)
                elif name == "max":
                    n, part = arg
                    sc, experts = MAX_PARTS[part]
                    width = (sc + 1) * P * len(experts)
                    dve.wait_ge(side_full[bank], nth)
                    nc.vector.tensor_reduce(top[:, sc, n, experts[0]:experts[-1] + 1],
                                            ps[:, 0:width].rearrange("p (e k) -> p e k", e=len(experts)), AX, ALU.max)\
                      .then_inc(top_ready, 1)
                elif name == "max_split":
                    half = arg[0]
                    done = FIRST_MAXIMA if half == 0 else len(MAX_JOBS)
                    dve.wait_ge(top_ready, b * len(MAX_JOBS) + done)
                    if later(b):
                        dve.wait_ge(negmax_ready, b * NEG)
                    i = slice(half * NEG // 2 * NX, (half + 1) * NEG // 2 * NX)
                    neg = neg_top[:, i]
                    chain.link(nc.vector.tensor_scalar(neg, top[:].rearrange("p s n e -> p (s n e)")[:, i], -1.0, None,
                                                       ALU.mult))
                    chain.link(nc.vector.tensor_copy(neg_part[:, i, 0], neg))
                    chain.link(nc.vector.tensor_tensor(neg, neg, neg_part[:, i, 0], ALU.subtract))
                    chain.link(nc.vector.tensor_copy(neg_part[:, i, 1], neg))
                    nc.vector.tensor_tensor(neg_part[:, i, 2], neg, neg_part[:, i, 1], ALU.subtract)\
                      .then_inc(top_split, 1)
                elif name == "collect":
                    sc = arg[0]
                    g = GROUPS.index((sc, sc))
                    dve.wait_ge(values_pe, b * NG + g + 1)
                    nc.vector.tensor_tensor(att[:, sc % 2], psum.banks[4].rearrange("p (e s) -> p e s", e=NX),
                                            not_pad[:, slot(b), sc * P:(sc + 1) * P].unsqueeze(1)
                                            .broadcast_to([P, NX, P]), ALU.mult).then_inc(att_ready, 1)
                elif name == "gate":
                    sc = arg[0]
                    dve.wait_ge(side_full[bank], nth)
                    at = NX * NH * NX
                    chain.link(nc.vector.reciprocal(rden[:, sc], ps[:, at:at + NX * NH].rearrange("p (e n) -> p e n", e=NX)))
                    chain.link(nc.vector.tensor_tensor(gprod[:], ps[:, 0:at].rearrange("p (e n g) -> p e n g", e=NX, n=NH),
                                                       rden[:, sc].unsqueeze(3).broadcast_to([P, NX, NH, NX]), ALU.mult))
                    nc.vector.tensor_reduce(glog[:, sc], gprod[:].rearrange("p e n g -> p n g e"), AX, ALU.add)\
                      .then_inc(tok_ready, 1)
                elif name == "mix_logits":
                    dve.wait_ge(tok_ready, (b + 1) * T)
                    if later(b):
                        dve.wait_ge(x4_ready, b)
                    chain.link(nc.vector.tensor_tensor(gl[:], glog[:],
                                                       gate_b[:].rearrange("p (n e) -> p n e", n=NH).unsqueeze(1)
                                                       .broadcast_to([P, T, NH, NX]), ALU.add))
                    chain.link(nc.vector.tensor_reduce(gtop[:], gl[:], AX, ALU.max))
                    nc.vector.tensor_tensor(gl[:], gl[:], gtop[:].unsqueeze(3).broadcast_to([P, T, NH, NX]),
                                            ALU.subtract).then_inc(gl_ready, 1)
                elif name == "mix_weights":
                    dve.wait_ge(gexp_ready, b + 1)
                    chain.link(nc.vector.tensor_reduce(gtop[:], gl[:], AX, ALU.add))
                    chain.link(nc.vector.reciprocal(gtop[:], gtop[:]))
                    chain.link(nc.vector.tensor_tensor(gl[:], gl[:], gtop[:].unsqueeze(3).broadcast_to([P, T, NH, NX]),
                                                       ALU.mult))
                    chain.link(nc.vector.tensor_tensor(gl[:], gl[:], rden[:].rearrange("p t e n -> p t n e"), ALU.mult))
                elif name == "mix":
                    sc = arg[0]
                    if sc == 0:
                        dve.wait_ge(tok_copied, (b + 1) * T)
                    chain.link(nc.vector.tensor_tensor(
                        mixw[:].rearrange("p e (n d) -> p e n d", n=NH),
                        tok[:, sc].rearrange("p e (n d) -> p e n d", n=NH),
                        gl[:, sc].rearrange("p n e -> p e n").unsqueeze(3).broadcast_to([P, NX, NH, HD]), ALU.mult))
                    chain.link(nc.vector.tensor_reduce(y[:, sc, :], mixw[:].rearrange("p e c -> p c e"), AX, ALU.add))
                    if sc == T - 1:
                        chain.link(nc.vector.tensor_tensor(y[:], y[:], resid[:], ALU.add))
                elif name in ("norm_mix", "norm_out"):
                    norm_heads()
                elif name == "fc1":
                    dve.wait_ge(h1_ready, b + 1)
                    nc.vector.scalar_tensor_tensor(out=h1, in0=fxT[:], scalar=0.0, in1=h1, op0=ALU.not_equal,
                                                   op1=ALU.mult).then_inc(h1m_ready, 1)
                elif name == "fc2":
                    dve.wait_ge(side_full[bank], nth)
                    nc.vector.tensor_tensor(heads(y[:]), ps.rearrange("p (a d) -> p a d", d=HD), row(fc2_b), ALU.add)\
                      .then_inc(y_biased, 1)
                    dve.wait_ge(y_biased, b + 1)
                    chain.link(nc.vector.scalar_tensor_tensor(out=y[:], in0=hn[:], scalar=0.0, in1=y[:],
                                                              op0=ALU.not_equal, op1=ALU.mult))
                    chain.link(nc.vector.tensor_tensor(y[:], y[:], hn[:], ALU.add))
                elif name == "fgate":
                    dve.wait_ge(side_full[bank], nth)
                    logits = ps[:, 0:T * NH].rearrange("p (t n) -> p t n", t=T)
                    chain.link(nc.vector.tensor_reduce(fmax[:], logits, AX, ALU.max))
                    nc.vector.tensor_tensor(fl[:], logits, fmax[:].unsqueeze(2).broadcast_to([P, T, NH]),
                                            ALU.subtract).then_inc(fl_ready, 1)
                elif name == "leave":
                    dve.wait_ge(fexp_ready, b + 1)
                    chain.link(nc.vector.tensor_reduce(fmax[:], fl[:], AX, ALU.add))
                    chain.link(nc.vector.reciprocal(fmax[:], fmax[:]))
                    nc.vector.tensor_tensor(fl[:], fl[:], fmax[:].unsqueeze(2).broadcast_to([P, T, NH]), ALU.mult)\
                      .then_inc(fl_scaled, 1)

            run_turns(dve, handle, chain, VEC_LINKS)


_INS = ["x", "adj",
        "L0_gnn_fc_w", "L0_gnn_fc_b", "L0_gnn_q_w", "L0_gnn_q_b", "L0_gnn_k_w", "L0_gnn_k_b", "L0_gnn_fp_w",
        "L0_gnn_fp_b", "L0_ffn_gate_w", "L0_ffn_gate_b", "L0_ffn_w1", "L0_ffn_b1", "L0_ffn_w2", "L0_ffn_b2",
        "L1_gnn_W", "L1_gnn_b", "L1_ffn_hl_w", "L1_ffn_hl_b", "L1_ffn_wq", "L1_ffn_wk", "L1_ffn_wv",
        "L1_ffn_gate_w", "L1_ffn_gate_b", "L1_ffn_ln_g", "L1_ffn_ln_b", "L1_ffn_fc1_w", "L1_ffn_fc1_b",
        "L1_ffn_fc2_w", "L1_ffn_fc2_b", "L1_ffn_fnorm_g", "L1_ffn_fnorm_b", "L1_ffn_fgate_w"]


def kernel(**inputs):
    import numpy as _np
    import concourse.bacc as _bacc
    from concourse import mybir as _mybir
    from concourse.bass_utils import run_bass_kernel_spmd as _run

    nc = _bacc.Bacc("TRN2", target_bir_lowering=False, num_devices=1)
    arrays, args = {}, {}
    for name in _INS:
        a = _np.ascontiguousarray(inputs[name])
        arrays[f"in_{name}_dram"] = a
        args[name] = nc.dram_tensor(f"in_{name}_dram", a.shape, _mybir.dt.from_np(a.dtype), kind="ExternalInput").ap()
    out = nc.dram_tensor("out_0_dram", (16, 512, 128), _mybir.dt.float32, kind="ExternalOutput").ap()
    build(nc, args, out)
    r = _run(nc, [arrays], core_ids=[0])
    return r.results[0]["out_0_dram"]
```
